# Optimizing a Trainium2 kernel written in Bass

```python
import numpy as np
import jax
import jax.numpy as jnp

def _softmax(x, axis=-1):
    return jax.nn.softmax(x, axis=axis)

def _gelu(x):
    return jax.nn.gelu(x, approximate=True)

def _silu(x):
    return jax.nn.silu(x)

def _sigmoid(x):
    return jax.nn.sigmoid(x)

def _layernorm(x, axis=-1, eps=1e-05):
    m = jnp.mean(x, axis=axis, keepdims=True)
    v = jnp.var(x, axis=axis, keepdims=True)
    return (x - m) / jnp.sqrt(v + eps)

def _scatter_add(tgt, idx, src, axis=0):
    return tgt.at[idx].add(src)

def _segment_sum(src, seg, n):
    return jax.ops.segment_sum(src, seg, n)
kernel_name = 'mk_conv_attn_hybrid_d4_conv_nchw128_r4_ca248a'

def setup_inputs(seed: int=0):
    np.random.seed(seed)
    _w = jnp.asarray

    def _rec_inputs():
        import jax
        import jax.numpy as jnp
        _gk = jax.random.key(seed)
        x = 7.22e-05 + 1 * jax.random.normal(jax.random.fold_in(_gk, 1), (16, 32, 16, 16), jnp.float32)
        return x
    x = _rec_inputs()

    def _L0_conv_setup():
        import jax, jax.numpy as jnp
        import numpy as np
        DIM = 32
        D_STATE = 16
        EXPAND = 2
        E = DIM * EXPAND
        BSZ, H, W = (16, 16, 16)
        LN_EPS = 1e-05
        key = jax.random.key(seed)
        ks = jax.random.split(key, 8)
        s_in = 1.0 / np.sqrt(DIM)
        s_out = 1.0 / np.sqrt(E)
        return {'x': jax.random.normal(ks[0], (BSZ, DIM, H, W), jnp.float32), 'A': jax.random.normal(ks[1], (D_STATE, D_STATE), jnp.float32) * 0.1, 'Bm': jax.random.normal(ks[2], (D_STATE, E), jnp.float32) * 0.1, 'Cm': jax.random.normal(ks[3], (E, D_STATE), jnp.float32) * 0.1, 'D': jax.random.normal(ks[4], (E,), jnp.float32) * 0.1, 'W_in': jax.random.uniform(ks[5], (E, DIM), jnp.float32, -s_in, s_in), 'b_in': jnp.zeros((E,), jnp.float32), 'W_out': jax.random.uniform(ks[6], (DIM, E), jnp.float32, -s_out, s_out), 'b_out': jnp.zeros((DIM,), jnp.float32), 'gamma': jnp.ones((DIM,), jnp.float32), 'beta': jnp.zeros((DIM,), jnp.float32)}
    _L0_conv_all = _L0_conv_setup()
    _L0_conv_in = {k: v for k, v in _L0_conv_all.items() if k in ('A', 'Bm', 'Cm', 'D', 'W_in', 'b_in', 'W_out', 'b_out', 'gamma', 'beta')}
    del _L0_conv_all

    def _L1_conv_setup():
        import jax, jax.numpy as jnp
        import numpy as np

        def _prelu(x, a):
            return jnp.where(x >= 0, x, a * x)

        def _conv1x1(x, w, b, a):
            y = jnp.einsum('oc,nchw->nohw', w, x) + b[None, :, None, None]
            return _prelu(y, a)
        key = jax.random.key(seed)
        ks = jax.random.split(key, 8)
        N, C, H, W = (4, 32, 16, 16)
        Cr = C // 2
        sC = 1.0 / np.sqrt(C)
        x = jax.random.normal(ks[0], (N, C, H, W), dtype=jnp.float32)
        w1 = jax.random.normal(ks[1], (Cr, C), dtype=jnp.float32) * sC
        b1 = jnp.zeros((Cr,), dtype=jnp.float32)
        a1 = jnp.asarray(0.25, dtype=jnp.float32)
        w2 = jax.random.normal(ks[2], (Cr, C), dtype=jnp.float32) * sC
        b2 = jnp.zeros((Cr,), dtype=jnp.float32)
        a2 = jnp.asarray(0.25, dtype=jnp.float32)
        wa = jax.random.normal(ks[3], (C, C), dtype=jnp.float32) * sC
        ba = jnp.zeros((C,), dtype=jnp.float32)
        aa = jnp.asarray(0.25, dtype=jnp.float32)
        return {'x': x, 'w1': w1, 'b1': b1, 'a1': a1, 'w2': w2, 'b2': b2, 'a2': a2, 'wa': wa, 'ba': ba, 'aa': aa}
    _L1_conv_all = _L1_conv_setup()
    _L1_conv_in = {k: v for k, v in _L1_conv_all.items() if k in ('w1', 'b1', 'a1', 'w2', 'b2', 'a2', 'wa', 'ba', 'aa')}
    del _L1_conv_all

    def _L2_attn_setup():
        import jax, jax.numpy as jnp
        import numpy as np
        DIM = 32
        N_HEADS = 4
        HEAD_DIM = DIM // N_HEADS
        RANK = 8
        SCALING = 16.0 / RANK
        ROPE_BASE = 10000.0
        INV_SQRT_HD = 1.0 / float(np.sqrt(HEAD_DIM))

        def _rope(x, cos, sin):
            B, S, H, D = x.shape
            xr = x.reshape(B, S, H, D // 2, 2)
            x1, x2 = (xr[..., 0], xr[..., 1])
            c = cos[None, :, None, :]
            s = sin[None, :, None, :]
            out = jnp.stack([x1 * c - x2 * s, x1 * s + x2 * c], axis=-1)
            return out.reshape(B, S, H, D)
        key = jax.random.key(seed)
        ks = jax.random.split(key, 11)
        B, S = (32, 64)
        w = lambda k, shp: jax.random.normal(k, shp, dtype=jnp.float32) * 0.05
        return {'x': jax.random.normal(ks[0], (B, S, DIM), dtype=jnp.float32), 'wq': w(ks[1], (DIM, DIM)), 'wk': w(ks[2], (DIM, DIM)), 'wv': w(ks[3], (DIM, DIM)), 'wo': w(ks[4], (DIM, DIM)), 'lora_A_q': w(ks[5], (RANK, DIM)), 'lora_B_q': w(ks[6], (DIM, RANK)), 'lora_A_k': w(ks[7], (RANK, DIM)), 'lora_B_k': w(ks[8], (DIM, RANK)), 'lora_A_v': w(ks[9], (RANK, DIM)), 'lora_B_v': w(ks[10], (DIM, RANK))}
    _L2_attn_all = _L2_attn_setup()
    _L2_attn_in = {k: v for k, v in _L2_attn_all.items() if k in ('wq', 'wk', 'wv', 'wo', 'lora_A_q', 'lora_B_q', 'lora_A_k', 'lora_B_k', 'lora_A_v', 'lora_B_v')}
    del _L2_attn_all

    def _L2_ffn_setup():
        import jax, jax.numpy as jnp
        import numpy as np
        BN_EPS = 1e-05
        key = jax.random.key(seed)
        k1, k2, k3 = jax.random.split(key, 3)
        B, T, I, H = (16, 512, 32, 32)
        x = jax.random.normal(k1, (B, T, I), dtype=jnp.float32)
        W = jax.random.normal(k2, (H, I), dtype=jnp.float32) * (1.0 / np.sqrt(I))
        V = jnp.linalg.qr(jax.random.normal(k3, (H, H), dtype=jnp.float32))[0]
        gamma = jnp.ones((H,), dtype=jnp.float32)
        beta = jnp.zeros((H,), dtype=jnp.float32)
        return {'x': x, 'W': W, 'V': V, 'gamma': gamma, 'beta': beta}
    _L2_ffn_all = _L2_ffn_setup()
    _L2_ffn_in = {k: v for k, v in _L2_ffn_all.items() if k in ('W', 'V', 'gamma', 'beta')}
    del _L2_ffn_all

    def _L3_attn_setup():
        import jax, jax.numpy as jnp
        import numpy as np
        CHUNK = 16
        D_MODEL = 32
        D_STATE = 16
        HEADDIM = 16
        D_INNER = 2 * D_MODEL
        NHEADS = D_INNER // HEADDIM
        CONV_DIM = D_INNER + 2 * D_STATE
        K = 4
        D_IN_PROJ = 2 * D_INNER + 2 * D_STATE + NHEADS
        EPS = 1e-05

        def _segsum(t):
            L = t.shape[-1]
            cs = jnp.cumsum(t, -1)
            seg = cs[..., :, None] - cs[..., None, :]
            mask = jnp.tril(jnp.ones((L, L), bool))
            return jnp.where(mask, seg, -jnp.inf)

        def _ssd(xh, dt, A, Bm, Cm):
            b, l, h, p = xh.shape
            n = Bm.shape[-1]
            c = l // CHUNK
            xdt = xh * dt[..., None]
            dA = dt * A
            rc = lambda t: t.reshape(b, c, CHUNK, *t.shape[2:])
            xc, dAc, Bc, Cc = (rc(xdt), rc(dA), rc(Bm), rc(Cm))
            Acs = jnp.cumsum(dAc, axis=2)
            Lmat = jnp.exp(_segsum(dAc.transpose(0, 1, 3, 2)))
            Y_diag = jnp.einsum('bcln,bcsn,bchls,bcshp->bclhp', Cc, Bc, Lmat, xc)
            decay_st = jnp.exp(Acs[:, :, -1:, :] - Acs)
            states = jnp.einsum('bcln,bclh,bclhp->bchpn', Bc, decay_st, xc)
            chunk_decay = jnp.exp(Acs[:, :, -1])

            def step(carry, inp):
                st, dec = inp
                new = st + carry * dec[:, :, None, None]
                return (new, carry)
            init = jnp.zeros((b, h, p, n), xh.dtype)
            _, prev = jax.lax.scan(step, init, (states.transpose(1, 0, 2, 3, 4), chunk_decay.transpose(1, 0, 2)))
            prev = prev.transpose(1, 0, 2, 3, 4)
            Y_off = jnp.einsum('bcln,bchpn,bclh->bclhp', Cc, prev, jnp.exp(Acs))
            return (Y_diag + Y_off).reshape(b, l, h, p)

        def _mamba3(x, in_proj, conv_w, conv_b, A_log, dt_bias, D, norm_w, out_proj):
            b, l, _ = x.shape
            zxbcdt = x @ in_proj
            z, xbc, dt = jnp.split(zxbcdt, [D_INNER, D_INNER + CONV_DIM], axis=-1)
            xp = jnp.pad(xbc, ((0, 0), (K - 1, 0), (0, 0)))
            conv = sum((xp[:, i:i + l, :] * conv_w[:, i] for i in range(K))) + conv_b
            xbc = jax.nn.silu(conv)
            xh, Bm, Cm = jnp.split(xbc, [D_INNER, D_INNER + D_STATE], axis=-1)
            xh = xh.reshape(b, l, NHEADS, HEADDIM)
            dt = jax.nn.softplus(dt + dt_bias)
            A = -jnp.exp(A_log)
            y = _ssd(xh, dt, A, Bm, Cm) + xh * D[None, None, :, None]
            yg = y.reshape(b, l, D_INNER) * jax.nn.silu(z)
            yn = yg * jax.lax.rsqrt(jnp.mean(yg * yg, -1, keepdims=True) + EPS) * norm_w
            return yn @ out_proj
        key = jax.random.key(seed)
        ks = jax.random.split(key, 19)
        inp = {'x': jax.random.normal(ks[0], (16, 1024, D_MODEL), jnp.float32)}
        for i, pre in enumerate(['fwd', 'bwd']):
            o = 1 + 9 * i
            inp[pre + '_in_proj'] = jax.random.normal(ks[o], (D_MODEL, D_IN_PROJ), jnp.float32) * D_MODEL ** (-0.5)
            inp[pre + '_conv_w'] = jax.random.normal(ks[o + 1], (CONV_DIM, K), jnp.float32) * 0.3
            inp[pre + '_conv_b'] = jnp.zeros((CONV_DIM,), jnp.float32)
            inp[pre + '_A_log'] = jnp.log(jax.random.uniform(ks[o + 2], (NHEADS,), jnp.float32, 1.0, 16.0))
            inp[pre + '_dt_bias'] = jax.random.normal(ks[o + 3], (NHEADS,), jnp.float32) * 0.5
            inp[pre + '_D'] = jnp.ones((NHEADS,), jnp.float32)
            inp[pre + '_norm_w'] = jnp.ones((D_INNER,), jnp.float32)
            inp[pre + '_out_proj'] = jax.random.normal(ks[o + 4], (D_INNER, D_MODEL), jnp.float32) * D_INNER ** (-0.5)
        return inp
    _L3_attn_all = _L3_attn_setup()
    _L3_attn_in = {k: v for k, v in _L3_attn_all.items() if k in ('fwd_in_proj', 'fwd_conv_w', 'fwd_conv_b', 'fwd_A_log', 'fwd_dt_bias', 'fwd_D', 'fwd_norm_w', 'fwd_out_proj', 'bwd_in_proj', 'bwd_conv_w', 'bwd_conv_b', 'bwd_A_log', 'bwd_dt_bias', 'bwd_D', 'bwd_norm_w', 'bwd_out_proj')}
    del _L3_attn_all

    def _L3_ffn_setup():
        import jax, jax.numpy as jnp
        import numpy as np
        NB, NOPS = (33, 19)
        D, H = (32, 128)
        B, S = (8, 256)
        CARRY_OPS = [0, 1, 2, 10, 11, 12, 13]

        def _build_masks():
            am = np.zeros((NB, NOPS), dtype=bool)
            fm = np.zeros((NB, NOPS), dtype=bool)
            fm[0, :] = True
            for b in range(1, 8):
                am[b, CARRY_OPS] = True
                fm[b, CARRY_OPS] = True
            am[8, [14, 15, 8, 9]] = True
            fm[8, [14, 15, 8, 9]] = True
            for b in range(16, 32):
                fm[b, [3, 4]] = True
            am[32, [10, 11, 12, 13]] = True
            fm[32, [5, 6, 7, 2, 4, 10, 11, 12, 13]] = True
            return (jnp.asarray(am), jnp.asarray(fm))
        key = jax.random.key(seed)
        ks = jax.random.split(key, 9)
        sd = 1.0 / np.sqrt(D)
        sh = 1.0 / np.sqrt(H)
        am, fm = _build_masks()
        return {'x': jax.random.normal(ks[0], (B, S, D), jnp.float32), 'ffn_w1': jax.random.normal(ks[1], (NB, NOPS, D, H), jnp.float32) * sd, 'ffn_b1': jnp.zeros((NB, NOPS, H), jnp.float32), 'ffn_w2': jax.random.normal(ks[2], (NB, NOPS, H, D), jnp.float32) * sh, 'ffn_b2': jnp.zeros((NB, NOPS, D), jnp.float32), 'wq': jax.random.normal(ks[3], (NB, NOPS, D, D), jnp.float32) * sd, 'wk': jax.random.normal(ks[4], (NB, NOPS, D, D), jnp.float32) * sd, 'wv': jax.random.normal(ks[5], (NB, NOPS, D, D), jnp.float32) * sd, 'wo': jax.random.normal(ks[6], (NB, NOPS, D, D), jnp.float32) * sd, 'attn_mask': am, 'ffn_mask': fm}
    _L3_ffn_all = _L3_ffn_setup()
    _L3_ffn_in = {k: v for k, v in _L3_ffn_all.items() if k in ('ffn_w1', 'ffn_b1', 'ffn_w2', 'ffn_b2', 'wq', 'wk', 'wv', 'wo', 'attn_mask', 'ffn_mask')}
    del _L3_ffn_all
    return {'x': x, 'L0_conv_A': _L0_conv_in['A'], 'L0_conv_Bm': _L0_conv_in['Bm'], 'L0_conv_Cm': _L0_conv_in['Cm'], 'L0_conv_D': _L0_conv_in['D'], 'L0_conv_W_in': _L0_conv_in['W_in'], 'L0_conv_b_in': _L0_conv_in['b_in'], 'L0_conv_W_out': _L0_conv_in['W_out'], 'L0_conv_b_out': _L0_conv_in['b_out'], 'L0_conv_gamma': _L0_conv_in['gamma'], 'L0_conv_beta': _L0_conv_in['beta'], 'L1_conv_w1': _L1_conv_in['w1'], 'L1_conv_b1': _L1_conv_in['b1'], 'L1_conv_a1': _L1_conv_in['a1'], 'L1_conv_w2': _L1_conv_in['w2'], 'L1_conv_b2': _L1_conv_in['b2'], 'L1_conv_a2': _L1_conv_in['a2'], 'L1_conv_wa': _L1_conv_in['wa'], 'L1_conv_ba': _L1_conv_in['ba'], 'L1_conv_aa': _L1_conv_in['aa'], 'L2_attn_wq': _L2_attn_in['wq'], 'L2_attn_wk': _L2_attn_in['wk'], 'L2_attn_wv': _L2_attn_in['wv'], 'L2_attn_wo': _L2_attn_in['wo'], 'L2_attn_lora_A_q': _L2_attn_in['lora_A_q'], 'L2_attn_lora_B_q': _L2_attn_in['lora_B_q'], 'L2_attn_lora_A_k': _L2_attn_in['lora_A_k'], 'L2_attn_lora_B_k': _L2_attn_in['lora_B_k'], 'L2_attn_lora_A_v': _L2_attn_in['lora_A_v'], 'L2_attn_lora_B_v': _L2_attn_in['lora_B_v'], 'L2_ffn_W': _L2_ffn_in['W'], 'L2_ffn_V': _L2_ffn_in['V'], 'L2_ffn_gamma': _L2_ffn_in['gamma'], 'L2_ffn_beta': _L2_ffn_in['beta'], 'L3_attn_fwd_in_proj': _L3_attn_in['fwd_in_proj'], 'L3_attn_fwd_conv_w': _L3_attn_in['fwd_conv_w'], 'L3_attn_fwd_conv_b': _L3_attn_in['fwd_conv_b'], 'L3_attn_fwd_A_log': _L3_attn_in['fwd_A_log'], 'L3_attn_fwd_dt_bias': _L3_attn_in['fwd_dt_bias'], 'L3_attn_fwd_D': _L3_attn_in['fwd_D'], 'L3_attn_fwd_norm_w': _L3_attn_in['fwd_norm_w'], 'L3_attn_fwd_out_proj': _L3_attn_in['fwd_out_proj'], 'L3_attn_bwd_in_proj': _L3_attn_in['bwd_in_proj'], 'L3_attn_bwd_conv_w': _L3_attn_in['bwd_conv_w'], 'L3_attn_bwd_conv_b': _L3_attn_in['bwd_conv_b'], 'L3_attn_bwd_A_log': _L3_attn_in['bwd_A_log'], 'L3_attn_bwd_dt_bias': _L3_attn_in['bwd_dt_bias'], 'L3_attn_bwd_D': _L3_attn_in['bwd_D'], 'L3_attn_bwd_norm_w': _L3_attn_in['bwd_norm_w'], 'L3_attn_bwd_out_proj': _L3_attn_in['bwd_out_proj'], 'L3_ffn_ffn_w1': _L3_ffn_in['ffn_w1'], 'L3_ffn_ffn_b1': _L3_ffn_in['ffn_b1'], 'L3_ffn_ffn_w2': _L3_ffn_in['ffn_w2'], 'L3_ffn_ffn_b2': _L3_ffn_in['ffn_b2'], 'L3_ffn_wq': _L3_ffn_in['wq'], 'L3_ffn_wk': _L3_ffn_in['wk'], 'L3_ffn_wv': _L3_ffn_in['wv'], 'L3_ffn_wo': _L3_ffn_in['wo'], 'L3_ffn_attn_mask': _L3_ffn_in['attn_mask'], 'L3_ffn_ffn_mask': _L3_ffn_in['ffn_mask']}

def reference(x, L0_conv_A, L0_conv_Bm, L0_conv_Cm, L0_conv_D, L0_conv_W_in, L0_conv_b_in, L0_conv_W_out, L0_conv_b_out, L0_conv_gamma, L0_conv_beta, L1_conv_w1, L1_conv_b1, L1_conv_a1, L1_conv_w2, L1_conv_b2, L1_conv_a2, L1_conv_wa, L1_conv_ba, L1_conv_aa, L2_attn_wq, L2_attn_wk, L2_attn_wv, L2_attn_wo, L2_attn_lora_A_q, L2_attn_lora_B_q, L2_attn_lora_A_k, L2_attn_lora_B_k, L2_attn_lora_A_v, L2_attn_lora_B_v, L2_ffn_W, L2_ffn_V, L2_ffn_gamma, L2_ffn_beta, L3_attn_fwd_in_proj, L3_attn_fwd_conv_w, L3_attn_fwd_conv_b, L3_attn_fwd_A_log, L3_attn_fwd_dt_bias, L3_attn_fwd_D, L3_attn_fwd_norm_w, L3_attn_fwd_out_proj, L3_attn_bwd_in_proj, L3_attn_bwd_conv_w, L3_attn_bwd_conv_b, L3_attn_bwd_A_log, L3_attn_bwd_dt_bias, L3_attn_bwd_D, L3_attn_bwd_norm_w, L3_attn_bwd_out_proj, L3_ffn_ffn_w1, L3_ffn_ffn_b1, L3_ffn_ffn_w2, L3_ffn_ffn_b2, L3_ffn_wq, L3_ffn_wk, L3_ffn_wv, L3_ffn_wo, L3_ffn_attn_mask, L3_ffn_ffn_mask):
    import jax
    import jax.numpy as jnp

    def _L0_conv_ref(x, A, Bm, Cm, D, W_in, b_in, W_out, b_out, gamma, beta):
        import jax, jax.numpy as jnp
        import numpy as np
        DIM = 32
        D_STATE = 16
        EXPAND = 2
        E = DIM * EXPAND
        BSZ, H, W = (16, 16, 16)
        LN_EPS = 1e-05
        Bsz, C, Hh, Ww = x.shape
        residual = x
        h = x.transpose(0, 2, 3, 1).reshape(Bsz, Hh * Ww, C)
        mu = jnp.mean(h, axis=-1, keepdims=True)
        var = jnp.mean((h - mu) ** 2, axis=-1, keepdims=True)
        hn = (h - mu) * jax.lax.rsqrt(var + LN_EPS) * gamma + beta
        z = jnp.einsum('blc,ec->ble', hn, W_in) + b_in
        u = jnp.einsum('ble,se->bls', z, Bm)
        u_tm = u.transpose(1, 0, 2)

        def step(state, u_t):
            state = jnp.tanh(state @ A.T + u_t)
            return (state, state)
        init = jnp.zeros((Bsz, A.shape[0]), z.dtype)
        _, states = jax.lax.scan(step, init, u_tm)
        states = states.transpose(1, 0, 2)
        y = jnp.einsum('bls,es->ble', states, Cm) + z * D
        out = jnp.einsum('ble,ce->blc', y, W_out) + b_out
        out = out.reshape(Bsz, Hh, Ww, C).transpose(0, 3, 1, 2)
        return out + residual

    def _L1_conv_ref(x, w1, b1, a1, w2, b2, a2, wa, ba, aa):
        import jax, jax.numpy as jnp
        import numpy as np

        def _prelu(x, a):
            return jnp.where(x >= 0, x, a * x)

        def _conv1x1(x, w, b, a):
            y = jnp.einsum('oc,nchw->nohw', w, x) + b[None, :, None, None]
            return _prelu(y, a)
        N, C, H, W = x.shape
        HW = H * W
        e1 = _conv1x1(x, w1, b1, a1).reshape(N, -1, HW)
        e2 = _conv1x1(x, w2, b2, a2).reshape(N, -1, HW)
        asm = _conv1x1(x, wa, ba, aa).reshape(N, C, HW)
        score = jnp.einsum('nci,ncj->nij', e1, e2)
        score = jax.nn.softmax(score, axis=2)
        out = jnp.einsum('nij,ncj->nci', score, asm)
        return out.reshape(N, C, H, W)

    def _L2_attn_ref(x, wq, wk, wv, wo, lora_A_q, lora_B_q, lora_A_k, lora_B_k, lora_A_v, lora_B_v):
        import jax, jax.numpy as jnp
        import numpy as np
        DIM = 32
        N_HEADS = 4
        HEAD_DIM = DIM // N_HEADS
        RANK = 8
        SCALING = 16.0 / RANK
        ROPE_BASE = 10000.0
        INV_SQRT_HD = 1.0 / float(np.sqrt(HEAD_DIM))

        def _rope(x, cos, sin):
            B, S, H, D = x.shape
            xr = x.reshape(B, S, H, D // 2, 2)
            x1, x2 = (xr[..., 0], xr[..., 1])
            c = cos[None, :, None, :]
            s = sin[None, :, None, :]
            out = jnp.stack([x1 * c - x2 * s, x1 * s + x2 * c], axis=-1)
            return out.reshape(B, S, H, D)
        B, S, _ = x.shape
        pos = jnp.arange(S, dtype=jnp.float32)
        inv_freq = 1.0 / ROPE_BASE ** (jnp.arange(0, HEAD_DIM, 2, dtype=jnp.float32) / HEAD_DIM)
        freqs = pos[:, None] * inv_freq[None, :]
        cos, sin = (jnp.cos(freqs), jnp.sin(freqs))

        def proj(w, A, Bm):
            return x @ w.T + x @ A.T @ Bm.T * SCALING
        q = proj(wq, lora_A_q, lora_B_q).reshape(B, S, N_HEADS, HEAD_DIM)
        k = proj(wk, lora_A_k, lora_B_k).reshape(B, S, N_HEADS, HEAD_DIM)
        v = proj(wv, lora_A_v, lora_B_v).reshape(B, S, N_HEADS, HEAD_DIM)
        q = _rope(q, cos, sin).transpose(0, 2, 1, 3)
        k = _rope(k, cos, sin).transpose(0, 2, 1, 3)
        v = v.transpose(0, 2, 1, 3)
        scores = jnp.einsum('bhqd,bhkd->bhqk', q, k) * INV_SQRT_HD
        causal = jnp.triu(jnp.ones((S, S), dtype=bool), k=1)
        scores = jnp.where(causal[None, None], -jnp.inf, scores)
        attn = jax.nn.softmax(scores, axis=-1)
        out = jnp.einsum('bhqk,bhkd->bhqd', attn, v)
        out = out.transpose(0, 2, 1, 3).reshape(B, S, DIM)
        return out @ wo.T

    def _L2_ffn_ref(x, W, V, gamma, beta):
        import jax, jax.numpy as jnp
        import numpy as np
        BN_EPS = 1e-05
        B, T, H = (x.shape[0], x.shape[1], W.shape[0])
        Wx = jnp.einsum('bti,hi->bth', x, W)
        flat = Wx.reshape(B * T, H)
        mean = jnp.mean(flat, axis=0)
        var = jnp.var(flat, axis=0)
        Wx = ((flat - mean) * jax.lax.rsqrt(var + BN_EPS) * gamma + beta).reshape(B, T, H)
        Vt = V.T

        def step(yt, wx_t):
            yt = jax.nn.sigmoid(wx_t + yt @ Vt)
            return (yt, yt)
        y0 = jnp.zeros((B, H), dtype=Wx.dtype)
        _, ys = jax.lax.scan(step, y0, jnp.swapaxes(Wx, 0, 1))
        return jnp.swapaxes(ys, 0, 1)

    def _L3_attn_ref(x, fwd_in_proj, fwd_conv_w, fwd_conv_b, fwd_A_log, fwd_dt_bias, fwd_D, fwd_norm_w, fwd_out_proj, bwd_in_proj, bwd_conv_w, bwd_conv_b, bwd_A_log, bwd_dt_bias, bwd_D, bwd_norm_w, bwd_out_proj):
        import jax, jax.numpy as jnp
        import numpy as np
        CHUNK = 16
        D_MODEL = 32
        D_STATE = 16
        HEADDIM = 16
        D_INNER = 2 * D_MODEL
        NHEADS = D_INNER // HEADDIM
        CONV_DIM = D_INNER + 2 * D_STATE
        K = 4
        D_IN_PROJ = 2 * D_INNER + 2 * D_STATE + NHEADS
        EPS = 1e-05

        def _segsum(t):
            L = t.shape[-1]
            cs = jnp.cumsum(t, -1)
            seg = cs[..., :, None] - cs[..., None, :]
            mask = jnp.tril(jnp.ones((L, L), bool))
            return jnp.where(mask, seg, -jnp.inf)

        def _ssd(xh, dt, A, Bm, Cm):
            b, l, h, p = xh.shape
            n = Bm.shape[-1]
            c = l // CHUNK
            xdt = xh * dt[..., None]
            dA = dt * A
            rc = lambda t: t.reshape(b, c, CHUNK, *t.shape[2:])
            xc, dAc, Bc, Cc = (rc(xdt), rc(dA), rc(Bm), rc(Cm))
            Acs = jnp.cumsum(dAc, axis=2)
            Lmat = jnp.exp(_segsum(dAc.transpose(0, 1, 3, 2)))
            Y_diag = jnp.einsum('bcln,bcsn,bchls,bcshp->bclhp', Cc, Bc, Lmat, xc)
            decay_st = jnp.exp(Acs[:, :, -1:, :] - Acs)
            states = jnp.einsum('bcln,bclh,bclhp->bchpn', Bc, decay_st, xc)
            chunk_decay = jnp.exp(Acs[:, :, -1])

            def step(carry, inp):
                st, dec = inp
                new = st + carry * dec[:, :, None, None]
                return (new, carry)
            init = jnp.zeros((b, h, p, n), xh.dtype)
            _, prev = jax.lax.scan(step, init, (states.transpose(1, 0, 2, 3, 4), chunk_decay.transpose(1, 0, 2)))
            prev = prev.transpose(1, 0, 2, 3, 4)
            Y_off = jnp.einsum('bcln,bchpn,bclh->bclhp', Cc, prev, jnp.exp(Acs))
            return (Y_diag + Y_off).reshape(b, l, h, p)

        def _mamba3(x, in_proj, conv_w, conv_b, A_log, dt_bias, D, norm_w, out_proj):
            b, l, _ = x.shape
            zxbcdt = x @ in_proj
            z, xbc, dt = jnp.split(zxbcdt, [D_INNER, D_INNER + CONV_DIM], axis=-1)
            xp = jnp.pad(xbc, ((0, 0), (K - 1, 0), (0, 0)))
            conv = sum((xp[:, i:i + l, :] * conv_w[:, i] for i in range(K))) + conv_b
            xbc = jax.nn.silu(conv)
            xh, Bm, Cm = jnp.split(xbc, [D_INNER, D_INNER + D_STATE], axis=-1)
            xh = xh.reshape(b, l, NHEADS, HEADDIM)
            dt = jax.nn.softplus(dt + dt_bias)
            A = -jnp.exp(A_log)
            y = _ssd(xh, dt, A, Bm, Cm) + xh * D[None, None, :, None]
            yg = y.reshape(b, l, D_INNER) * jax.nn.silu(z)
            yn = yg * jax.lax.rsqrt(jnp.mean(yg * yg, -1, keepdims=True) + EPS) * norm_w
            return yn @ out_proj
        h_f = _mamba3(x, fwd_in_proj, fwd_conv_w, fwd_conv_b, fwd_A_log, fwd_dt_bias, fwd_D, fwd_norm_w, fwd_out_proj)
        xr = x[:, ::-1, :]
        h_b = _mamba3(xr, bwd_in_proj, bwd_conv_w, bwd_conv_b, bwd_A_log, bwd_dt_bias, bwd_D, bwd_norm_w, bwd_out_proj)[:, ::-1, :]
        return h_f + h_b

    def _L3_ffn_ref(x, ffn_w1, ffn_b1, ffn_w2, ffn_b2, wq, wk, wv, wo, attn_mask, ffn_mask):
        import jax, jax.numpy as jnp
        import numpy as np
        NB, NOPS = (33, 19)
        D, H = (32, 128)
        B, S = (8, 256)
        CARRY_OPS = [0, 1, 2, 10, 11, 12, 13]

        def _build_masks():
            am = np.zeros((NB, NOPS), dtype=bool)
            fm = np.zeros((NB, NOPS), dtype=bool)
            fm[0, :] = True
            for b in range(1, 8):
                am[b, CARRY_OPS] = True
                fm[b, CARRY_OPS] = True
            am[8, [14, 15, 8, 9]] = True
            fm[8, [14, 15, 8, 9]] = True
            for b in range(16, 32):
                fm[b, [3, 4]] = True
            am[32, [10, 11, 12, 13]] = True
            fm[32, [5, 6, 7, 2, 4, 10, 11, 12, 13]] = True
            return (jnp.asarray(am), jnp.asarray(fm))
        scale = jnp.asarray(1.0 / np.sqrt(D), x.dtype)

        def step(h, p):
            op = jnp.argmax(h[0, 0, :NOPS])
            q = h @ p['wq'][op]
            k = h @ p['wk'][op]
            v = h @ p['wv'][op]
            attn = jax.nn.softmax(jnp.einsum('bqd,bkd->bqk', q, k) * scale, axis=-1)
            y = jnp.einsum('bqk,bkd->bqd', attn, v) @ p['wo'][op]
            h = jnp.where(p['am'][op], y, h)
            z = jax.nn.relu(h @ p['w1'][op] + p['b1'][op]) @ p['w2'][op] + p['b2'][op]
            h = jnp.where(p['fm'][op], z, h)
            return (h, None)
        xs = {'w1': ffn_w1, 'b1': ffn_b1, 'w2': ffn_w2, 'b2': ffn_b2, 'wq': wq, 'wk': wk, 'wv': wv, 'wo': wo, 'am': attn_mask, 'fm': ffn_mask}
        out, _ = jax.lax.scan(step, x, xs)
        return out

    def _gn(v, G=32, eps=1e-05):
        B_, C_, H_, W_ = v.shape
        g = v.reshape(B_, G, C_ // G, H_, W_)
        m = jnp.mean(g, axis=(2, 3, 4), keepdims=True)
        s = jnp.var(g, axis=(2, 3, 4), keepdims=True)
        return ((g - m) / jnp.sqrt(s + eps)).reshape(v.shape)

    def _ln_c(v, eps=1e-06):
        m = jnp.mean(v, axis=1, keepdims=True)
        s = jnp.var(v, axis=1, keepdims=True)
        return (v - m) / jnp.sqrt(s + eps)

    def _ln_t(v, eps=1e-05):
        m = jnp.mean(v, axis=-1, keepdims=True)
        s = jnp.var(v, axis=-1, keepdims=True)
        return (v - m) / jnp.sqrt(s + eps)

    def _to_tokens(v):
        B_, C_, H_, W_ = v.shape
        return v.reshape(B_, C_, H_ * W_).transpose(0, 2, 1)

    def _from_tokens(t, like):
        B_, C_, H_, W_ = like.shape
        return t.transpose(0, 2, 1).reshape(B_, C_, H_, W_)
    x = _L0_conv_ref(x, L0_conv_A, L0_conv_Bm, L0_conv_Cm, L0_conv_D, L0_conv_W_in, L0_conv_b_in, L0_conv_W_out, L0_conv_b_out, L0_conv_gamma, L0_conv_beta)
    x = x + _L1_conv_ref(_gn(x), L1_conv_w1, L1_conv_b1, L1_conv_a1, L1_conv_w2, L1_conv_b2, L1_conv_a2, L1_conv_wa, L1_conv_ba, L1_conv_aa)
    t = _to_tokens(x)
    t = t + _L2_attn_ref(_ln_t(t), L2_attn_wq, L2_attn_wk, L2_attn_wv, L2_attn_wo, L2_attn_lora_A_q, L2_attn_lora_B_q, L2_attn_lora_A_k, L2_attn_lora_B_k, L2_attn_lora_A_v, L2_attn_lora_B_v)
    t = t + _L2_ffn_ref(_ln_t(t), L2_ffn_W, L2_ffn_V, L2_ffn_gamma, L2_ffn_beta)
    t = t + _L3_attn_ref(_ln_t(t), L3_attn_fwd_in_proj, L3_attn_fwd_conv_w, L3_attn_fwd_conv_b, L3_attn_fwd_A_log, L3_attn_fwd_dt_bias, L3_attn_fwd_D, L3_attn_fwd_norm_w, L3_attn_fwd_out_proj, L3_attn_bwd_in_proj, L3_attn_bwd_conv_w, L3_attn_bwd_conv_b, L3_attn_bwd_A_log, L3_attn_bwd_dt_bias, L3_attn_bwd_D, L3_attn_bwd_norm_w, L3_attn_bwd_out_proj)
    t = t + _L3_ffn_ref(_ln_t(t), L3_ffn_ffn_w1, L3_ffn_ffn_b1, L3_ffn_ffn_w2, L3_ffn_ffn_b2, L3_ffn_wq, L3_ffn_wk, L3_ffn_wv, L3_ffn_wo, L3_ffn_attn_mask, L3_ffn_ffn_mask)
    x = _from_tokens(t, x)
    return x

_drawn_inputs = setup_inputs


def setup_inputs(seed=0):
    import zlib

    import numpy as np

    out = dict(_drawn_inputs(seed))
    spreads = {'L0_conv_b_in': (0.0, 0.376),
     'L0_conv_b_out': (0.0, 0.1),
     'L0_conv_gamma': (1.0, 0.569),
     'L0_conv_beta': (0.0, 0.79),
     'L1_conv_b1': (0.0, 0.1),
     'L1_conv_b2': (0.0, 0.486),
     'L1_conv_ba': (0.0, 0.1),
     'L2_ffn_gamma': (1.0, 0.6),
     'L2_ffn_beta': (0.0, 0.354),
     'L3_attn_fwd_conv_b': (0.0, 0.1),
     'L3_attn_fwd_D': (1.0, 0.2),
     'L3_attn_fwd_norm_w': (1.0, 0.2),
     'L3_attn_bwd_conv_b': (0.0, 0.1),
     'L3_attn_bwd_D': (1.0, 0.2),
     'L3_attn_bwd_norm_w': (1.0, 0.2),
     'L3_ffn_ffn_b1': (0.0, 0.1),
     'L3_ffn_ffn_b2': (0.0, 0.1)}
    factors = {'L2_attn_wq': 8.0,
     'L2_attn_wk': 8.0,
     'L2_attn_lora_A_q': 8.0,
     'L2_attn_lora_B_q': 8.0,
     'L2_attn_lora_A_k': 8.0,
     'L2_attn_lora_B_k': 8.0,
     'L2_attn_lora_A_v': 6.98,
     'L2_attn_lora_B_v': 7.453,
     'L3_attn_bwd_A_log': 3.618,
     'L3_attn_fwd_dt_bias': 2.769}
    for name, (base, spread) in spreads.items():
        noise = np.random.default_rng([zlib.crc32(name.encode()), seed]).standard_normal(out[name].shape)
        drawn = base * np.exp(spread * noise) if base else spread * noise
        out[name] = jnp.asarray(drawn.astype(out[name].dtype))
    for name, factor in factors.items():
        out[name] = (out[name] * factor).astype(out[name].dtype)
    return out
```

```python
from contextlib import ExitStack

import numpy as np

import concourse.bass as bass
from concourse import mybir

ALU = mybir.AluOpType
ACT = mybir.ActivationFunctionType
F32 = mybir.dt.float32
BF16 = mybir.dt.bfloat16
U32 = mybir.dt.uint32
I32 = mybir.dt.int32
AX = mybir.AxisListType.X

P = 128
B, C, T = 16, 32, 256
G = P // C
J = B // G
N = J * T
HALF = N // 2
TT = T // P
HEADS = 4
HD = C // HEADS
E2 = 2 * C
NS = 16
PH = E2 // HEADS
K = 4
UNROLL = 16
NB, NOPS, HID = 33, 19, 128
EPS = 1e-5
MASKED = -1e30

WEIGHTS = [
    ("ident", P), ("avg_c", P), ("block", P), ("eps", 1), ("zero", 1), ("one", 1),
    ("L0_W_in", P), ("L0_BmT", P), ("L0_AT", P), ("L0_Cm", P), ("L0_W_outT", P),
    ("L0_D", 1), ("L0_b_in", 1), ("L0_W_inT", E2), ("L0_beta", 1), ("L0_gamma", 1), ("L0_b_out", 1),
    ("ones_row", HALF),
    ("L1_w1T", P), ("L1_w2T", P), ("L1_waT", P),
    ("L1_b1", 1), ("L1_b2", 1), ("L1_ba", 1), ("L1_a1", 1), ("L1_a2", 1), ("L1_aa", 1),
    ("neg_ident", P), ("ones32", C), ("group_mask", G),
    ("L2_wqT", P), ("L2_wkT", P), ("L2_wvT", P), ("L2_woT", P),
    ("L2_A_q", P), ("L2_A_k", P), ("L2_A_v", P), ("L2_B_qT", P), ("L2_B_kT", P), ("L2_B_vT", P),
    ("cos", T), ("sin", T), ("head_mask", G * HEADS), ("head_ones", HEADS * C),
    ("F_WT", P), ("F_VT", P), ("F_gamma", 1), ("F_beta", 1), ("avg_g", P),
    ("M_dtW", 32), ("M_dt_bias", 1), ("M_A_log", 1), ("row_head", HEADS),
]
for _d in ("fwd", "bwd"):
    WEIGHTS += [(f"{_d}_proj", E2 + 2 * NS), (f"{_d}_taps", E2 + 2 * NS), (f"{_d}_z", E2), (f"{_d}_bx", E2),
                (f"{_d}_bB", 1), (f"{_d}_bC", 1), (f"{_d}_D", E2), (f"{_d}_norm", 1), (f"{_d}_out", 2 * C)]
COL = {}
NW = 0
for _n, _w in WEIGHTS:
    COL[_n] = (NW, _w)
    NW += _w

CONSTS = [("identb", P), ("zeros", P), ("mask_above", P), ("mask_below", P), ("zeros2", P),
          ("sel_rows", 2 * G * P), ("sel_cols", 2 * G * HEADS)]
CCOL = {}
NC = 0
for _n, _w in CONSTS:
    CCOL[_n] = (NC, _w)
    NC += _w


def hybrid_block(nc, x, weights, consts, w1, b1, w2, b2, wq, wk, wv, wo, attn_mask, ffn_mask, out, upto=99, dump=None):
    with ExitStack() as ctx:
        def sb(name, shape, dt=F32):
            return ctx.enter_context(nc.sbuf_tensor(name, shape, dt))

        class Signals(dict):
            def __missing__(self, what):
                self[what] = ctx.enter_context(nc.semaphore("s_" + what.replace(" ", "_")))
                return self[what]

        s = Signals()

        class Chain:
            def __init__(self, eng, sem):
                self.eng, self.sem, self.n = eng, sem, 0

            def __call__(self, ins):
                self.n += 1
                ins.then_inc(self.sem, 1)
                self.eng.wait_ge(self.sem, self.n)

        ps = ctx.enter_context(nc.psum_tensor("ps", [P, 8, HALF], F32))
        wsb = sb("wsb", [P, NW])
        csb = sb("csb", [P, NC], BF16)

        def W(name, rows=P):
            at, w = COL[name]
            return wsb[0:rows, at:at + w]

        def CB(name, rows=P):
            at, w = CCOL[name]
            return csb[0:rows, at:at + w]

        def CB_pair(first, second):
            assert CCOL[first][0] + CCOL[first][1] == CCOL[second][0]
            return csb[:, CCOL[first][0]:CCOL[second][0] + CCOL[second][1]]

        def banks(a, b):
            return ps[:, a:b, :].rearrange("p a b -> p (a b)")

        X = sb("X", [P, N])
        xc = sb("xc", [P, N])
        sq = sb("sq", [P, N])
        xn = sb("xn", [P, N])
        u_w = sb("u_w", [P, P])
        g1 = sb("g1", [P, P])
        g2 = sb("g2", [P, P])
        d_wout = sb("d_wout", [E2, P])
        z_b = sb("z_b", [E2, 1])
        u_brow = sb("u_brow", [1, P])
        o_b = sb("o_b", [P, 1])
        st = sb("st", [P, J, T + 1])
        bn6 = sb("bn6", [P, J, 6])
        mv = sb("mv", [P, J, 2])
        rstd = sb("rstd", [P, J])
        prob = sb("prob", [P, 2, 3 * HALF])
        oat = sb("oat", [P, N])
        lora = sb("lora", [P, 3, P])
        den = sb("den", [P, N])
        vt = sb("vt", [P, J * TT, P])
        arena = sb("arena", [P, 29696])

        class Arena:
            def __init__(self):
                self.at = 0

            def __call__(self, *dims):
                n = int(np.prod(dims))
                v = arena[:, self.at:self.at + n]
                self.at += n
                assert self.at <= 29696
                names = " ".join("abcd"[:len(dims)])
                if len(dims) == 1:
                    return v
                return v.rearrange(f"p ({names}) -> p {names}", **dict(zip("abcd", dims)))

        at = Arena()
        pr = at(3, N)
        pm = at(3, N)
        e2z = at(G, J, T)
        mbx = at(J, TT, P)
        e1m = at(N)
        at = Arena()
        wqkv = at(3, P)
        wrot = at(2, P)
        qk = at(2, N)
        qrs = at(N)
        kz = at(G * HEADS, J, T)
        vz = at(HEADS, J * TT * G, C)
        mb = at(J * TT * G * HEADS)
        nmr = at(P)
        nm = sb("nm", [P, 2, P], BF16)
        fst = sb("fst", [P, 8])
        at = Arena()
        xs = at(J, G, T + K - 1)
        wxz = at(2, 2 * E2)
        wbc = at(2, 2, C)
        wout = at(2, 2 * C)
        xt = at(J * TT, G, E2)
        zt = at(J * TT, G, E2)
        xdt = at(J * TT, G, E2)
        bp = at(N)
        cp = at(N)
        bz = at(G, J, T)
        dtt = at(J * TT, 2 * G * HEADS)
        yt = at(J * TT, G, E2)
        ysq = xdt
        yf = at(2, 2, N)
        decay = at(2, HALF)
        gram = at(2, HALF)
        drow = yf.rearrange("p a b c -> p (a b) c")
        cs = at(J, T + 1)
        c3 = sb("c3", [3 * 32, J, T + 1], BF16)
        c3x = sb("c3x", [3 * 32, HEADS, J * (T + 1)], BF16)
        mst = sb("mst", [P, 2, J * TT * G])

        xr = x.rearrange("(j g) c h w -> (g c) j (h w)", g=G)
        Xj = X[:].rearrange("p (j t) -> p j t", j=J)

        def halves(t):
            return [t[:, h * HALF:(h + 1) * HALF] for h in range(2)]

        def norm_tensor(pe, n):
            for h in range(2):
                pe.wait_ge(s["X ready"], n + 1)
                nc.tensor.matmul(ps[:, h, :], W("avg_c"), halves(X)[h], start=True, stop=True).then_inc(s["mean"], 1)
            for h in range(2):
                pe.wait_ge(s["squares"], 2 * n + h + 1)
                nc.tensor.matmul(ps[:, 2 + h, :], W("avg_c"), halves(sq)[h], start=True, stop=True).then_inc(s["variance"], 1)

        def norm_vector(dve, n):
            for h in range(2):
                dve.wait_ge(s["mean"], 2 * n + h + 1)
                nc.vector.tensor_tensor(halves(xc)[h], halves(X)[h], ps[:, h, :], ALU.subtract).then_inc(s["centred"], 1)
            for h in range(2):
                dve.wait_ge(s["sigma"], 2 * n + h + 1)
                nc.vector.reciprocal(halves(sq)[h], halves(sq)[h]).then_inc(s["1/sigma"], 1)
            for h in range(2):
                dve.wait_ge(s["1/sigma"], 2 * n + h + 1)
                nc.vector.tensor_tensor(halves(xn)[h], halves(xc)[h], halves(sq)[h], ALU.mult).then_inc(s["normalised"], 1)

        def norm_scalar(act, n):
            for h in range(2):
                act.wait_ge(s["centred"], 2 * n + h + 1)
                nc.scalar.activation(halves(sq)[h], halves(xc)[h], ACT.Square).then_inc(s["squares"], 1)
            for h in range(2):
                act.wait_ge(s["variance"], 2 * n + h + 1)
                nc.scalar.activation(halves(sq)[h], ps[:, 2 + h, :], ACT.Sqrt, bias=W("eps")).then_inc(s["sigma"], 1)

        def recur_tensor(pe, n, wt, states):
            for tc in range(TT):
                with pe.Fori(0, P // UNROLL) as turn:
                    t0 = turn * UNROLL
                    for k in range(UNROLL):
                        pe.wait_ge(s["state"], t0 + (n * T + tc * P + k + 1))
                        nc.tensor.matmul(ps[:, tc, :].rearrange("p (j t) -> p j t", j=J)[:, :, bass.ds(t0 + k, 1)],
                                         wt, states[:, :, bass.ds(t0 + (tc * P + k), 1)],
                                         start=False, stop=True, skip_group_check=True).then_inc(s["pre-state"], 1)

        def recur_scalar(act, n, func, states):
            for tc in range(TT):
                with act.Fori(0, P // UNROLL) as turn:
                    t0 = turn * UNROLL
                    for k in range(UNROLL):
                        act.wait_ge(s["pre-state"], t0 + (n * T + tc * P + k + 1))
                        nc.scalar.activation(states[:, :, bass.ds(t0 + (tc * P + k + 1), 1)],
                                             ps[:, tc, :].rearrange("p (j t) -> p j t", j=J)[:, :, bass.ds(t0 + k, 1)],
                                             func).then_inc(s["state"], 1)

        def dve_y(dve, d, quarter):
            dve.wait_ge(s["M products"], 3 * B * d + 12 * (quarter + 1))
            if quarter == 0 and d == 1:
                dve.wait_ge(s["M rows turned"], 1)
            src = ps[:, 6 + quarter % 2, :].rearrange("p (g a e) -> p a g e", g=G, a=TT)
            nc.vector.tensor_copy(yt[:, quarter * TT:(quarter + 1) * TT, :, :], src).then_inc(s["M y"], 1)

        at = Arena()
        w1z = at(G, HID)
        wbd = at(4, P)
        hidden = at(2 * G, HALF)
        rq = at(2, N)
        rkz = at(G, J, T)
        rmb = at(J * TT * G)
        w2s = at(C)
        b1s = at(1)
        b2s = at(1)
        h0 = sb("h0", [C, C])
        best = sb("best", [1, 8])
        op_at = sb("op_at", [1, 8], U32)
        masks = sb("masks", [1, 2, NB * NOPS], I32)
        either = at(NB * NOPS)[0:1].bitcast(I32)
        rnm = sb("rnm", [J * TT * G, 2, P], BF16)

        def routed(name, eng, attention, feed_forward, picked):
            count = [eng.alloc_register(f"n_{what}") for what in ("pick", "attention", "ffn")]
            for r in count:
                eng.reg_mov(r, 0)
            op, any_, use_a, use_f = (eng.alloc_register(r) for r in ("op", "any_mask", "attention_mask", "ffn_mask"))
            eng.wait_ge(s["op picked"], 1)
            eng.reg_load(op, op_at[0:1, 0:1])
            with eng.Fori(0, NB) as block_i:
                at_op = nc.s_assert_within(block_i * NOPS + eng.snap(op), 0, NB * NOPS - 1)
                eng.reg_load(any_, either[0:1, bass.ds(at_op, 1)])
                with eng.If_ne(any_, 0):
                    eng.reg_load(use_a, masks[0:1, 0, bass.ds(at_op, 1)])
                    eng.reg_load(use_f, masks[0:1, 1, bass.ds(at_op, 1)])
                    o = nc.s_assert_within(eng.snap(op), 0, NOPS - 1)
                    with eng.If_ne(use_a, 0):
                        attention(block_i, o, eng.snap(count[1]))
                        eng.reg_add(count[1], count[1], 1)
                    eng.reg_add(count[0], count[0], 1)
                    with eng.If_ne(use_f, 0):
                        feed_forward(block_i, o, eng.snap(count[2]))
                        eng.reg_add(count[2], count[2], 1)
                    picked(eng.snap(count[0]))
                    eng.wait_ge(s["op picked"], eng.snap(count[0]) + 1)
                    eng.sem_inc(s[name + " saw the pick"], 1)
                    eng.reg_load(op, op_at[0:1, 0:1])

        M_BLOCKS = (((0, 0), (0, 1), (1, 1)), ((0, 0), (1, 0), (1, 1)))

        block = ctx.enter_context(nc.Block())

        @block.sync
        def _(sp):
            sp.dma_start(Xj, xr).then_inc(s["x loaded"], 16)
            sp.dma_start(wsb[:], weights).then_inc(s["weights loaded"], 16)
            sp.dma_start(csb[:], consts).then_inc(s["consts loaded"], 16)
            if upto >= 4:
                sp.wait_ge(s["M weights"], 1)
                sp.wait_ge(s["normalised"], 8)
                for i in range(K):
                    for g in range(G):
                        sp.dma_start(xs[C * i:C * i + C, :, g, K - 1 - i:K - 1 - i + T],
                                     xn[C * g:C * g + C, :].rearrange("p (j t) -> p j t", j=J)).then_inc(s["M stack"], 16)
            if upto < 99:
                sp.wait_ge(s["stage done"], 1)
                if dump == "X":
                    sp.dma_start(out.rearrange("(j g) c h w -> (g c) j (h w)", g=G), Xj).then_inc(s["stored"], 16)
                sp.wait_ge(s["stored"], 16)
                return
            sp.dma_start(masks[:, 0, :], attn_mask.rearrange("(a n) o -> a (n o)", a=1)).then_inc(s["masks loaded"], 16)
            sp.dma_start(masks[:, 1, :], ffn_mask.rearrange("(a n) o -> a (n o)", a=1)).then_inc(s["masks loaded"], 16)
            sp.wait_ge(s["R cleared"], 1)

            def attention(i, op, n):
                for m, w in enumerate((wq, wk, wv, wo)):
                    for g in range(G):
                        sp.dma_start(wbd[C * g:C * g + C, m, C * g:C * g + C],
                                     w[bass.ds(i, 1), bass.ds(op, 1), :, :].rearrange("a b c d -> (a b c) d"))\
                            .then_inc(s["R attention weights"], 16)

            def feed_forward(i, op, n):
                at = (bass.ds(i, 1), bass.ds(op, 1))
                for g in range(G):
                    sp.dma_start(w1z[C * g:C * g + C, g, :], w1[at[0], at[1], :, :].rearrange("a b c d -> (a b c) d"))\
                        .then_inc(s["R ffn weights"], 16)
                sp.dma_start(b1s, b1[at[0], at[1], :].rearrange("a b (c d) -> (a b c) d", d=1)).then_inc(s["R ffn weights"], 16)
                sp.dma_start(w2s, w2[at[0], at[1], :, :].rearrange("a b c d -> (a b c) d")).then_inc(s["R ffn weights"], 16)
                sp.dma_start(b2s, b2[at[0], at[1], :].rearrange("a b (c d) -> (a b) c d", d=1).to_broadcast([G, C, 1]))\
                    .then_inc(s["R ffn weights"], 16)

            routed("sync", sp, attention, feed_forward, lambda n: None)
            sp.wait_ge(s["X ready"], 6)
            sp.dma_start(out.rearrange("(j g) c h w -> (g c) j (h w)", g=G), Xj).then_inc(s["stored"], 16)
            sp.wait_ge(s["stored"], 16)

        @block.tensor
        def _(pe):
            pe.wait_ge(s["weights loaded"], 16)
            nc.tensor.matmul(ps[:, 4, 0:P], W("L0_W_in", E2), W("L0_BmT", E2), start=True, stop=True)
            nc.tensor.matmul(ps[:, 4, P:2 * P], W("L0_Cm", E2), W("L0_W_outT", E2), start=True, stop=True)
            nc.tensor.matmul(ps[0:E2, 5, 0:1], W("L0_W_inT", C), W("L0_beta", C), start=True, stop=True).then_inc(s["L0 folds"], 1)
            pe.wait_ge(s["L0 z bias"], 1)
            nc.tensor.matmul(ps[:, 4, 2 * P:3 * P], W("L0_W_in", E2), d_wout[:], start=True, stop=True)
            nc.tensor.matmul(ps[0:1, 5, P:2 * P], z_b[:], W("L0_BmT", E2), start=True, stop=True)
            nc.tensor.matmul(ps[:, 5, 1:2], d_wout[:], z_b[:], start=True, stop=True).then_inc(s["L0 folds"], 1)
            for i, w in enumerate("qkv"):
                mm = nc.tensor.matmul(ps[:, 6, i * P:(i + 1) * P], W("L2_A_" + w, HD), W(f"L2_B_{w}T", HD), start=True, stop=True)
            mm.then_inc(s["lora products"], 1)
            norm_tensor(pe, 0)
            pe.wait_ge(s["L0 weights"], 1)
            pe.wait_ge(s["normalised"], 2)
            xnj = xn[:].rearrange("p (j t) -> p j t", j=J)
            for tc in range(TT):
                nc.tensor.matmul(ps[:, tc, :], u_w[:], xnj[:, :, tc * P:(tc + 1) * P], start=True, stop=False)
                mm = nc.tensor.matmul(ps[:, tc, :], u_brow[:], W("ones_row", 1), start=False, stop=True)
            pe.wait_ge(s["start state"], 1)
            recur_tensor(pe, 0, W("L0_AT"), st)
            pe.wait_ge(s["state"], T + 1)
            for h in range(2):
                nc.tensor.matmul(ps[:, 2 + h, :], g1[:], st[:, 2 * h:2 * h + 2, 1:T + 1], start=True, stop=False)
                nc.tensor.matmul(ps[:, 2 + h, :], g2[:], halves(xn)[h], start=False, stop=True).then_inc(s["L0 out"], 1)
            pe.wait_ge(s["gn done"], 1)
            for i, w in enumerate(("L1_w1T", "L1_w2T", "L1_waT")):
                for h in range(2):
                    nc.tensor.matmul(ps[:, 2 * i + h, :], W(w), halves(xn)[h], start=True, stop=True).then_inc(s["L1 proj"], 1)
            pe.wait_ge(s["L1 prelu"], 3)
            for jt in range(J * TT):
                mm = nc.tensor.matmul(ps[:, 6 + jt // 4, (jt % 4) * P:(jt % 4 + 1) * P], pm[:, 2, jt * P:(jt + 1) * P],
                                      W("ident"), is_transpose=True, start=True, stop=True)
            mm.then_inc(s["values turned"], 1)
            pe.wait_ge(s["L1 keys"], 1)
            q1 = pm[:, 0, :].rearrange("p (j t) -> p j t", j=J)
            for b in range(B):
                j, g = b // G, b % G
                if b >= 4:
                    pe.wait_ge(s["L1 max"], b - 3)
                for qt in range(TT):
                    mm = nc.tensor.matmul(ps[:, b % 4, qt * T:(qt + 1) * T], q1[:, j, qt * P:(qt + 1) * P], e2z[:, g, j, :],
                                          start=True, stop=True)
                mm.then_inc(s["L1 scores"], 1)
            pe.wait_ge(s["L1 max"], B)
            for jt in range(J * TT):
                mm = nc.tensor.matmul(ps[:, 4 + jt // 4, (jt % 4) * P:(jt % 4 + 1) * P], mbx[:, jt // TT, jt % TT, :],
                                      W("neg_ident"), start=True, stop=True)
            mm.then_inc(s["L1 max rows"], 1)
            pe.wait_ge(s["L1 queries"], 1)
            q2 = e1m[:].rearrange("p (j t) -> p j t", j=J)
            pe.wait_ge(s["values by token"], 1)
            for b in range(B + 1):
                if b < B:
                    j, g = b // G, b % G
                    if b >= 4:
                        pe.wait_ge(s["L1 exp"], b - 3)
                    for kt in range(TT):
                        mm = nc.tensor.matmul(ps[:, b % 4, kt * T:(kt + 1) * T], e2z[:, g, j, kt * P:(kt + 1) * P], q2[:, j, :],
                                              start=True, stop=True)
                    mm.then_inc(s["L1 scores T"], 1)
                if b >= 1:
                    j, g = (b - 1) // G, (b - 1) % G
                    pe.wait_ge(s["L1 exp"], b)
                    for kt in range(TT):
                        pk = prob[:, (b - 1) % 2, kt * T:(kt + 1) * T]
                        cols = slice((j % 2) * T, (j % 2 + 1) * T)
                        nc.tensor.matmul(ps[C * g:C * g + C, 4 + j // 2, cols], vt[:, j * TT + kt, C * g:C * g + C], pk,
                                         start=(kt == 0), stop=(kt == TT - 1))
                        mm = nc.tensor.matmul(ps[C * g:C * g + C, 6 + j // 2, cols], W("ones32"), pk,
                                              start=(kt == 0), stop=(kt == TT - 1))
                    mm.then_inc(s["L1 pv"], 1)
            if upto == 1:
                return
            norm_tensor(pe, 1)
            pe.wait_ge(s["L2 weights"], 1)
            pe.wait_ge(s["normalised"], 4)
            for i, w in enumerate((wqkv[:, 0, :], wrot[:, 0, :], wqkv[:, 1, :], wrot[:, 1, :])):
                for h in range(2):
                    if i < 2:
                        pe.wait_ge(s["normalised"], 4)
                    mm = nc.tensor.matmul(ps[:, 2 * i + h, :], w, halves(xn)[h], start=True, stop=True)
                mm.then_inc(s["L2 proj"], 1)
            pe.wait_ge(s["L2 rotated"], 2)
            for h in range(2):
                mm = nc.tensor.matmul(ps[:, h, :], wqkv[:, 2, :], halves(xn)[h], start=True, stop=True)
            mm.then_inc(s["L2 proj"], 1)
            pe.wait_ge(s["L2 values"], 1)
            for jt in range(J * TT):
                mm = nc.tensor.matmul(ps[:, 2 + jt // 4, (jt % 4) * P:(jt % 4 + 1) * P], oat[:, jt * P:(jt + 1) * P],
                                      W("ident"), is_transpose=True, start=True, stop=True)
            mm.then_inc(s["values turned"], 1)
            pe.wait_ge(s["consts loaded"], 16)
            pe.wait_ge(s["L2 keys scalar"], 1)
            pe.wait_ge(s["L2 values split"], 1)
            q = qk[:, 0, :].rearrange("p (j t) -> p j t", j=J)
            for b in range(B):
                j, g = b // G, b % G
                k0 = 3 * (b % 2)
                if b >= 2:
                    pe.wait_ge(s["L2 max"], 2 * b - 2)
                nc.tensor.matmul(ps[:, k0, :], CB("identb"), CB("mask_above").unsqueeze(1).to_broadcast([P, HEADS, P]),
                                 start=True, stop=False)
                for h in range(HEADS):
                    nc.tensor.matmul(ps[:, k0, h * P:(h + 1) * P], q[:, j, 0:P], kz[:, g * HEADS + h, j, 0:P],
                                     start=False, stop=(h == HEADS - 1))
                for pair in range(2):
                    nc.tensor.matmul(ps[:, k0 + 1 + pair, :], CB("identb"),
                                     CB_pair("zeros", "mask_above").unsqueeze(1).to_broadcast([P, 2, T]), start=True, stop=False)
                    for h in range(2):
                        mm = nc.tensor.matmul(ps[:, k0 + 1 + pair, h * T:(h + 1) * T], q[:, j, P:T],
                                              kz[:, g * HEADS + 2 * pair + h, j, :], start=False, stop=(h == 1))
                mm.then_inc(s["L2 scores"], 1)
            pe.wait_ge(s["L2 max"], 2 * B)
            nc.tensor.matmul(ps[:, 6, 0:P], mb, W("neg_ident"), start=True, stop=True).then_inc(s["L2 max rows"], 1)
            pe.wait_ge(s["L2 max parts"], 2)
            for b in range(B + 1):
                if b < B:
                    j, g = b // G, b % G
                    if b >= 1:
                        pe.wait_ge(s["L2 exp"], 2 * b - 1)
                    for pair in range(2):
                        nc.tensor.matmul(ps[:, pair, :], CB("identb"),
                                         CB_pair("mask_below", "zeros2").unsqueeze(1).to_broadcast([P, 2, T]), start=True, stop=False)
                        for h in range(2):
                            gh = g * HEADS + 2 * pair + h
                            nc.tensor.matmul(ps[:, pair, h * T:(h + 1) * T], kz[:, gh, j, 0:P], q[:, j, :], start=False, stop=False)
                            for qt in range(TT):
                                row = (j * TT + qt) * G * HEADS + gh
                                for part in range(2):
                                    mm = nc.tensor.matmul(ps[:, pair, h * T + qt * P:h * T + (qt + 1) * P],
                                                          CB("identb")[:, row:row + 1].to_broadcast([P, P]), nm[:, part, :],
                                                          start=False, stop=(h == 1 and qt == 1 and part == 1))
                    mm.then_inc(s["L2 scores T"], 1)
                    if b >= 1:
                        pe.wait_ge(s["L2 exp"], 2 * b)
                    nc.tensor.matmul(ps[:, 2, :], CB("identb"), CB("mask_below").unsqueeze(1).to_broadcast([P, HEADS, P]),
                                     start=True, stop=False)
                    for h in range(HEADS):
                        gh = g * HEADS + h
                        row = (j * TT + 1) * G * HEADS + gh
                        nc.tensor.matmul(ps[:, 2, h * P:(h + 1) * P], kz[:, gh, j, P:T], q[:, j, P:T], start=False, stop=False)
                        for part in range(2):
                            mm = nc.tensor.matmul(ps[:, 2, h * P:(h + 1) * P], CB("identb")[:, row:row + 1].to_broadcast([P, P]),
                                                  nm[:, part, :], start=False, stop=(h == HEADS - 1 and part == 1))
                    mm.then_inc(s["L2 scores T"], 1)
                if b >= 1:
                    j, g = (b - 1) // G, (b - 1) % G
                    pe.wait_ge(s["L2 exp"], 2 * b)
                    for bank, lhs in ((4, lambda h, kt: vz[:, h, (j * TT + kt) * G + g, :]),
                                      (6, lambda h, kt: W("head_ones")[:, C * h:C * h + C])):
                        for h in range(HEADS):
                            c0 = (j % 2) * T
                            nc.tensor.matmul(ps[C * g:C * g + C, bank + j // 2, c0:c0 + T], lhs(h, 0),
                                             prob[:, (b - 1) % 2, h * T:(h + 1) * T], start=(h == 0), stop=False)
                            mm = nc.tensor.matmul(ps[C * g:C * g + C, bank + j // 2, c0 + P:c0 + T], lhs(h, 1),
                                                  prob[:, (b - 1) % 2, 2 * HALF + h * P:2 * HALF + (h + 1) * P],
                                                  start=False, stop=(h == HEADS - 1))
                    mm.then_inc(s["L2 pv"], 1)
            pe.wait_ge(s["L2 attended"], 1)
            for h in range(2):
                nc.tensor.matmul(ps[:, h, :], W("L2_woT"), halves(oat)[h], start=True, stop=True).then_inc(s["L2 out"], 1)
            if upto == 2:
                return
            norm_tensor(pe, 2)
            pe.wait_ge(s["normalised"], 6)
            for h in range(2):
                nc.tensor.matmul(ps[:, 4 + h, :], W("F_WT"), halves(xn)[h], start=True, stop=True).then_inc(s["F proj"], 1)
            pe.wait_ge(s["F row stats"], 1)
            nc.tensor.matmul(ps[:, 6, 0:2], W("avg_g"), fst[:, 0:2], start=True, stop=True).then_inc(s["F stats"], 1)
            pe.wait_ge(s["F input"], 1)
            for tc in range(TT):
                nc.tensor.matmul(ps[:, tc, :], W("ident"), xnj[:, :, tc * P:(tc + 1) * P], start=True, stop=True)
            recur_tensor(pe, 1, W("F_VT"), st)
            if upto == 3:
                return
            norm_tensor(pe, 3)
            pe.wait_ge(s["normalised"], 8)
            for h in range(2):
                mm = nc.tensor.matmul(ps[0:2 * G * HEADS, 4 + h, :], W("M_dtW"), halves(xn)[h], start=True, stop=True)
            mm.then_inc(s["M dt proj"], 1)
            pe.wait_ge(s["M dt"], 1)
            dt_rows = drow[0:2 * G * HEADS, 3, :]
            for jt in range(J * TT):
                mm = nc.tensor.matmul(ps[:, 6, jt * 2 * G * HEADS:(jt + 1) * 2 * G * HEADS], dt_rows[:, jt * P:(jt + 1) * P],
                                      W("ident", 2 * G * HEADS)[:, 0:2 * G * HEADS], is_transpose=True, start=True, stop=True)
            mm.then_inc(s["M dt turned"], 1)
            pe.wait_ge(s["M decay parts"], 1)
            pe.wait_ge(s["M weights"], 1)
            pe.wait_ge(s["M stack"], 16 * K * G)
            for d in range(2):
                off = (K - 1) * d
                for r in range(2):
                    for k in range(16):
                        jt, g = (r * 16 + k) // G, (r * 16 + k) % G
                        if d == 1 and r == 0 and k == 0:
                            pe.wait_ge(s["M turned"], 1)
                        if k == 0 and r == 1 and d == 0:
                            pe.wait_ge(s["M dt by token"], 1)
                        mm = nc.tensor.matmul(ps[:, 4 * r + k // 4, (k % 4) * P:(k % 4 + 1) * P],
                                              xs[:, jt // TT, g, off + (jt % TT) * P:off + (jt % TT + 1) * P], wxz[:, d, :],
                                              start=True, stop=True)
                        if k % 4 == 3:
                            mm.then_inc(s["M xz"], 1)
                pe.wait_ge(s["M z"], 8 * d + 4)
                for i in range(2):
                    for h in range(2):
                        for g in range(G):
                            mm = nc.tensor.matmul(ps[C * g:C * g + C, 2 * i + h, :], wbc[:, d, i, :],
                                                  xs[:, 2 * h:2 * h + 2, g, off:off + T], start=True, stop=True)
                    mm.then_inc(s["M bc"], 1)
                pe.wait_ge(s["M xdt"], d + 1)
                pe.wait_ge(s["M B split"], d + 1)
                pe.wait_ge(s["M C"], d + 1)
                pe.wait_ge(s["M z"], 8 * d + 8)
                cpj = cp.rearrange("p (j t) -> p j t", j=J)
                blocks = M_BLOCKS[d]

                def scores(b):
                    j, g = b // G, b % G
                    for n, (st_, tt_) in enumerate(blocks):
                        mm = nc.tensor.matmul(ps[:, 4 + b % 2, n * P:(n + 1) * P], bz[:, g, j, st_ * P:(st_ + 1) * P],
                                              cpj[:, j, tt_ * P:(tt_ + 1) * P], start=(n == 0), stop=(n == 2))
                    mm.then_inc(s["M CB"], 1)

                for n in range(3 * B + 2):
                    if n < 3 * B:
                        b, (st_, tt_) = n // 3, blocks[n % 3]
                        j, g = b // G, b % G
                        count = 3 * B * d + n
                        if count >= 4:
                            pe.wait_ge(s["M decay"], count - 3)
                        if n % 3 == 0:
                            if 3 * B * d + 3 * (b - 1) > 0 and b >= 2:
                                pe.wait_ge(s["M gram"], 3 * B * d + 3 * (b - 1))
                            scores(b)
                        diag = st_ == tt_
                        if diag:
                            nc.tensor.matmul(ps[:, n % 4, :], CB("identb"),
                                             CB("mask_below" if d == 0 else "mask_above").unsqueeze(1).to_broadcast([P, HEADS, P]),
                                             start=True, stop=False)
                        c0 = (1 - d) + st_ * P
                        nc.tensor.matmul(ps[:, n % 4, :], c3[:, j, c0:c0 + P],
                                         CB("sel_cols", 96)[:, (d * G + g) * HEADS:(d * G + g + 1) * HEADS].unsqueeze(2)
                                         .to_broadcast([96, HEADS, P]), start=not diag, stop=False)
                        c0 = j * (T + 1) + (1 - d) + tt_ * P
                        nc.tensor.matmul(ps[:, n % 4, :], CB("sel_rows", 96)[:, (d * G + g) * P:(d * G + g + 1) * P],
                                         c3x[:, :, c0:c0 + P], start=False, stop=True).then_inc(s["M exponent"], 1)
                    if n >= 2:
                        m = n - 2
                        b, (st_, tt_) = m // 3, blocks[m % 3]
                        j, g = b // G, b % G
                        bank = 6 + (b // 4) % 2
                        if m % 12 == 0 and 4 * d + b // 4 >= 2:
                            pe.wait_ge(s["M y"], 4 * d + b // 4 - 1)
                        pe.wait_ge(s["M gram"], 3 * B * d + m + 1)
                        for h in range(HEADS):
                            c0 = (b % 4) * 2 * E2 + tt_ * E2 + h * PH
                            mm = nc.tensor.matmul(ps[:, bank, c0:c0 + PH], gram[:, m % 2, h * P:(h + 1) * P],
                                                  xdt[:, j * TT + st_, g, h * PH:(h + 1) * PH],
                                                  start=(m % 12 == 0 and h == 0), stop=(m % 12 == 11 and h == HEADS - 1))
                        mm.then_inc(s["M products"], 1)
                pe.wait_ge(s["M normed"], d + 1)
                pe.wait_ge(s["M decay"], 3 * B * (d + 1))
                for jt in range(J * TT):
                    for gp in range(2):
                        j, tt_ = jt // TT, jt % TT
                        c0 = (j % 2) * T + tt_ * P
                        mm = nc.tensor.matmul(ps[:, 2 * gp + j // 2, c0:c0 + P], yt[:, jt, 2 * gp:2 * gp + 2, :].rearrange("p a b -> p (a b)"),
                                              W("ident"), is_transpose=True, start=True, stop=True)
                mm.then_inc(s["M rows turned"], 1)
            pe.wait_ge(s["M turned"], 2)
            for h in range(2):
                for g in range(G):
                    for d in range(2):
                        mm = nc.tensor.matmul(ps[C * g:C * g + C, 4 + h, :], wout[:, d, (g % 2) * C:(g % 2 + 1) * C],
                                              yf[:, d, g // 2, h * HALF:(h + 1) * HALF], start=(d == 0), stop=(d == 1))
            mm.then_inc(s["M out"], 1)
            if upto == 4:
                return
            norm_tensor(pe, 4)

            def attention(i, op, n):
                pe.wait_ge(s["R attention weights"], n * 256 + 256)
                for m in range(3):
                    for h in range(2):
                        mm = nc.tensor.matmul(ps[:, 2 * m + h, :], wbd[:, m, :], halves(xn)[h], start=True, stop=True)
                    mm.then_inc(s["R proj"], 1)
                pe.wait_ge(s["R copied"], n * 3 + 3)
                for jt in range(J * TT):
                    mm = nc.tensor.matmul(ps[:, 6 + jt // 4, (jt % 4) * P:(jt % 4 + 1) * P], oat[:, jt * P:(jt + 1) * P],
                                          W("ident"), is_transpose=True, start=True, stop=True)
                mm.then_inc(s["R values turned"], 1)
                pe.wait_ge(s["R keys"], n + 1)
                q = rq[:, 0, :].rearrange("p (j t) -> p j t", j=J)
                for b in range(B):
                    j, g = b // G, b % G
                    if b >= 4:
                        pe.wait_ge(s["R max"], n * B + (b - 3))
                    for qt in range(TT):
                        mm = nc.tensor.matmul(ps[:, b % 4, qt * T:(qt + 1) * T], q[:, j, qt * P:(qt + 1) * P], rkz[:, g, j, :],
                                              start=True, stop=True)
                    mm.then_inc(s["R scores"], 1)
                pe.wait_ge(s["R max"], n * B + B)
                nc.tensor.matmul(ps[0:J * TT * G, 4, 0:P], rmb, W("neg_ident"), start=True, stop=True).then_inc(s["R max rows"], 1)
                pe.wait_ge(s["R max parts"], n * 2 + 2)
                pe.wait_ge(s["R values by token"], n + 1)
                rows = J * TT * G
                for b in range(B + 1):
                    if b < B:
                        j, g = b // G, b % G
                        if b >= 4:
                            pe.wait_ge(s["R exp"], n * B + (b - 3))
                        for kt in range(TT):
                            nc.tensor.matmul(ps[:, b % 4, kt * T:(kt + 1) * T], rkz[:, g, j, kt * P:(kt + 1) * P], q[:, j, :],
                                             start=(kt == 0), stop=False)
                            for qt in range(TT):
                                row = (j * TT + qt) * G + g
                                for part in range(2):
                                    c0 = kt * T + qt * P
                                    mm = nc.tensor.matmul(ps[:, b % 4, c0:c0 + P],
                                                          CB("identb", rows)[:, row:row + 1].to_broadcast([rows, P]),
                                                          rnm[:, part, :], start=False, stop=(kt == 1 and qt == 1 and part == 1))
                        mm.then_inc(s["R scores T"], 1)
                    if b >= 1:
                        j, g = (b - 1) // G, (b - 1) % G
                        pe.wait_ge(s["R exp"], n * B + b)
                        for kt in range(TT):
                            pk = prob[:, (b - 1) % 2, kt * T:(kt + 1) * T]
                            cols = slice((j % 2) * T, (j % 2 + 1) * T)
                            nc.tensor.matmul(ps[C * g:C * g + C, 4 + j // 2, cols], vt[:, j * TT + kt, C * g:C * g + C], pk,
                                             start=(kt == 0), stop=(kt == TT - 1))
                            mm = nc.tensor.matmul(ps[C * g:C * g + C, 6 + j // 2, cols], W("ones32"), pk,
                                                  start=(kt == 0), stop=(kt == TT - 1))
                        mm.then_inc(s["R pv"], 1)
                pe.wait_ge(s["R attended"], n + 1)
                for h in range(2):
                    mm = nc.tensor.matmul(ps[:, h, :], wbd[:, 3, :], halves(oat)[h], start=True, stop=True)
                mm.then_inc(s["R attention out"], 1)
                pe.wait_ge(s["R attention written"], n + 1)

            def feed_forward(i, op, n):
                pe.wait_ge(s["R ffn weights"], n * 112 + 112)
                for k in range(2 * G + 1):
                    if k < 2 * G:
                        if k >= 4:
                            done = s["R relu scalar"] if k % 2 == 0 else s["R relu vector"]
                            pe.wait_ge(done, n * 4 + (k - 4) // 2 + 1)
                        nc.tensor.matmul(ps[:, k % 4, :], w1z[:, k % G, :], halves(xn)[k // G], start=True, stop=True)\
                            .then_inc(s["R hidden"], 1)
                    if k >= 1:
                        m = k - 1
                        pe.wait_ge(s["R relu scalar"] if m % 2 == 0 else s["R relu vector"], n * 4 + m // 2 + 1)
                        g = m % G
                        nc.tensor.matmul(ps[C * g:C * g + C, 4 + m // G, :], w2s, hidden[:, m, :], start=True, stop=True)\
                            .then_inc(s["R ffn out"], 1)

            routed("tensor", pe, attention, feed_forward, lambda n: None)

        @block.scalar
        def _(act):
            norm_scalar(act, 0)
            act.preload_act_table(ACT.Tanh)
            act.wait_ge(s["X ready"], 1)
            nc.scalar.activation(st[:, :, 0:1], X[:, 0:J].rearrange("p (j t) -> p j t", t=1), ACT.Copy, scale=0.0).then_inc(s["state"], 1)
            recur_scalar(act, 0, ACT.Tanh, st)
            act.wait_ge(s["gn stats"], 1)
            nc.scalar.activation(rstd[:], mv[:, :, 1], ACT.Sqrt, bias=W("eps")).then_inc(s["gn sigma"], 1)
            for i, bias in enumerate(("L1_b1", "L1_b2", "L1_ba")):
                act.wait_ge(s["L1 proj"], 2 * i + 2)
                nc.scalar.activation(pr[:, i, :], ps[:, 2 * i:2 * i + 2, :].rearrange("p a b -> p (a b)"), ACT.Identity,
                                     bias=W(bias)).then_inc(s["L1 biased"], 1)
            act.wait_ge(s["values turned"], 1)
            nc.scalar.activation(vt[:].rearrange("p a b -> p (a b)"), ps[:, 6:8, :].rearrange("p a b -> p (a b)"),
                                 ACT.Copy).then_inc(s["values by token"], 1)
            for b in range(B):
                act.wait_ge(s["L1 scores T"], b + 1)
                if b >= 2:
                    act.wait_ge(s["L1 pv"], b - 1)
                nc.scalar.activation(prob[:, b % 2, 0:HALF], ps[:, b % 4, :], ACT.Exp).then_inc(s["L1 exp"], 1)
            if upto == 1:
                return
            norm_scalar(act, 1)
            act.wait_ge(s["L2 proj"], 5)
            nc.scalar.activation(oat[:], banks(0, 2), ACT.Copy).then_inc(s["L2 values"], 1)
            act.wait_ge(s["L2 rotated"], 2)
            for gh in range(8, G * HEADS):
                ins = nc.scalar.activation(kz[:, gh, :, :].rearrange("p j t -> p (j t)"), qk[:, 1, :], ACT.Copy,
                                           scale=W("head_mask")[:, gh:gh + 1])
            ins.then_inc(s["L2 keys scalar"], 1)
            act.preload_act_table(ACT.Exp)
            for b in range(B):
                if b >= 2:
                    act.wait_ge(s["L2 pv"], b - 1)
                act.wait_ge(s["L2 scores T"], 2 * b + 1)
                nc.scalar.activation(prob[:, b % 2, 0:2 * HALF], banks(0, 2), ACT.Exp, scale=HD ** -0.5).then_inc(s["L2 exp"], 1)
                act.wait_ge(s["L2 scores T"], 2 * b + 2)
                nc.scalar.activation(prob[:, b % 2, 2 * HALF:3 * HALF], ps[:, 2, :], ACT.Exp, scale=HD ** -0.5)\
                    .then_inc(s["L2 exp"], 1)
            if upto == 2:
                return
            norm_scalar(act, 2)
            act.wait_ge(s["F variance"], 1)
            nc.scalar.activation(fst[:, 3:4], fst[:, 3:4], ACT.Sqrt, bias=W("eps")).then_inc(s["F sigma"], 1)
            act.preload_act_table(ACT.Sigmoid)
            recur_scalar(act, 1, ACT.Sigmoid, st)
            if upto == 3:
                return
            norm_scalar(act, 3)
            rows = 2 * G * HEADS
            act.wait_ge(s["M dt steps"], 1)
            nc.scalar.activation(drow[0:rows, 1, :], drow[0:rows, 1, :], ACT.Exp).then_inc(s["M dt exp"], 1)
            nc.scalar.activation(fst[0:rows, 4:5], W("M_A_log", rows), ACT.Exp).then_inc(s["M dt exp"], 1)
            act.wait_ge(s["M dt exp"], 1)
            nc.scalar.activation(drow[0:rows, 1, :], drow[0:rows, 1, :], ACT.Ln, bias=W("one", rows)).then_inc(s["M dt log"], 1)
            act.wait_ge(s["M dt turned"], 1)
            nc.scalar.activation(dtt.rearrange("p a b -> p (a b)"), ps[:, 6, 0:J * TT * rows], ACT.Copy).then_inc(s["M dt by token"], 1)
            for d in range(2):
                name = ("fwd", "bwd")[d]
                for q in range(8):
                    act.wait_ge(s["M x"], 8 * d + q + 1)
                    c0 = slice(4 * q, 4 * q + 4)
                    xq = xt.rearrange("p a g e -> p (a g) e")[:, c0, :]
                    nc.scalar.activation(zt.rearrange("p a g e -> p (a g) e")[:, c0, :],
                                         ps[:, q, :].rearrange("p (a c) -> p a c", c=2 * E2)[:, :, E2:2 * E2], ACT.Silu)\
                        .then_inc(s["M z"], 1)
                    nc.scalar.activation(xq, xq, ACT.Silu).then_inc(s["M x silu"], 1)
                act.wait_ge(s["M bc"], 2 * d + 1)
                nc.scalar.activation(bp, banks(0, 2), ACT.Silu, bias=W(name + "_bB")).then_inc(s["M B"], 1)
                act.wait_ge(s["M bc"], 2 * d + 2)
                nc.scalar.activation(cp, banks(2, 4), ACT.Silu, bias=W(name + "_bC")).then_inc(s["M C"], 1)
                act.preload_act_table(ACT.Exp)
                for n in range(3 * B):
                    count = 3 * B * d + n
                    act.wait_ge(s["M exponent"], count + 1)
                    if count >= 2:
                        act.wait_ge(s["M gram"], count - 1)
                    nc.scalar.activation(decay[:, n % 2, :], ps[:, n % 4, :], ACT.Exp).then_inc(s["M decay"], 1)
                act.wait_ge(s["M square sums"], d + 1)
                nc.scalar.activation(mst[:, 0, :], mst[:, 0, :], ACT.Sqrt, bias=W("eps"), scale=1.0 / E2).then_inc(s["M sigma"], 1)
                act.wait_ge(s["M rows turned"], d + 1)
                nc.scalar.activation(yf[:, d, :, :].rearrange("p a b -> p (a b)"), banks(0, 4), ACT.Copy).then_inc(s["M turned"], 1)
            if upto == 4:
                return
            norm_scalar(act, 4)

            def attention(i, op, n):
                for m, dst in enumerate((rq[:, 0, :], rq[:, 1, :], oat[:])):
                    act.wait_ge(s["R proj"], n * 3 + (m + 1))
                    nc.scalar.activation(dst, banks(2 * m, 2 * m + 2), ACT.Copy).then_inc(s["R copied"], 1)
                act.wait_ge(s["R values turned"], n + 1)
                nc.scalar.activation(vt[:].rearrange("p a b -> p (a b)"), banks(6, 8), ACT.Copy).then_inc(s["R values by token"], 1)
                for b in range(B):
                    act.wait_ge(s["R scores T"], n * B + (b + 1))
                    if b >= 2:
                        act.wait_ge(s["R pv"], n * B + (b - 1))
                    nc.scalar.activation(prob[:, b % 2, 0:HALF], ps[:, b % 4, :], ACT.Exp, scale=C ** -0.5).then_inc(s["R exp"], 1)

            def feed_forward(i, op, n):
                act.wait_ge(s["R ffn weights"], n * 112 + 112)
                for k in range(0, 2 * G, 2):
                    act.wait_ge(s["R hidden"], n * 8 + (k + 1))
                    nc.scalar.activation(hidden[:, k, :], ps[:, k % 4, :], ACT.Relu, bias=b1s).then_inc(s["R relu scalar"], 1)

            routed("scalar", act, attention, feed_forward, lambda n: None)

        @block.vector
        def _(dve):
            link = Chain(dve, s["vector step"])
            dve.wait_ge(s["x loaded"], 16)
            nc.vector.memset(mbx[:].rearrange("p a b c -> p (a b c)"), 0.0).then_inc(s["X ready"], 1)
            dve.wait_ge(s["weights loaded"], 16)
            nc.vector.tensor_scalar(d_wout[:], W("L0_W_outT", E2), W("L0_D", E2), None, ALU.mult).then_inc(s["L0 d_wout"], 1)
            dve.wait_ge(s["L0 folds"], 1)
            nc.vector.tensor_tensor(z_b[:], W("L0_b_in", E2), ps[0:E2, 5, 0:1], ALU.add).then_inc(s["L0 d_wout"], 1)
            dve.wait_ge(s["L0 d_wout"], 2)
            nc.vector.scalar_tensor_tensor(u_w[:], ps[:, 4, 0:P], W("L0_gamma"), W("block"), ALU.mult, ALU.mult)
            nc.vector.tensor_tensor(g1[:], W("block"), ps[:, 4, P:2 * P], ALU.mult).then_inc(s["L0 z bias"], 1)
            dve.wait_ge(s["L0 folds"], 2)
            nc.vector.scalar_tensor_tensor(g2[:], ps[:, 4, 2 * P:3 * P], W("L0_gamma"), W("block"), ALU.mult, ALU.mult)
            nc.vector.tensor_copy(u_brow[:], ps[0:1, 5, P:2 * P])
            nc.vector.tensor_tensor(o_b[:], W("L0_b_out"), ps[:, 5, 1:2], ALU.add).then_inc(s["L0 weights"], 1)
            dve.wait_ge(s["lora products"], 1)
            nc.vector.tensor_copy(lora[:].rearrange("p a b -> p (a b)"), ps[:, 6, 0:3 * P])
            norm_vector(dve, 0)
            nc.vector.tensor_copy(mv[:, 0, :], X[:, 0:2]).then_inc(s["start state"], 1)
            for h in range(2):
                dve.wait_ge(s["L0 out"], h + 1)
                link(nc.vector.scalar_tensor_tensor(halves(X)[h], ps[:, 2 + h, :], o_b[:], halves(X)[h], ALU.add, ALU.add))
            for j in range(J):
                ins = nc.vector.bn_stats(bn6[:, j, :], Xj[:, j, :])
            link(ins)
            for j in range(J):
                ins = nc.vector.bn_aggr(mv[:, j, :], bn6[:, j, :])
            ins.then_inc(s["gn stats"], 1)
            dve.wait_ge(s["gn sigma"], 1)
            link(nc.vector.reciprocal(rstd[:], rstd[:]))
            for j in range(J):
                ins = nc.vector.tensor_scalar(xn[:, j * T:(j + 1) * T], Xj[:, j, :], mv[:, j, 0:1], rstd[:, j:j + 1],
                                              ALU.subtract, ALU.mult)
            ins.then_inc(s["gn done"], 1)
            for i, (bias, a) in enumerate((("L1_b1", "L1_a1"), ("L1_b2", "L1_a2"), ("L1_ba", "L1_aa"))):
                dve.wait_ge(s["L1 biased"], i + 1)
                link(nc.vector.tensor_scalar(pm[:, i, :], pr[:, i, :], 0.0, W(a), ALU.min, ALU.mult))
                nc.vector.scalar_tensor_tensor(pm[:, i, :], pr[:, i, :], 0.0, pm[:, i, :], ALU.max, ALU.add)\
                    .then_inc(s["L1 prelu"], 1)
            dve.wait_ge(s["L1 prelu"], 3)
            for g in range(G):
                ins = nc.vector.tensor_scalar(e2z[:, g, :, :].rearrange("p j t -> p (j t)"), pm[:, 1, :],
                                              W("group_mask")[:, g:g + 1], None, ALU.mult)
            ins.then_inc(s["L1 keys"], 1)
            for b in range(B):
                j, g = b // G, b % G
                dve.wait_ge(s["L1 scores"], b + 1)
                nc.vector.reduce_max(mbx[:, j, :, C * g + NS], ps[:, b % 4, :].rearrange("p (q k) -> p q k", q=TT), AX)\
                    .then_inc(s["L1 max"], 1)
            dve.wait_ge(s["L1 max rows"], 1)
            nc.vector.tensor_tensor(e1m[:], pm[:, 0, :], ps[:, 4:6, :].rearrange("p a b -> p (a b)"), ALU.add)\
                .then_inc(s["L1 queries"], 1)
            dve.wait_ge(s["L1 pv"], B)
            link(nc.vector.reciprocal(den[:], ps[:, 6:8, :].rearrange("p a b -> p (a b)")))
            link(nc.vector.tensor_tensor(oat[:], den[:], ps[:, 4:6, :].rearrange("p a b -> p (a b)"), ALU.mult))
            nc.vector.tensor_tensor(X[:], X[:], oat[:], ALU.add).then_inc(s["X ready"], 1)
            if upto == 1:
                dve.wait_ge(s["X ready"], 2)
                nc.vector.memset(bn6[:, 0, 0:1], 0.0).then_inc(s["stage done"], 1)
                return

            for i, w in enumerate("qkv"):
                link(nc.vector.scalar_tensor_tensor(wqkv[:, i, :], lora[:, i, :], 2.0,
                                                    W("block"), ALU.mult, ALU.mult))
                link(nc.vector.tensor_tensor(wqkv[:, i, :], wqkv[:, i, :], W(f"L2_w{w}T"), ALU.add))
            for i in range(2):
                even = wqkv[:, i, :].rearrange("p (d two) -> p two d", two=2)
                turned = wrot[:, i, :].rearrange("p (d two) -> p two d", two=2)
                nc.vector.tensor_scalar(turned[:, 0, :], even[:, 1, :], -1.0, None, ALU.mult)
                ins = nc.vector.tensor_copy(turned[:, 1, :], even[:, 0, :])
            ins.then_inc(s["L2 weights"], 1)
            norm_vector(dve, 1)
            nc.vector.memset(vz, 0.0).then_inc(s["vector step"], 1)
            link.n += 1
            for i in range(2):
                dve.wait_ge(s["L2 proj"], 2 * i + 2)
                angle = [W(t).unsqueeze(1).to_broadcast([P, J, T]) for t in ("cos", "sin")]
                bank = [ps[:, 4 * i + 2 * r:4 * i + 2 * r + 2, :].rearrange("p a (j t) -> p (a j) t", t=T) for r in range(2)]
                nc.vector.tensor_tensor(qk[:, i, :].rearrange("p (j t) -> p j t", j=J), angle[0], bank[0], ALU.mult)
                link(nc.vector.tensor_tensor(qrs.rearrange("p (j t) -> p j t", j=J), angle[1], bank[1], ALU.mult))
                ins = nc.vector.tensor_tensor(qk[:, i, :], qk[:, i, :], qrs, ALU.add)
                ins.then_inc(s["L2 rotated"], 1)
                dve.wait_ge(s["L2 rotated"], i + 1)
            for gh in range(8):
                ins = nc.vector.tensor_scalar(kz[:, gh, :, :].rearrange("p j t -> p (j t)"), qk[:, 1, :],
                                              W("head_mask")[:, gh:gh + 1], None, ALU.mult)
            dve.wait_ge(s["values turned"], 2)
            for h in range(HEADS):
                ins = nc.vector.tensor_copy(vz[:, h, :, HD * h:HD * (h + 1)],
                                            banks(2, 4).rearrange("p (r c) -> p r c", c=C)[:, :, HD * h:HD * (h + 1)])
            ins.then_inc(s["L2 values split"], 1)
            mbv = mb.rearrange("p (j q g h) -> p j q g h", j=J, q=TT, g=G)
            for b in range(B):
                j, g = b // G, b % G
                k0 = 3 * (b % 2)
                dve.wait_ge(s["L2 scores"], b + 1)
                nc.vector.reduce_max(mbv[:, j, 0, g, :], ps[:, k0, :].rearrange("p (h k) -> p h k", h=HEADS), AX)\
                    .then_inc(s["L2 max"], 1)
                nc.vector.reduce_max(mbv[:, j, 1, g, :], banks(k0 + 1, k0 + 3).rearrange("p (h k) -> p h k", h=HEADS), AX)\
                    .then_inc(s["L2 max"], 1)
            dve.wait_ge(s["L2 max rows"], 1)
            nc.vector.tensor_copy(nm[:, 0, :], ps[:, 6, 0:P]).then_inc(s["L2 max parts"], 1)
            dve.wait_ge(s["L2 max parts"], 1)
            nc.vector.tensor_tensor(nm[:, 1, :], ps[:, 6, 0:P], nm[:, 0, :], ALU.subtract).then_inc(s["L2 max parts"], 1)
            dve.wait_ge(s["L2 pv"], B)
            link(nc.vector.reciprocal(den[:], banks(6, 8)))
            nc.vector.tensor_tensor(oat[:], den[:], banks(4, 6), ALU.mult).then_inc(s["L2 attended"], 1)
            for h in range(2):
                dve.wait_ge(s["L2 out"], h + 1)
                ins = nc.vector.tensor_tensor(halves(X)[h], halves(X)[h], ps[:, h, :], ALU.add)
            ins.then_inc(s["X ready"], 1)
            if upto == 2:
                dve.wait_ge(s["X ready"], 3)
                nc.vector.memset(bn6[:, 0, 0:1], 0.0).then_inc(s["stage done"], 1)
                return

            norm_vector(dve, 2)
            for h in range(2):
                dve.wait_ge(s["F proj"], h + 1)
                ins = nc.vector.bn_stats(bn6[:, h, :], ps[:, 4 + h, :])
            link(ins)
            link(nc.vector.bn_aggr(fst[:, 0:2], bn6[:, 0:2, :].rearrange("p a b -> p (a b)")))
            nc.vector.scalar_tensor_tensor(fst[:, 1:2], fst[:, 0:1], fst[:, 0:1], fst[:, 1:2], ALU.mult, ALU.add)\
                .then_inc(s["F row stats"], 1)
            dve.wait_ge(s["F stats"], 1)
            link(nc.vector.tensor_copy(fst[:, 2:4], ps[:, 6, 0:2]))
            link(nc.vector.tensor_tensor(fst[:, 4:5], fst[:, 2:3], fst[:, 2:3], ALU.mult))
            nc.vector.tensor_tensor(fst[:, 3:4], fst[:, 3:4], fst[:, 4:5], ALU.subtract).then_inc(s["F variance"], 1)
            dve.wait_ge(s["F sigma"], 1)
            link(nc.vector.reciprocal(fst[:, 3:4], fst[:, 3:4]))
            link(nc.vector.tensor_tensor(fst[:, 5:6], fst[:, 3:4], W("F_gamma"), ALU.mult))
            link(nc.vector.tensor_tensor(fst[:, 6:7], fst[:, 2:3], fst[:, 5:6], ALU.mult))
            link(nc.vector.tensor_tensor(fst[:, 6:7], W("F_beta"), fst[:, 6:7], ALU.subtract))
            nc.vector.tensor_scalar(xn[:], banks(4, 6), fst[:, 5:6], fst[:, 6:7], ALU.mult, ALU.add).then_inc(s["F input"], 1)
            nc.vector.memset(wbc.rearrange("p a b c -> p (a b c)"), 0.0)
            nc.vector.memset(xs[:, :, :, 0:K - 1], 0.0)
            link(nc.vector.memset(xs[:, :, :, T:T + K - 1], 0.0))
            for d, name in enumerate(("fwd", "bwd")):
                nc.vector.tensor_tensor(wxz[:, d, 0:E2], W(name + "_proj")[:, 0:E2], W(name + "_taps")[:, 0:E2], ALU.mult)
                nc.vector.tensor_copy(wxz[:, d, E2:2 * E2], W(name + "_z"))
                nc.vector.tensor_tensor(wbc[:, d, :, 0:NS], W(name + "_proj")[:, E2:].rearrange("p (a b) -> p a b", a=2),
                                        W(name + "_taps")[:, E2:].rearrange("p (a b) -> p a b", a=2), ALU.mult)
                ins = nc.vector.tensor_scalar(wout[:, d, :], W(name + "_out"), W(name + "_norm"), None, ALU.mult)
            ins.then_inc(s["M weights"], 1)
            dve.wait_ge(s["state"], 2 * T + 1)
            nc.vector.tensor_tensor(Xj, Xj, st[:, :, 1:T + 1], ALU.add).then_inc(s["X ready"], 1)
            if upto == 3:
                dve.wait_ge(s["X ready"], 4)
                nc.vector.memset(bn6[:, 0, 0:1], 0.0).then_inc(s["stage done"], 1)
                return
            norm_vector(dve, 3)
            rows = 2 * G * HEADS
            dve.wait_ge(s["M dt proj"], 1)
            link(nc.vector.tensor_scalar(drow[0:rows, 0, :], ps[0:rows, 4:6, :].rearrange("p a b -> p (a b)"),
                                         W("M_dt_bias", rows), None, ALU.add))
            nc.vector.scalar_tensor_tensor(drow[0:rows, 1, :], drow[0:rows, 0, :], -1.0, drow[0:rows, 0, :], ALU.mult, ALU.min)\
                .then_inc(s["M dt steps"], 1)
            dve.wait_ge(s["M dt log"], 1)
            nc.vector.scalar_tensor_tensor(drow[0:rows, 3, :], drow[0:rows, 0, :], 0.0, drow[0:rows, 1, :], ALU.max, ALU.add)\
                .then_inc(s["M dt"], 1)
            dve.wait_ge(s["M dt"], 1)
            dve.wait_ge(s["M dt exp"], 2)
            nc.vector.memset(cs[0:rows, :, 0:1], 0.0)
            nc.vector.memset(drow[0:rows, 1, 0:T], 1.0)
            link(nc.vector.tensor_scalar(drow[0:rows, 2, :], drow[0:rows, 3, :], fst[0:rows, 4:5], -1.0, ALU.mult, ALU.mult))
            for j in range(J):
                ins = nc.vector.tensor_tensor_scan(cs[0:rows, j, 1:T + 1], drow[0:rows, 1, 0:T], drow[0:rows, 2, j * T:(j + 1) * T],
                                                   0.0, ALU.mult, ALU.add)
            link(ins)
            for part in range(3):
                link(nc.vector.tensor_copy(c3[32 * part:32 * part + 32, :, :], cs[0:rows, :, :]))
                if part < 2:
                    link(nc.vector.tensor_tensor(cs[0:rows, :, :], cs[0:rows, :, :], c3[32 * part:32 * part + 32, :, :], ALU.subtract))
            for h in range(HEADS):
                ins = nc.vector.tensor_scalar(c3x[:, h, :], c3[:].rearrange("p j t -> p (j t)"), W("row_head", 96)[:, h:h + 1], None, ALU.mult)
            ins.then_inc(s["M decay parts"], 1)
            bx = lambda t: t.rearrange("p a g e -> p (a g) e")
            for d, name in enumerate(("fwd", "bwd")):
                for q in range(8):
                    dve.wait_ge(s["M xz"], 8 * d + q + 1)
                    nc.vector.tensor_tensor(bx(xt)[:, 4 * q:4 * q + 4, :], W(name + "_bx").unsqueeze(1).to_broadcast([P, 4, E2]),
                                            ps[:, q, :].rearrange("p (a c) -> p a c", c=2 * E2)[:, :, 0:E2], ALU.add)\
                        .then_inc(s["M x"], 1)
                dve.wait_ge(s["M x silu"], 8 * (d + 1))
                dve.wait_ge(s["M dt by token"], 1)
                gh = G * HEADS
                nc.vector.tensor_tensor(xdt.rearrange("p a g (h e) -> p a (g h) e", h=HEADS),
                                        xt.rearrange("p a g (h e) -> p a (g h) e", h=HEADS),
                                        dtt[:, :, d * gh:(d + 1) * gh].unsqueeze(3).to_broadcast([P, J * TT, gh, PH]), ALU.mult)\
                    .then_inc(s["M xdt"], 1)
                dve.wait_ge(s["M B"], d + 1)
                for g in range(G):
                    ins = nc.vector.tensor_scalar(bz[:, g, :, :].rearrange("p j t -> p (j t)"), bp, W("group_mask")[:, g:g + 1],
                                                  None, ALU.mult)
                ins.then_inc(s["M B split"], 1)
                link(nc.vector.tensor_tensor(bx(xt), bx(xt), W(name + "_D").unsqueeze(1).to_broadcast([P, 32, E2]), ALU.mult))
                for n in range(3 * B):
                    b, count = n // 3, 3 * B * d + n
                    dve.wait_ge(s["M CB"], B * d + b + 1)
                    dve.wait_ge(s["M decay"], count + 1)
                    if count >= 2:
                        dve.wait_ge(s["M products"], count - 1)
                    nc.vector.tensor_tensor(gram[:, n % 2, :].rearrange("p (h t) -> p h t", h=HEADS),
                                            decay[:, n % 2, :].rearrange("p (h t) -> p h t", h=HEADS),
                                            ps[:, 4 + b % 2, (n % 3) * P:(n % 3 + 1) * P].unsqueeze(1).to_broadcast([P, HEADS, P]),
                                            ALU.mult).then_inc(s["M gram"], 1)
                    if n % 12 == 2 and n > 12:
                        dve_y(dve, d, n // 12 - 1)
                dve_y(dve, d, 3)
                dve.wait_ge(s["M y"], 4 * (d + 1))
                link(nc.vector.tensor_tensor(bx(yt), bx(yt), bx(xt), ALU.add))
                nc.vector.tensor_tensor(bx(yt), bx(yt), bx(zt), ALU.mult).then_inc(s["M gate"], 1)
                dve.wait_ge(s["M gate"], d + 1)
                link(nc.vector.tensor_tensor(bx(ysq), bx(yt), bx(yt), ALU.mult))
                nc.vector.tensor_reduce(mst[:, 0, :], bx(ysq), AX, ALU.add).then_inc(s["M square sums"], 1)
                dve.wait_ge(s["M sigma"], d + 1)
                link(nc.vector.reciprocal(mst[:, 1, :], mst[:, 0, :]))
                nc.vector.tensor_tensor(bx(yt), bx(yt), mst[:, 1, :].unsqueeze(2).to_broadcast([P, 32, E2]), ALU.mult)\
                    .then_inc(s["M normed"], 1)
            dve.wait_ge(s["M out"], 1)
            nc.vector.tensor_tensor(X[:], X[:], banks(4, 6), ALU.add).then_inc(s["X ready"], 1)
            if upto == 4:
                dve.wait_ge(s["X ready"], 5)
                nc.vector.memset(bn6[:, 0, 0:1], 0.0).then_inc(s["stage done"], 1)
                return

            norm_vector(dve, 4)
            dve.wait_ge(s["masks loaded"], 32)
            nc.vector.memset(w1z, 0.0)
            nc.vector.memset(wbd, 0.0).then_inc(s["R cleared"], 1)
            link(nc.vector.tensor_tensor(either, masks[:, 0, :], masks[:, 1, :], ALU.max))
            dve.wait_ge(s["normalised"], 10)
            picks = s["first of tokens"]

            def pick(n):
                nc.vector.transpose(h0[:], xn[0:C, 0:C]).then_inc(picks, 1)
                dve.wait_ge(picks, n * 3 + 1)
                dve.sem_inc(s["vector pick step"], 1)
                nc.vector.max(best[:], h0[0:1, 0:NOPS]).then_inc(picks, 1)
                dve.wait_ge(picks, n * 3 + 2)
                dve.sem_inc(s["vector pick step"], 1)
                nc.vector.max_index(op_at[:], best[:], h0[0:1, 0:NOPS]).then_inc(picks, 1)
                dve.wait_ge(picks, n * 3 + 3)
                nc.vector.memset(h0[0:1, 0:1], 0.0).then_inc(s["op picked"], 1)

            def attention(i, op, n):
                dve.wait_ge(s["R copied"], n * 3 + 2)
                for g in range(G):
                    ins = nc.vector.tensor_scalar(rkz[:, g, :, :].rearrange("p j t -> p (j t)"), rq[:, 1, :],
                                                  W("group_mask")[:, g:g + 1], None, ALU.mult)
                ins.then_inc(s["R keys"], 1)
                for b in range(B):
                    j, g = b // G, b % G
                    dve.wait_ge(s["R scores"], n * B + (b + 1))
                    nc.vector.reduce_max(rmb.rearrange("p (j q g) -> p j q g", j=J, q=TT)[:, j, :, g],
                                         ps[:, b % 4, :].rearrange("p (q k) -> p q k", q=TT), AX).then_inc(s["R max"], 1)
                dve.wait_ge(s["R max rows"], n + 1)
                rows = J * TT * G
                nc.vector.tensor_copy(rnm[:, 0, :], ps[0:rows, 4, 0:P]).then_inc(s["R max parts"], 1)
                dve.wait_ge(s["R max parts"], n * 2 + 1)
                nc.vector.tensor_tensor(rnm[:, 1, :], ps[0:rows, 4, 0:P], rnm[:, 0, :], ALU.subtract).then_inc(s["R max parts"], 1)
                dve.wait_ge(s["R pv"], n * B + B)
                nc.vector.reciprocal(den[:], banks(6, 8)).then_inc(s["R reciprocal"], 1)
                dve.wait_ge(s["R reciprocal"], n + 1)
                nc.vector.tensor_tensor(oat[:], den[:], banks(4, 6), ALU.mult).then_inc(s["R attended"], 1)
                dve.wait_ge(s["R attention out"], n + 1)
                nc.vector.tensor_copy(xn[:], banks(0, 2)).then_inc(s["R attention written"], 1)
                dve.wait_ge(s["R attention written"], n + 1)

            def feed_forward(i, op, n):
                dve.wait_ge(s["R ffn weights"], n * 112 + 112)
                for k in range(1, 2 * G, 2):
                    dve.wait_ge(s["R hidden"], n * 8 + (k + 1))
                    nc.vector.tensor_scalar(hidden[:, k, :], ps[:, k % 4, :], b1s, 0.0, ALU.add, ALU.max)\
                        .then_inc(s["R relu vector"], 1)
                for h in range(2):
                    dve.wait_ge(s["R ffn out"], n * 8 + 4 * (h + 1))
                    ins = nc.vector.tensor_scalar(halves(xn)[h], ps[:, 4 + h, :], b2s, None, ALU.add)
                ins.then_inc(s["R ffn written"], 1)
                dve.wait_ge(s["R ffn written"], n + 1)

            pick(0)
            routed("vector", dve, attention, feed_forward, pick)
            nc.vector.tensor_tensor(X[:], X[:], xn[:], ALU.add).then_inc(s["X ready"], 1)


def _grouped(w):
    out = np.zeros((P, P), np.float32)
    for g in range(G):
        out[C * g:C * g + w.shape[0], C * g:C * g + w.shape[1]] = w
    return out


def _slots(v):
    out = np.zeros(v.shape[:-1] + (G, C), np.float32)
    out[..., :, :v.shape[-1]] = v[..., None, :]
    return out.reshape(v.shape[:-1] + (P,))


def _pack(a):
    w = np.zeros((P, NW), np.float32)

    def put(name, v):
        at, width = COL[name]
        v = np.asarray(v, np.float32)
        if v.ndim == 1:
            v = v[:, None]
        assert v.shape[1] == width, (name, v.shape)
        w[:v.shape[0], at:at + width] = v

    eye = np.eye(P, dtype=np.float32)
    put("ident", eye)
    put("neg_ident", -eye)
    put("block", _grouped(np.ones((C, C))))
    put("avg_c", _grouped(np.full((C, C), 1.0 / C)))
    put("avg_g", np.tile(np.eye(C), (G, G)) / G)
    put("eps", np.full(P, EPS))
    put("one", np.ones(P))
    put("ones_row", np.ones((1, HALF)))
    put("ones32", np.ones((P, C)))
    put("group_mask", np.repeat(np.eye(G), C, axis=0))
    put("head_mask", np.repeat(np.eye(G * HEADS), HD, axis=0))
    put("head_ones", np.tile(np.repeat(np.eye(HEADS), HD, axis=1).reshape(1, -1), (P, 1)))
    put("L0_W_in", np.tile(a["L0_conv_W_in"], (1, G)))
    put("L0_BmT", _slots(a["L0_conv_Bm"].T))
    put("L0_AT", _grouped(a["L0_conv_A"].T))
    put("L0_Cm", _slots(a["L0_conv_Cm"]))
    put("L0_W_outT", np.tile(a["L0_conv_W_out"].T, (1, G)))
    put("L0_D", a["L0_conv_D"])
    put("L0_b_in", a["L0_conv_b_in"])
    put("L0_W_inT", a["L0_conv_W_in"].T)
    put("L0_beta", a["L0_conv_beta"])
    put("L0_gamma", np.tile(a["L0_conv_gamma"], G))
    put("L0_b_out", np.tile(a["L0_conv_b_out"], G))
    for n in ("w1", "w2", "wa"):
        put(f"L1_{n}T", _grouped(a[f"L1_conv_{n}"].T))
    put("L1_b1", _slots(a["L1_conv_b1"]))
    put("L1_b2", _slots(np.concatenate([a["L1_conv_b2"], np.ones(1, np.float32)])))
    put("L1_ba", _slots(a["L1_conv_ba"]))
    for n in ("a1", "a2", "aa"):
        put("L1_" + n, np.broadcast_to(a["L1_conv_" + n], (P,)))
    for n in "qkvo":
        put(f"L2_w{n}T", _grouped(a["L2_attn_w" + n].T))
    for n in "qkv":
        put(f"L2_A_{n}", np.tile(a["L2_attn_lora_A_" + n], (1, G)))
        put(f"L2_B_{n}T", np.tile(a["L2_attn_lora_B_" + n].T, (1, G)))
    freq = (1.0 / np.float32(10000.0) ** (np.arange(0, HD, 2, dtype=np.float32) / HD)).astype(np.float32)
    angle = np.arange(T, dtype=np.float32)[:, None] * freq[None, :]
    put("cos", np.tile(np.repeat(np.cos(angle), 2, axis=1).T, (P // HD, 1)))
    put("sin", np.tile(np.repeat(np.sin(angle), 2, axis=1).T, (P // HD, 1)))
    put("F_WT", _grouped(a["L2_ffn_W"].T))
    put("F_VT", _grouped(a["L2_ffn_V"].T))
    put("F_gamma", np.tile(a["L2_ffn_gamma"], G))
    put("F_beta", np.tile(a["L2_ffn_beta"], G))
    dtw, dtb, alog = np.zeros((P, 2, G, HEADS), np.float32), np.zeros((2, G, HEADS), np.float32), np.zeros((2, G, HEADS), np.float32)
    for d, name in enumerate(("fwd", "bwd")):
        m = {k: a[f"L3_attn_{name}_{k}"] for k in ("in_proj", "conv_w", "conv_b", "A_log", "dt_bias", "D", "norm_w", "out_proj")}
        taps = m["conv_w"].T if d == 0 else m["conv_w"].T[::-1]
        put(name + "_proj", np.tile(m["in_proj"][:, E2:2 * E2 + 2 * NS], (K, 1)))
        put(name + "_taps", np.repeat(taps, C, axis=0))
        z = np.zeros((K, C, E2), np.float32)
        z[K - 1 if d == 0 else 0] = m["in_proj"][:, :E2]
        put(name + "_z", z.reshape(P, E2))
        put(name + "_bx", np.tile(m["conv_b"][None, :E2], (P, 1)))
        put(name + "_bB", _slots(m["conv_b"][E2:E2 + NS]))
        put(name + "_bC", _slots(m["conv_b"][E2 + NS:]))
        put(name + "_D", np.tile(np.repeat(m["D"], PH)[None], (P, 1)))
        put(name + "_norm", np.tile(m["norm_w"], 2))
        o = np.zeros((2, E2, 2, C), np.float32)
        o[0, :, 0] = o[1, :, 1] = m["out_proj"]
        put(name + "_out", o.reshape(P, 2 * C))
        for g in range(G):
            dtw[C * g:C * g + C, d, g] = m["in_proj"][:, 2 * E2 + 2 * NS:]
        dtb[d], alog[d] = m["dt_bias"], m["A_log"]
    put("M_dtW", dtw.reshape(P, -1))
    put("M_dt_bias", dtb.reshape(-1))
    put("M_A_log", alog.reshape(-1))
    put("row_head", np.tile(np.eye(HEADS), (P // HEADS, 1)))
    return w


def _pack_consts(dtype):
    c = np.zeros((P, NC), np.float32)

    def put(name, v):
        at, width = CCOL[name]
        c[:v.shape[0], at:at + width] = v

    r = np.arange(P)
    put("identb", np.eye(P))
    put("mask_above", np.where(r[None, :] > r[:, None], MASKED, 0))
    put("mask_below", np.where(r[None, :] < r[:, None], MASKED, 0))
    rows = np.zeros((2, G, HEADS, 2, G, P), np.float32)
    cols = np.zeros((2 * G * HEADS, 2 * G * HEADS), np.float32)
    for d in range(2):
        for g in range(G):
            rows[d, g, :, d, g, :] = 1 - 2 * d
    np.fill_diagonal(cols, np.repeat([-1.0, 1.0], G * HEADS))
    put("sel_rows", np.tile(rows.reshape(32, -1), (3, 1)))
    put("sel_cols", np.tile(cols, (3, 1)))
    return c.astype(dtype)


def _words(mask):
    padded = np.zeros(mask.shape + (4,), np.uint8)
    padded[..., 0] = mask.view(np.uint8)
    return padded.view(np.int32)[..., 0]


def kernel(**inputs):
    import concourse.bacc as bacc
    from concourse.bass_utils import run_bass_kernel_spmd

    a = {k: np.asarray(v) for k, v in inputs.items()}
    nc = bacc.Bacc("TRN2", target_bir_lowering=False, num_devices=1)
    arrays = {
        "x": np.ascontiguousarray(a["x"]),
        "weights": _pack(a),
        "consts": _pack_consts(mybir.dt.np(BF16)),
        "w1": a["L3_ffn_ffn_w1"], "b1": a["L3_ffn_ffn_b1"], "w2": a["L3_ffn_ffn_w2"], "b2": a["L3_ffn_ffn_b2"],
        "wq": a["L3_ffn_wq"], "wk": a["L3_ffn_wk"], "wv": a["L3_ffn_wv"], "wo": a["L3_ffn_wo"],
        "attn_mask": _words(a["L3_ffn_attn_mask"]), "ffn_mask": _words(a["L3_ffn_ffn_mask"]),
    }
    arrays = {k: np.ascontiguousarray(v) for k, v in arrays.items()}
    args = {k: nc.dram_tensor(k, v.shape, mybir.dt.from_np(v.dtype), kind="ExternalInput").ap() for k, v in arrays.items()}
    args["out"] = nc.dram_tensor("out", (B, C, 16, 16), F32, kind="ExternalOutput").ap()
    hybrid_block(nc, **args)
    return run_bass_kernel_spmd(nc, [arrays], core_ids=[0]).results[0]["out"]
```

```python
from contextlib import ExitStack

import numpy as np

import concourse.bass as bass
from concourse import mybir

ALU = mybir.AluOpType
ACT = mybir.ActivationFunctionType
F32 = mybir.dt.float32
BF16 = mybir.dt.bfloat16
U32 = mybir.dt.uint32
I32 = mybir.dt.int32
AX = mybir.AxisListType.X

P = 128
B, C, T = 16, 32, 256
G = P // C
J = B // G
N = J * T
HALF = N // 2
TT = T // P
HEADS = 4
HD = C // HEADS
E2 = 2 * C
NS = 16
PH = E2 // HEADS
K = 4
NB, NOPS, HID = 33, 19, 128
ARENA = 29696
BANKS = 8
STEP_BANK = HALF // B
assert BANKS * STEP_BANK == T
STEPS = 6
assert STEPS * STEPS >= NB
EPS = 1e-5
MASKED = -1e30

ROWS = 2 * G * HEADS

WEIGHTS = [
    ("ident", P), ("avg_c", P), ("avg_by_group", G), ("block", P), ("eps", 1), ("one", 1),
    ("L0_W_in", P), ("L0_BmT", P), ("L0_AT", P), ("L0_Cm", P), ("L0_W_outT", P),
    ("L0_D", 1), ("L0_b_in", 1), ("L0_W_inT", E2), ("L0_beta", 1), ("L0_gamma", 1), ("L0_b_out", 1),
    ("L1_w1T", P), ("L1_w2T", P), ("L1_waT", P),
    ("L1_b1", 1), ("L1_b2", 1), ("L1_ba", 1), ("L1_a1", 1), ("L1_a2", 1), ("L1_aa", 1),
    ("neg_ident", P), ("ones32", C), ("group_mask", G),
    ("L2_wqT", P), ("L2_wkT", P), ("L2_wvT", P),
    ("L2_A_q", P), ("L2_A_k", P), ("L2_A_v", P), ("L2_B_qT", P), ("L2_B_kT", P), ("L2_B_vT", P),
    ("cos", T), ("sin", T), ("head_mask", G * HEADS), ("L2_wo_by_head", C),
    ("F_WT", P), ("F_VT", P), ("F_gamma", 1), ("F_beta", 1), ("avg_g", P),
    ("M_dtW", 2 * ROWS), ("M_dt_bias", 1), ("M_A_log", 1), ("M_sign", 1),
    ("key_rows", G), ("query_ones", G), ("query_rows", HEADS), ("key_minus_ones", HEADS), ("avg_e", 2 * C),
]
for _d in ("fwd", "bwd"):
    WEIGHTS += [(f"{_d}_proj", E2 + 2 * NS), (f"{_d}_taps", E2 + 2 * NS), (f"{_d}_z", 2 * P), (f"{_d}_bx", 1),
                (f"{_d}_bB", 1), (f"{_d}_bC", 1), (f"{_d}_D", 1), (f"{_d}_norm", 1), (f"{_d}_out", 2 * C)]
COL = {}
NW = 0
for _n, _w in WEIGHTS:
    COL[_n] = (NW, _w)
    NW += _w

CONSTS = [("identb", P), ("zeros", P), ("mask_above", P), ("mask_below", P), ("zeros2", P)]
CCOL = {}
NC = 0
for _n, _w in CONSTS:
    CCOL[_n] = (NC, _w)
    NC += _w


def hybrid_block(nc, x, weights, consts, w1, b1, w2, b2, wq, wk, wv, wo, attn_mask, ffn_mask, out, upto=99, dump=None):
    with ExitStack() as ctx:
        def sb(name, shape, dt=F32):
            return ctx.enter_context(nc.sbuf_tensor(name, shape, dt))

        class Signals(dict):
            def __missing__(self, what):
                self[what] = ctx.enter_context(nc.semaphore("s_" + what.replace(" ", "_")))
                return self[what]

        s = Signals()

        class Chain:
            def __init__(self, eng, sem):
                self.eng, self.sem, self.n = eng, sem, 0

            def __call__(self, ins):
                self.n += 1
                ins.then_inc(self.sem, 1)
                self.eng.wait_ge(self.sem, self.n)

        ps = ctx.enter_context(nc.psum_tensor("ps", [P, 8, HALF], F32))
        wsb = sb("wsb", [P, NW])
        csb = sb("csb", [P, NC], BF16)

        def W(name, rows=P):
            at, w = COL[name]
            return wsb[0:rows, at:at + w]

        def CB(name, rows=P):
            at, w = CCOL[name]
            return csb[0:rows, at:at + w]

        def CB_pair(first, second):
            assert CCOL[first][0] + CCOL[first][1] == CCOL[second][0]
            return csb[:, CCOL[first][0]:CCOL[second][0] + CCOL[second][1]]

        def banks(a, b):
            return ps[:, a:b, :].rearrange("p a b -> p (a b)")

        X = sb("X", [P, N])
        xc = sb("xc", [P, N])
        sq = sb("sq", [P, N])
        sigma = sb("sigma", [P, J * TT * G])
        xn = sb("xn", [P, N])
        u_w = sb("u_w", [P, P])
        g1 = sb("g1", [P, P])
        g2 = sb("g2", [P, P])
        d_wout = sb("d_wout", [E2, P])
        z_b = sb("z_b", [E2, 1])
        u_b = sb("u_b", [P, 1])
        o_b = sb("o_b", [P, 1])
        bn6 = sb("bn6", [P, J, 6])
        mv = sb("mv", [P, J, 2])
        rstd = sb("rstd", [P, J])
        prob = sb("prob", [P, 2, 3 * HALF])
        prob6 = prob[:].rearrange("p a (b c) -> p (a b) c", c=HALF)
        oat = sb("oat", [P, N])
        lora = sb("lora", [P, 3, P])
        den = sb("den", [P, N])
        vt = sb("vt", [P, J * TT, P])
        arena = sb("arena", [P, ARENA])
        states = arena[:, ARENA - B * (T + 1):].rearrange("p (g j t) -> p g j t", g=G, j=J)

        class Arena:
            def __init__(self):
                self.at = 0

            def __call__(self, *dims):
                n = int(np.prod(dims))
                v = arena[:, self.at:self.at + n]
                self.at += n
                assert self.at <= ARENA
                names = " ".join("abcd"[:len(dims)])
                if len(dims) == 1:
                    return v
                return v.rearrange(f"p ({names}) -> p {names}", **dict(zip("abcd", dims)))

        at = Arena()
        pr = at(3, N)
        pm = at(3, N)
        e2z = at(G, J, T)
        mbx = at(J, TT, P)
        e1m = at(N)
        at = Arena()
        wqkv = at(3, P)
        wrot = at(2, P)
        qk = at(2, N)
        qrs = at(N)
        kz = at(G * HEADS, J, T)
        mb = at(J * TT * G * HEADS)
        nmr = at(P)
        nm = sb("nm", [P, 2, P], BF16)
        fst = sb("fst", [P, 8])
        at = Arena()
        xs = at(J, G, T + K - 1)
        wx = at(2, E2)
        wbc = at(2, 2, C)
        wout = at(2, 2 * C)
        xf = at(J, 2 * T)
        xdt = at(J * TT, G, HEADS, 2 * PH)
        bp = at(N)
        cp = at(N)
        bz = at(G, J, T)
        drow = bz.rearrange("p a b c -> p a (b c)")
        dtt = at(J * TT, 2 * ROWS)
        zf = at(J, 2 * T)
        yg = at(J, 2 * T)
        decay = at(3, HALF)
        gram = at(3, HALF)
        cs = at(J, T + 1)
        c3 = sb("c3", [P, J, T + 1], BF16)
        by_token = sb("by_token", [P, HEADS * N], BF16)
        low = lambda t: t.bitcast(BF16).rearrange("p (a n) -> p a n", n=N)
        key_side = ((low(xc[:]), low(sq[:])), (low(den[:]), low(vt[:].rearrange("p a b -> p (a b)"))))
        prob_flat = prob[:].rearrange("p a b -> p (a b)")
        query_side = (by_token[:].rearrange("p (h n) -> p h n", h=HEADS), low(prob_flat[:, 0:2 * N]))
        projected = prob_flat[:, 2 * N:3 * N]

        xr = x.rearrange("(j g) c h w -> (g c) j (h w)", g=G)
        Xj = X[:].rearrange("p (j t) -> p j t", j=J)

        def halves(t):
            return [t[:, h * HALF:(h + 1) * HALF] for h in range(2)]

        def norm_tensor(pe, n):
            for h in range(2):
                pe.wait_ge(s["X ready"], n + 1)
                nc.tensor.matmul(ps[:, h, :], W("avg_c"), halves(X)[h], start=True, stop=True).then_inc(s["mean"], 1)
            for h in range(2):
                pe.wait_ge(s["squares"], 2 * n + h + 1)
                for jt in range(h * 4, h * 4 + 4):
                    mm = nc.tensor.matmul(ps[:, h, jt * G:(jt + 1) * G], sq[:, jt * P:(jt + 1) * P], W("avg_by_group"),
                                          start=True, stop=True)
                mm.then_inc(s["variance"], 1)
            for h in range(2):
                pe.wait_ge(s["1/sigma"], 2 * n + h + 1)
                for jt in range(h * 4, h * 4 + 4):
                    mm = nc.tensor.matmul(ps[:, 2 + h, (jt % 4) * P:(jt % 4 + 1) * P],
                                          sq[:, jt * P:(jt + 1) * P], W("ident"),
                                          start=True, stop=True)
                mm.then_inc(s["1/sigma rows"], 1)

        def norm_vector(dve, n):
            for h in range(2):
                dve.wait_ge(s["mean"], 2 * n + h + 1)
                nc.vector.tensor_tensor(halves(xc)[h], halves(X)[h], ps[:, h, :], ALU.subtract).then_inc(s["centred"], 1)
            for h in range(2):
                dve.wait_ge(s["sigma"], 2 * n + h + 1)
                cols = sigma[:, h * 4 * G:(h + 1) * 4 * G]
                nc.vector.reciprocal(cols, cols).then_inc(s["1/sigma by token"], 1)
                dve.wait_ge(s["1/sigma by token"], 2 * n + h + 1)
                nc.vector.tensor_copy(halves(sq)[h].rearrange("p (a c) -> p a c", c=C),
                                      cols.unsqueeze(2).to_broadcast([P, 4 * G, C])).then_inc(s["1/sigma"], 1)
            for h in range(2):
                dve.wait_ge(s["1/sigma rows"], 2 * n + h + 1)
                nc.vector.tensor_tensor(halves(xn)[h], halves(xc)[h], ps[:, 2 + h, :], ALU.mult).then_inc(s["normalised"], 1)

        def norm_scalar(act, n):
            act.preload_act_table(ACT.Sqrt)
            for h in range(2):
                act.wait_ge(s["centred"], 2 * n + h + 1)
                nc.scalar.activation(halves(sq)[h], halves(xc)[h], ACT.Square).then_inc(s["squares"], 1)
            for h in range(2):
                act.wait_ge(s["variance"], 2 * n + h + 1)
                cols = slice(h * 4 * G, (h + 1) * 4 * G)
                nc.scalar.activation(sigma[:, cols], ps[:, h, cols], ACT.Sqrt, bias=W("eps")).then_inc(s["sigma"], 1)

        xnj = xn[:].rearrange("p (j t) -> p j t", j=J)

        def bank_fill(n, k, g, rows, w_in):
            mm = nc.tensor.matmul(ps[0:rows, k, g * P:(g + 1) * P], w_in[:, C * g:C * g + rows],
                                  xnj[:, :, STEP_BANK * k:STEP_BANK * (k + 1)], start=(g == 0), stop=True, skip_group_check=True)
            if g == G - 1:
                mm.then_inc(s["bank filled"], 1)

        def bank_out(k, g, rows, w_out):
            mm = nc.tensor.matmul(ps[C * g:C * g + C, k, 0:P], w_out, states[0:rows, g, :, STEP_BANK * k + 1:STEP_BANK * (k + 1) + 1],
                                  start=True, stop=True)
            if g == G - 1:
                mm.then_inc(s["bank out"], 1)

        def step_columns(k, rows, t):
            return ps[0:rows, k, :].rearrange("p (b t) -> p b t", t=STEP_BANK)[:, :, t]

        def recur_tensor(pe, n, rows, w_in, w_state, w_out):
            for t in range(T):
                k, r = t // STEP_BANK, t % STEP_BANK
                if r == 0 and n == 0:
                    pe.wait_ge(s["bank biased"], k + 1)
                if t > 0:
                    pe.wait_ge(s["state"], n * T + t)
                nc.tensor.matmul(step_columns(k, rows, r), w_state, states[0:rows, :, :, t].rearrange("p g j -> p (g j)"),
                                 start=False, stop=True, skip_group_check=True).then_inc(s["pre-state"], 1)
                if k > 0 and r in (4, 7, 10, 13):
                    bank_out(k - 1, (r - 4) // 3, rows, w_out)
                if k < BANKS - 1 and r in (17, 20, 23, 26):
                    if n == 0 and k + 1 == 6 and r == 17:
                        pe.wait_ge(s["L0 skip added"], 2)
                    if n == 1 and STEP_BANK * (k + 1) == P and r == 17:
                        pe.wait_ge(s["F input"], 2)
                    bank_fill(n, k + 1, (r - 17) // 3, rows, w_in)
            pe.wait_ge(s["state"], (n + 1) * T)
            for g in range(G):
                bank_out(BANKS - 1, g, rows, w_out)

        def recur_scalar(act, n, rows, func):
            for t in range(T):
                act.wait_ge(s["pre-state"], n * T + t + 1)
                nc.scalar.activation(states[0:rows, :, :, t + 1].rearrange("p g j -> p (g j)"),
                                     step_columns(t // STEP_BANK, rows, t % STEP_BANK), func).then_inc(s["state"], 1)

        def add_bank_out(dve, n, k):
            dve.wait_ge(s["bank out"], BANKS * n + k + 1)
            cols = Xj[:, :, STEP_BANK * k:STEP_BANK * (k + 1)]
            return nc.vector.tensor_tensor(cols, cols, ps[:, k, 0:P].rearrange("p (j t) -> p j t", j=J), ALU.add)

        def gate(dve, link, d, j):
            dve.wait_ge(s["M products"], 3 * B * d + 12 * (j + 1))
            link(nc.vector.scalar_tensor_tensor(yg[:, j, :], xf[:, j, :], W(("fwd", "bwd")[d] + "_D"), ps[:, 6 + j % 2, :],
                                                ALU.mult, ALU.add))
            dve.wait_ge(s["M z"], 4 * (d + 1))
            nc.vector.tensor_tensor(yg[:, j, :], yg[:, j, :], zf[:, j, :], ALU.mult).then_inc(s["M y"], 1)

        def decay_part(link, d, part):
            rows, dst = cs[ROWS * d:ROWS * (d + 1), :, :], c3[ROWS * part:ROWS * (part + 1), :, :]
            link(nc.vector.tensor_copy(dst, rows))
            if part < 2:
                link(nc.vector.tensor_tensor(rows, rows, dst, ALU.subtract))

        def decay_operand(d, k):
            sums = c3[:, :, 1 - d:1 - d + T]
            if k < G:
                return nc.vector.tensor_scalar(key_side[d][k // 2][:, k % 2, :].rearrange("p (j t) -> p j t", j=J), sums,
                                               W("key_rows")[:, k:k + 1], W("query_ones")[:, k:k + 1], ALU.mult, ALU.add)
            h = k - G
            return nc.vector.tensor_scalar(query_side[d][:, h, :].rearrange("p (j t) -> p j t", j=J), sums,
                                           W("query_rows")[:, h:h + 1], W("key_minus_ones")[:, h:h + 1], ALU.mult, ALU.add)

        at = Arena()
        w1z = at(G, HID)
        w1s = at(HID)
        w4 = at(4, C)
        wbd = at(4, P)
        hidden = at(2 * G, HALF)
        rq = at(2, N)
        rkz = at(G, J, T)
        rmb = at(J * TT * G)
        w2s = at(C)
        b1s = at(1)
        b2s = at(1)
        h0 = sb("h0", [C, C])
        best = sb("best", [1, 8])
        op_at = sb("op_at", [1, 8], U32)
        masks = sb("masks", [1, 2, NB * NOPS], I32)
        flags = prob[0:1].rearrange("p a b -> p (a b)")[:, 0:(NB + 1) * NOPS].rearrange("p (n o) -> p n o", n=NB + 1)
        skipped = sb("skipped", [1, NOPS])
        acting = sb("acting", [1, (NB + 1) * NOPS], I32)
        rnm = nm[0:J * TT * G]

        def routed(name, eng, attention, feed_forward, picked):
            count = [eng.alloc_register(f"n_{what}") for what in ("pick", "attention", "ffn")]
            for r in count:
                eng.reg_mov(r, 0)
            op, at, use_a, use_f = (eng.alloc_register(r) for r in ("op", "block", "attention_mask", "ffn_mask"))
            eng.wait_ge(s["op picked"], 1)
            eng.reg_load(op, op_at[0:1, 0:1])
            eng.reg_load(at, acting[0:1, bass.ds(nc.s_assert_within(eng.snap(op), 0, NOPS - 1), 1)])
            with eng.Fori(0, STEPS):
                with eng.If_lt(at, NB):
                    with eng.Fori(0, STEPS):
                        with eng.If_lt(at, NB):
                            i = nc.s_assert_within(eng.snap(at), 0, NB - 1)
                            o = nc.s_assert_within(eng.snap(op), 0, NOPS - 1)
                            at_op = nc.s_assert_within(i * NOPS + o, 0, NB * NOPS - 1)
                            eng.reg_load(use_a, masks[0:1, 0, bass.ds(at_op, 1)])
                            eng.reg_load(use_f, masks[0:1, 1, bass.ds(at_op, 1)])
                            with eng.If_ne(use_a, 0):
                                attention(i, o, eng.snap(count[1]))
                                eng.reg_add(count[1], count[1], 1)
                            eng.reg_add(count[0], count[0], 1)
                            with eng.If_ne(use_f, 0):
                                feed_forward(i, o, eng.snap(count[2]))
                                eng.reg_add(count[2], count[2], 1)
                            picked(eng.snap(count[0]))
                            eng.wait_ge(s["op picked"], eng.snap(count[0]) + 1)
                            eng.sem_inc(s[name + " saw the pick"], 1)
                            eng.reg_load(op, op_at[0:1, 0:1])
                            after = nc.s_assert_within(eng.snap(at) * NOPS + NOPS + eng.snap(op), 0, (NB + 1) * NOPS - 1)
                            eng.reg_load(at, acting[0:1, bass.ds(after, 1)])

        M_BLOCKS = (((0, 0), (0, 1), (1, 1)), ((0, 0), (1, 0), (1, 1)))

        block = ctx.enter_context(nc.Block())

        @block.sync
        def _(sp):
            sp.dma_start(Xj, xr).then_inc(s["x loaded"], 16)
            l0 = COL["L1_w1T"][0]
            sp.dma_start(wsb[:, 0:l0], weights[:, 0:l0]).then_inc(s["L0 weights loaded"], 16)
            sp.dma_start(wsb[:, l0:], weights[:, l0:]).then_inc(s["weights loaded"], 16)
            sp.dma_start(csb[:], consts).then_inc(s["consts loaded"], 16)
            sp.dma_start(masks[:, 0, :], attn_mask.rearrange("(a n) o -> a (n o)", a=1)).then_inc(s["masks loaded"], 16)
            sp.dma_start(masks[:, 1, :], ffn_mask.rearrange("(a n) o -> a (n o)", a=1)).then_inc(s["masks loaded"], 16)
            if upto >= 4:
                sp.wait_ge(s["M weights"], 1)
                sp.wait_ge(s["normalised"], 8)
                for i in range(K):
                    for g in range(G):
                        sp.dma_start(xs[C * i:C * i + C, :, g, K - 1 - i:K - 1 - i + T],
                                     xn[C * g:C * g + C, :].rearrange("p (j t) -> p j t", j=J)).then_inc(s["M stack"], 16)
            if upto < 99:
                sp.wait_ge(s["stage done"], 1)
                if dump == "X":
                    sp.dma_start(out.rearrange("(j g) c h w -> (g c) j (h w)", g=G), Xj).then_inc(s["stored"], 16)
                sp.wait_ge(s["stored"], 16)
                return
            sp.wait_ge(s["normalised"], 10)

            def attention(i, op, n):
                for m, w in enumerate((wq, wk, wv, wo)):
                    sp.dma_start(w4[:, m, :], w[bass.ds(i, 1), bass.ds(op, 1), :, :].rearrange("a b c d -> (a b) c d")
                                 .to_broadcast([G, C, C])).then_inc(s["R attention weights"], 16)

            def feed_forward(i, op, n):
                at = (bass.ds(i, 1), bass.ds(op, 1))
                sp.dma_start(w1s, w1[at[0], at[1], :, :].rearrange("a b c d -> (a b) c d").to_broadcast([G, C, HID]))\
                    .then_inc(s["R ffn weights"], 16)
                sp.dma_start(b1s, b1[at[0], at[1], :].rearrange("a b (c d) -> (a b c) d", d=1)).then_inc(s["R ffn weights"], 16)
                sp.dma_start(w2s, w2[at[0], at[1], :, :].rearrange("a b c d -> (a b c) d")).then_inc(s["R ffn weights"], 16)
                sp.dma_start(b2s, b2[at[0], at[1], :].rearrange("a b (c d) -> (a b) c d", d=1).to_broadcast([G, C, 1]))\
                    .then_inc(s["R ffn weights"], 16)

            routed("sync", sp, attention, feed_forward, lambda n: None)
            sp.wait_ge(s["X ready"], 6)
            sp.dma_start(out.rearrange("(j g) c h w -> (g c) j (h w)", g=G), Xj).then_inc(s["stored"], 16)
            sp.wait_ge(s["stored"], 16)

        @block.tensor
        def _(pe):
            pe.wait_ge(s["L0 weights loaded"], 16)
            nc.tensor.matmul(ps[:, 4, 0:P], W("L0_W_in", E2), W("L0_BmT", E2), start=True, stop=True)
            nc.tensor.matmul(ps[:, 4, P:2 * P], W("L0_Cm", E2), W("L0_W_outT", E2), start=True, stop=True)
            nc.tensor.matmul(ps[0:E2, 5, 0:1], W("L0_W_inT", C), W("L0_beta", C), start=True, stop=True).then_inc(s["L0 folds"], 1)
            pe.wait_ge(s["L0 z bias"], 1)
            nc.tensor.matmul(ps[:, 4, 2 * P:3 * P], W("L0_W_in", E2), d_wout[:], start=True, stop=True)
            nc.tensor.matmul(ps[:, 5, 2:3], W("L0_BmT", E2), z_b[:], start=True, stop=True)
            nc.tensor.matmul(ps[:, 5, 1:2], d_wout[:], z_b[:], start=True, stop=True).then_inc(s["L0 folds"], 1)
            norm_tensor(pe, 0)
            pe.wait_ge(s["L0 weights"], 1)
            pe.wait_ge(s["normalised"], 2)
            for g in range(G):
                bank_fill(0, 0, g, NS, u_w[:])
            for h in range(2):
                nc.tensor.matmul(ps[:, 6 + h, :], g2[:], halves(xn)[h], start=True, stop=True).then_inc(s["L0 skip"], 1)
            recur_tensor(pe, 0, NS, u_w[:], W("L0_AT", NS)[:, 0:NS], g1[0:NS, 0:C])
            pe.wait_ge(s["weights loaded"], 16)
            for i, w in enumerate("qkv"):
                mm = nc.tensor.matmul(ps[:, 0, i * P:(i + 1) * P], W("L2_A_" + w, HD), W(f"L2_B_{w}T", HD), start=True, stop=True)
            mm.then_inc(s["lora products"], 1)
            pe.wait_ge(s["gn done"], 1)
            for i, w in enumerate(("L1_w1T", "L1_w2T", "L1_waT")):
                for h in range(2):
                    nc.tensor.matmul(ps[:, 2 * i + h, :], W(w), halves(xn)[h], start=True, stop=True).then_inc(s["L1 proj"], 1)
            pe.wait_ge(s["L1 prelu"], 3)
            for jt in range(J * TT):
                mm = nc.tensor.matmul(ps[:, 6 + jt // 4, (jt % 4) * P:(jt % 4 + 1) * P], pm[:, 2, jt * P:(jt + 1) * P],
                                      W("ident"), is_transpose=True, start=True, stop=True)
            mm.then_inc(s["values turned"], 1)
            pe.wait_ge(s["L1 keys"], 1)
            q1 = pm[:, 0, :].rearrange("p (j t) -> p j t", j=J)
            for b in range(B):
                j, g = b // G, b % G
                if b >= 4:
                    pe.wait_ge(s["L1 max"], b - 3)
                for qt in range(TT):
                    mm = nc.tensor.matmul(ps[:, b % 4, qt * T:(qt + 1) * T], q1[:, j, qt * P:(qt + 1) * P], e2z[:, g, j, :],
                                          start=True, stop=True)
                mm.then_inc(s["L1 scores"], 1)
            pe.wait_ge(s["L1 max"], B)
            for jt in range(J * TT):
                mm = nc.tensor.matmul(ps[:, 4 + jt // 4, (jt % 4) * P:(jt % 4 + 1) * P], mbx[:, jt // TT, jt % TT, :],
                                      W("neg_ident"), start=True, stop=True)
            mm.then_inc(s["L1 max rows"], 1)
            pe.wait_ge(s["L1 queries"], 1)
            q2 = e1m[:].rearrange("p (j t) -> p j t", j=J)
            pe.wait_ge(s["values by token"], 1)
            for quarter in range(J + 1):
                if quarter < J:
                    j = quarter
                    for g in range(G):
                        b = j * G + g
                        if b >= 4:
                            pe.wait_ge(s["L1 exp"], b - 3)
                        for kt in range(TT):
                            mm = nc.tensor.matmul(ps[:, b % 4, kt * T:(kt + 1) * T], e2z[:, g, j, kt * P:(kt + 1) * P], q2[:, j, :],
                                                  start=True, stop=True)
                        mm.then_inc(s["L1 scores T"], 1)
                if quarter >= 1:
                    j = quarter - 1
                    cols = slice((j % 2) * T, (j % 2 + 1) * T)
                    pe.wait_ge(s["L1 exp"], G * quarter)
                    for kt in range(TT):
                        for bank in (4, 6):
                            for g in range(G):
                                lhs = vt[:, j * TT + kt, C * g:C * g + C] if bank == 4 else W("ones32")
                                mm = nc.tensor.matmul(ps[C * g:C * g + C, bank + j // 2, cols], lhs,
                                                      prob6[:, (j * G + g) % 6, kt * T:(kt + 1) * T],
                                                      start=(kt == 0), stop=(kt == TT - 1))
                    mm.then_inc(s["L1 pv"], 1)
            if upto == 1:
                return
            norm_tensor(pe, 1)
            pe.wait_ge(s["L2 weights"], 1)
            pe.wait_ge(s["normalised"], 4)
            for i, w in enumerate((wqkv[:, 0, :], wrot[:, 0, :], wqkv[:, 1, :], wrot[:, 1, :])):
                for h in range(2):
                    if i < 2:
                        pe.wait_ge(s["normalised"], 4)
                    mm = nc.tensor.matmul(ps[:, 2 * i + h, :], w, halves(xn)[h], start=True, stop=True)
                mm.then_inc(s["L2 proj"], 1)
            pe.wait_ge(s["L2 rotated"], 2)
            for h in range(2):
                mm = nc.tensor.matmul(ps[:, h, :], wqkv[:, 2, :], halves(xn)[h], start=True, stop=True)
            mm.then_inc(s["L2 proj"], 1)
            pe.wait_ge(s["L2 values"], 1)
            for jt in range(J * TT):
                mm = nc.tensor.matmul(ps[:, 2 + jt // 4, (jt % 4) * P:(jt % 4 + 1) * P], oat[:, jt * P:(jt + 1) * P],
                                      W("ident"), is_transpose=True, start=True, stop=True)
            mm.then_inc(s["values turned"], 1)
            pe.wait_ge(s["consts loaded"], 16)
            pe.wait_ge(s["L2 keys scalar"], 1)
            pe.wait_ge(s["L2 values by token"], 1)
            q = qk[:, 0, :].rearrange("p (j t) -> p j t", j=J)
            for b in range(B):
                j, g = b // G, b % G
                k0 = 3 * (b % 2)
                if b >= 2:
                    pe.wait_ge(s["L2 max"], 2 * b - 2)
                nc.tensor.matmul(ps[:, k0, :], CB("identb"), CB("mask_above").unsqueeze(1).to_broadcast([P, HEADS, P]),
                                 start=True, stop=False)
                for h in range(HEADS):
                    nc.tensor.matmul(ps[:, k0, h * P:(h + 1) * P], q[:, j, 0:P], kz[:, g * HEADS + h, j, 0:P],
                                     start=False, stop=(h == HEADS - 1))
                for pair in range(2):
                    nc.tensor.matmul(ps[:, k0 + 1 + pair, :], CB("identb"),
                                     CB_pair("zeros", "mask_above").unsqueeze(1).to_broadcast([P, 2, T]), start=True, stop=False)
                    for h in range(2):
                        mm = nc.tensor.matmul(ps[:, k0 + 1 + pair, h * T:(h + 1) * T], q[:, j, P:T],
                                              kz[:, g * HEADS + 2 * pair + h, j, :], start=False, stop=(h == 1))
                mm.then_inc(s["L2 scores"], 1)
            pe.wait_ge(s["L2 max"], 2 * B)
            nc.tensor.matmul(ps[:, 6, 0:P], mb, W("neg_ident"), start=True, stop=True).then_inc(s["L2 max rows"], 1)
            pe.wait_ge(s["L2 max parts"], 2)

            def project(b):
                j, g = b // G, b % G
                pe.wait_ge(s["L2 attended"], b + 1)
                nc.tensor.matmul(ps[C * g:C * g + C, 6 + j // 2, (j % 2) * T:(j % 2 + 1) * T], W("L2_wo_by_head"),
                                 oat[:, g * T:(g + 1) * T], start=True, stop=True).then_inc(s["L2 out"], 1)

            for b in range(B + 1):
                if b < B:
                    j, g = b // G, b % G
                    if b >= 1:
                        pe.wait_ge(s["L2 exp"], 2 * b - 1)
                    for pair in range(2):
                        nc.tensor.matmul(ps[:, pair, :], CB("identb"),
                                         CB_pair("mask_below", "zeros2").unsqueeze(1).to_broadcast([P, 2, T]), start=True, stop=False)
                        for h in range(2):
                            gh = g * HEADS + 2 * pair + h
                            nc.tensor.matmul(ps[:, pair, h * T:(h + 1) * T], kz[:, gh, j, 0:P], q[:, j, :], start=False, stop=False)
                            for qt in range(TT):
                                row = (j * TT + qt) * G * HEADS + gh
                                for part in range(2):
                                    mm = nc.tensor.matmul(ps[:, pair, h * T + qt * P:h * T + (qt + 1) * P],
                                                          CB("identb")[:, row:row + 1].to_broadcast([P, P]), nm[:, part, :],
                                                          start=False, stop=(h == 1 and qt == 1 and part == 1))
                    mm.then_inc(s["L2 scores T"], 1)
                    if b >= 1:
                        pe.wait_ge(s["L2 exp"], 2 * b)
                    nc.tensor.matmul(ps[:, 2, :], CB("identb"), CB("mask_below").unsqueeze(1).to_broadcast([P, HEADS, P]),
                                     start=True, stop=False)
                    for h in range(HEADS):
                        gh = g * HEADS + h
                        row = (j * TT + 1) * G * HEADS + gh
                        nc.tensor.matmul(ps[:, 2, h * P:(h + 1) * P], kz[:, gh, j, P:T], q[:, j, P:T], start=False, stop=False)
                        for part in range(2):
                            mm = nc.tensor.matmul(ps[:, 2, h * P:(h + 1) * P], CB("identb")[:, row:row + 1].to_broadcast([P, P]),
                                                  nm[:, part, :], start=False, stop=(h == HEADS - 1 and part == 1))
                    mm.then_inc(s["L2 scores T"], 1)
                if b >= 3:
                    project(b - 3)
                if b >= 1:
                    m = b - 1
                    j, g = m // G, m % G
                    pe.wait_ge(s["L2 exp"], 2 * b)
                    for part in range(2):
                        for kt in range(TT):
                            for h in range(HEADS):
                                pk = (prob[:, m % 2, h * T:(h + 1) * T] if kt == 0 else
                                      prob[:, m % 2, 2 * HALF + h * P:2 * HALF + (h + 1) * P])
                                lhs = vt[:, j * TT + kt, C * g:C * g + C] if part == 0 else W("ones32")
                                mm = nc.tensor.matmul(ps[C * h:C * h + C, 4 + m % 2, part * T + kt * P:(part + 1) * T], lhs, pk,
                                                      start=(kt == 0), stop=(kt == 1))
                    mm.then_inc(s["L2 pv"], 1)
            for b in (B - 2, B - 1):
                project(b)
            if upto == 2:
                return
            norm_tensor(pe, 2)
            pe.wait_ge(s["normalised"], 6)
            for h in range(2):
                nc.tensor.matmul(ps[:, 4 + h, :], W("F_WT"), halves(xn)[h], start=True, stop=True).then_inc(s["F proj"], 1)
            pe.wait_ge(s["F row stats"], 1)
            nc.tensor.matmul(ps[:, 6, 0:2], W("avg_g"), fst[:, 0:2], start=True, stop=True).then_inc(s["F stats"], 1)
            pe.wait_ge(s["F input"], 1)
            for g in range(G):
                bank_fill(1, 0, g, C, W("ident"))
            recur_tensor(pe, 1, C, W("ident"), W("F_VT", C)[:, 0:C], W("ident", C)[:, 0:C])
            if upto == 3:
                return
            norm_tensor(pe, 3)
            pe.wait_ge(s["normalised"], 8)
            for h in range(2):
                mm = nc.tensor.matmul(ps[0:2 * ROWS, 4 + h, :], W("M_dtW"), halves(xn)[h], start=True, stop=True)
            mm.then_inc(s["M dt proj"], 1)

            def project_x(d):
                off = (K - 1) * d
                for gp in range(2):
                    for h in range(2):
                        for gl in range(2):
                            mm = nc.tensor.matmul(ps[E2 * gl:E2 * (gl + 1), 2 * gp + h, :], wx[:, d, :],
                                                  xs[:, 2 * h:2 * h + 2, 2 * gp + gl, off:off + T], start=True, stop=True)
                        mm.then_inc(s["M x proj"], 1)

            def project_z(d):
                for gp in range(2):
                    for h in range(2):
                        nc.tensor.matmul(ps[:, 2 * gp + h, :], W(("fwd", "bwd")[d] + "_z")[:, gp * P:(gp + 1) * P], halves(xn)[h],
                                         start=True, stop=True).then_inc(s["M z proj"], 1)

            def project_out(d):
                pe.wait_ge(s["M squares"], J * (d + 1))
                for bank, lhs, rhs, done in ((4, W("avg_e"), zf, s["M mean squares"]), (6, wout[:, d, :], yg, s["M out"])):
                    for h in range(2):
                        for gp in range(2):
                            mm = nc.tensor.matmul(ps[2 * C * gp:2 * C * (gp + 1), bank + h, :], lhs,
                                                  rhs[:, 2 * h:2 * h + 2, gp * T:(gp + 1) * T], start=True, stop=True)
                        mm.then_inc(done, 1)

            project_z(0)
            pe.wait_ge(s["M weights"], 1)
            pe.wait_ge(s["M stack"], 16 * K * G)
            pe.wait_ge(s["M z"], 4)
            project_x(0)
            pe.wait_ge(s["M dt"], 1)
            for jt in range(J * TT):
                mm = nc.tensor.matmul(ps[:, 6, jt * 2 * ROWS:(jt + 1) * 2 * ROWS], drow[0:2 * ROWS, 3, jt * P:(jt + 1) * P],
                                      W("ident", 2 * ROWS)[:, 0:2 * ROWS], is_transpose=True, start=True, stop=True)
            mm.then_inc(s["M dt turned"], 1)
            for d in range(2):
                off = (K - 1) * d
                if d == 1:
                    pe.wait_ge(s["M decay"], 3 * B)
                    project_x(1)
                    project_out(0)
                pe.wait_ge(s["M x"], 4 * (d + 1))
                for jt in range(J * TT):
                    for gp in range(2):
                        c0 = gp * T + (jt % TT) * P
                        mm = nc.tensor.matmul(ps[:, jt // 2, (2 * (jt % 2) + gp) * P:(2 * (jt % 2) + gp + 1) * P],
                                              xf[:, jt // TT, c0:c0 + P], W("ident"), is_transpose=True, start=True, stop=True)
                    if jt % 2 == 1:
                        mm.then_inc(s["M x turned"], 1)
                for i in range(2):
                    if d == 1:
                        pe.wait_ge(s["M sigma"] if i == 0 else s["M out saved"], 2 if i == 0 else 1)
                    elif i == 1:
                        pe.wait_ge(s["M dt by token"], 1)
                    for h in range(2):
                        for g in range(G):
                            mm = nc.tensor.matmul(ps[C * g:C * g + C, 4 + 2 * i + h, :], wbc[:, d, i, :],
                                                  xs[:, 2 * h:2 * h + 2, g, off:off + T], start=True, stop=True)
                    mm.then_inc(s["M bc"], 1)
                if d == 1:
                    pe.wait_ge(s["M xdt"], 2)
                    project_z(1)
                pe.wait_ge(s["M decay operands"], d + 1)
                pe.wait_ge(s["M xdt"], d + 1)
                pe.wait_ge(s["M B split"], d + 1)
                pe.wait_ge(s["M C"], d + 1)
                pe.wait_ge(s["M z"], 4 * (d + 1))
                cpj = cp.rearrange("p (j t) -> p j t", j=J)
                blocks = M_BLOCKS[d]

                for n in range(3 * B + 2):
                    if n < 3 * B:
                        b, (st_, tt_) = n // 3, blocks[n % 3]
                        j, g = b // G, b % G
                        count = 3 * B * d + n
                        if count >= 4:
                            pe.wait_ge(s["M decay"], count - 3)
                        if n % 3 == 0:
                            if b >= 2:
                                pe.wait_ge(s["M gram"], 3 * B * d + 3 * (b - 1))
                            for i, (sk, tq) in enumerate(blocks):
                                mm = nc.tensor.matmul(ps[:, 4 + b % 2, i * P:(i + 1) * P], bz[:, g, j, sk * P:(sk + 1) * P],
                                                      cpj[:, j, tq * P:(tq + 1) * P], start=(i == 0), stop=(i == 2))
                            mm.then_inc(s["M CB"], 1)
                        diag = st_ == tt_
                        if diag:
                            nc.tensor.matmul(ps[:, n % 4, :], CB("identb"),
                                             CB("mask_below" if d == 0 else "mask_above").unsqueeze(1).to_broadcast([P, HEADS, P]),
                                             start=True, stop=False)
                        keys, queries = j * T + st_ * P, j * T + tt_ * P
                        nc.tensor.matmul(ps[:, n % 4, :], key_side[d][g // 2][:, g % 2, keys:keys + P],
                                         query_side[d][:, :, queries:queries + P], start=not diag, stop=True)\
                            .then_inc(s["M exponent"], 1)
                    if n >= 2:
                        m = n - 2
                        b, (st_, tt_) = m // 3, blocks[m % 3]
                        j, g = b // G, b % G
                        first = m % 3 == (0 if tt_ == 0 else 1 + d)
                        last = m % 3 == (d if tt_ == 0 else 2)
                        if m % 12 == 0 and 4 * d + j >= 2:
                            pe.wait_ge(s["M y"], 4 * d + j - 1)
                        pe.wait_ge(s["M gram"], 3 * B * d + m + 1)
                        c0 = (g // 2) * T + tt_ * P
                        y = [ps[E2 * (g % 2) + C * pair:E2 * (g % 2) + C * (pair + 1), 6 + j % 2, c0:c0 + P] for pair in range(2)]
                        for i in range(2):
                            for pair in range(2):
                                h = 2 * pair + i
                                mm = nc.tensor.matmul(y[pair], xdt[:, j * TT + st_, g, h, :], gram[:, m % 3, h * P:(h + 1) * P],
                                                      start=(first and i == 0), stop=(last and i == 1))
                        mm.then_inc(s["M products"], 1)
            project_out(1)
            if upto == 4:
                return
            norm_tensor(pe, 4)

            def attention(i, op, n):
                pe.wait_ge(s["R attention weights spread"], n + 1)
                for m in range(3):
                    for h in range(2):
                        mm = nc.tensor.matmul(ps[:, 2 * m + h, :], wbd[:, m, :], halves(xn)[h], start=True, stop=True)
                    mm.then_inc(s["R proj"], 1)
                pe.wait_ge(s["R copied"], n * 3 + 3)
                for jt in range(J * TT):
                    mm = nc.tensor.matmul(ps[:, 6 + jt // 4, (jt % 4) * P:(jt % 4 + 1) * P], oat[:, jt * P:(jt + 1) * P],
                                          W("ident"), is_transpose=True, start=True, stop=True)
                mm.then_inc(s["R values turned"], 1)
                pe.wait_ge(s["R keys"], n + 1)
                q = rq[:, 0, :].rearrange("p (j t) -> p j t", j=J)
                for b in range(B):
                    j, g = b // G, b % G
                    if b >= 4:
                        pe.wait_ge(s["R max"], n * B + (b - 3))
                    for qt in range(TT):
                        mm = nc.tensor.matmul(ps[:, b % 4, qt * T:(qt + 1) * T], q[:, j, qt * P:(qt + 1) * P], rkz[:, g, j, :],
                                              start=True, stop=True)
                    mm.then_inc(s["R scores"], 1)
                pe.wait_ge(s["R max"], n * B + B)
                nc.tensor.matmul(ps[0:J * TT * G, 4, 0:P], rmb, W("neg_ident"), start=True, stop=True).then_inc(s["R max rows"], 1)
                pe.wait_ge(s["R max parts"], n * 2 + 2)
                pe.wait_ge(s["R values by token"], n + 1)
                rows = J * TT * G
                for b in range(B + 1):
                    if b < B:
                        j, g = b // G, b % G
                        if b >= 4:
                            pe.wait_ge(s["R exp"], n * B + (b - 3))
                        for kt in range(TT):
                            nc.tensor.matmul(ps[:, b % 4, kt * T:(kt + 1) * T], rkz[:, g, j, kt * P:(kt + 1) * P], q[:, j, :],
                                             start=(kt == 0), stop=False)
                            for qt in range(TT):
                                row = (j * TT + qt) * G + g
                                for part in range(2):
                                    c0 = kt * T + qt * P
                                    mm = nc.tensor.matmul(ps[:, b % 4, c0:c0 + P],
                                                          CB("identb", rows)[:, row:row + 1].to_broadcast([rows, P]),
                                                          rnm[:, part, :], start=False, stop=(kt == 1 and qt == 1 and part == 1))
                        mm.then_inc(s["R scores T"], 1)
                    if b >= 1:
                        j, g = (b - 1) // G, (b - 1) % G
                        pe.wait_ge(s["R exp"], n * B + b)
                        for kt in range(TT):
                            pk = prob[:, (b - 1) % 2, kt * T:(kt + 1) * T]
                            cols = slice((j % 2) * T, (j % 2 + 1) * T)
                            nc.tensor.matmul(ps[C * g:C * g + C, 4 + j // 2, cols], vt[:, j * TT + kt, C * g:C * g + C], pk,
                                             start=(kt == 0), stop=(kt == TT - 1))
                            mm = nc.tensor.matmul(ps[C * g:C * g + C, 6 + j // 2, cols], W("ones32"), pk,
                                                  start=(kt == 0), stop=(kt == TT - 1))
                        mm.then_inc(s["R pv"], 1)
                pe.wait_ge(s["R attended"], n + 1)
                for h in range(2):
                    mm = nc.tensor.matmul(ps[:, h, :], wbd[:, 3, :], halves(oat)[h], start=True, stop=True)
                mm.then_inc(s["R attention out"], 1)
                pe.wait_ge(s["R attention written"], n + 1)

            def feed_forward(i, op, n):
                pe.wait_ge(s["R ffn weights"], n * 64 + 64)
                for k in range(2 * G + 1):
                    if k < 2 * G:
                        if k >= 4:
                            done = s["R relu scalar"] if k % 2 == 0 else s["R relu vector"]
                            pe.wait_ge(done, n * 4 + (k - 4) // 2 + 1)
                        if k < G:
                            pe.wait_ge(s["R first weights spread"], n * G + (k + 1))
                        nc.tensor.matmul(ps[:, k % 4, :], w1z[:, k % G, :], halves(xn)[k // G], start=True, stop=True)\
                            .then_inc(s["R hidden"], 1)
                    if k >= 1:
                        m = k - 1
                        pe.wait_ge(s["R relu scalar"] if m % 2 == 0 else s["R relu vector"], n * 4 + m // 2 + 1)
                        g = m % G
                        nc.tensor.matmul(ps[C * g:C * g + C, 4 + m // G, :], w2s, hidden[:, m, :], start=True, stop=True)\
                            .then_inc(s["R ffn out"], 1)

            routed("tensor", pe, attention, feed_forward, lambda n: None)

        @block.scalar
        def _(act):
            norm_scalar(act, 0)
            act.preload_act_table(ACT.Tanh)
            recur_scalar(act, 0, NS, ACT.Tanh)
            act.wait_ge(s["gn stats"], 1)
            nc.scalar.activation(rstd[:], mv[:, :, 1], ACT.Sqrt, bias=W("eps")).then_inc(s["gn sigma"], 1)
            for i, bias in enumerate(("L1_b1", "L1_b2", "L1_ba")):
                act.wait_ge(s["L1 proj"], 2 * i + 2)
                nc.scalar.activation(pr[:, i, :], ps[:, 2 * i:2 * i + 2, :].rearrange("p a b -> p (a b)"), ACT.Identity,
                                     bias=W(bias)).then_inc(s["L1 biased"], 1)
            act.wait_ge(s["values turned"], 1)
            nc.scalar.activation(vt[:].rearrange("p a b -> p (a b)"), ps[:, 6:8, :].rearrange("p a b -> p (a b)"),
                                 ACT.Copy).then_inc(s["values by token"], 1)
            for b in range(B):
                act.wait_ge(s["L1 scores T"], b + 1)
                if b >= 6:
                    act.wait_ge(s["L1 pv"], (b - 6) // G + 1)
                nc.scalar.activation(prob6[:, b % 6, :], ps[:, b % 4, :], ACT.Exp).then_inc(s["L1 exp"], 1)
            if upto == 1:
                return
            norm_scalar(act, 1)
            act.wait_ge(s["L2 proj"], 5)
            nc.scalar.activation(oat[:], banks(0, 2), ACT.Copy).then_inc(s["L2 values"], 1)
            act.wait_ge(s["L2 rotated"], 2)
            for gh in range(8, G * HEADS):
                ins = nc.scalar.activation(kz[:, gh, :, :].rearrange("p j t -> p (j t)"), qk[:, 1, :], ACT.Copy,
                                           scale=W("head_mask")[:, gh:gh + 1])
            ins.then_inc(s["L2 keys scalar"], 1)
            act.preload_act_table(ACT.Exp)
            for b in range(B):
                if b >= 2:
                    act.wait_ge(s["L2 pv"], b - 1)
                act.wait_ge(s["L2 scores T"], 2 * b + 1)
                nc.scalar.activation(prob[:, b % 2, 0:2 * HALF], banks(0, 2), ACT.Exp, scale=HD ** -0.5).then_inc(s["L2 exp"], 1)
                act.wait_ge(s["L2 scores T"], 2 * b + 2)
                nc.scalar.activation(prob[:, b % 2, 2 * HALF:3 * HALF], ps[:, 2, :], ACT.Exp, scale=HD ** -0.5)\
                    .then_inc(s["L2 exp"], 1)
            if upto == 2:
                return
            norm_scalar(act, 2)
            act.wait_ge(s["F variance"], 1)
            nc.scalar.activation(fst[:, 3:4], fst[:, 3:4], ACT.Sqrt, bias=W("eps")).then_inc(s["F sigma"], 1)
            act.preload_act_table(ACT.Sigmoid)
            recur_scalar(act, 1, C, ACT.Sigmoid)
            if upto == 3:
                return
            norm_scalar(act, 3)
            rows = 2 * ROWS
            act.wait_ge(s["M dt steps"], 1)
            nc.scalar.activation(drow[0:rows, 1, :], drow[0:rows, 1, :], ACT.Exp).then_inc(s["M dt exp"], 1)
            nc.scalar.activation(fst[0:rows, 4:5], W("M_A_log", rows), ACT.Exp).then_inc(s["M dt exp"], 1)
            act.wait_ge(s["M dt exp"], 1)
            nc.scalar.activation(drow[0:rows, 1, :], drow[0:rows, 1, :], ACT.Ln, bias=W("one", rows)).then_inc(s["M dt log"], 1)
            act.preload_act_table(ACT.Silu)

            def gates(d):
                for k in range(4):
                    gp, h = k // 2, k % 2
                    act.wait_ge(s["M z proj"], 4 * d + k + 1)
                    nc.scalar.activation(zf[:, 2 * h:2 * h + 2, gp * T:(gp + 1) * T],
                                         ps[:, k, :].rearrange("p (j t) -> p j t", j=2), ACT.Silu).then_inc(s["M z"], 1)

            def sigmas(d):
                for h in range(2):
                    act.wait_ge(s["M mean squares"], 2 * d + h + 1)
                    if d == 1:
                        act.wait_ge(s["M forward added"], 1)
                    nc.scalar.activation(halves(oat)[h], ps[:, 4 + h, :], ACT.Sqrt, bias=W("eps")).then_inc(s["M sigma"], 1)

            def squares(d, j):
                act.wait_ge(s["M y"], J * d + j + 1)
                nc.scalar.activation(zf[:, j, :], yg[:, j, :], ACT.Square).then_inc(s["M squares"], 1)

            gates(0)
            for d in range(2):
                name = ("fwd", "bwd")[d]
                if d == 1:
                    sigmas(0)
                    act.wait_ge(s["M y"], J)
                for k in range(4):
                    gp, h = k // 2, k % 2
                    act.wait_ge(s["M x proj"], 4 * d + k + 1)
                    nc.scalar.activation(xf[:, 2 * h:2 * h + 2, gp * T:(gp + 1) * T],
                                         ps[:, k, :].rearrange("p (j t) -> p j t", j=2), ACT.Silu, bias=W(name + "_bx"))\
                        .then_inc(s["M x"], 1)
                if d == 0:
                    act.wait_ge(s["M dt turned"], 1)
                    nc.scalar.activation(dtt.rearrange("p a b -> p (a b)"), ps[:, 6, :], ACT.Copy).then_inc(s["M dt by token"], 1)
                act.wait_ge(s["M bc"], 2 * d + 1)
                nc.scalar.activation(bp, banks(4, 6), ACT.Silu, bias=W(name + "_bB")).then_inc(s["M B"], 1)
                act.wait_ge(s["M bc"], 2 * d + 2)
                nc.scalar.activation(cp, banks(6, 8), ACT.Silu, bias=W(name + "_bC")).then_inc(s["M C"], 1)
                if d == 1:
                    gates(1)
                act.preload_act_table(ACT.Exp)
                for n in range(3 * B):
                    count = 3 * B * d + n
                    act.wait_ge(s["M exponent"], count + 1)
                    if count >= 3:
                        act.wait_ge(s["M gram"], count - 2)
                    nc.scalar.activation(decay[:, n % 3, :], ps[:, n % 4, :], ACT.Exp).then_inc(s["M decay"], 1)
                    if n % 12 == 6 and n > 12:
                        squares(d, n // 12 - 1)
                squares(d, J - 1)
                act.preload_act_table(ACT.Sqrt)
            sigmas(1)
            if upto == 4:
                return
            norm_scalar(act, 4)

            def attention(i, op, n):
                for m, dst in enumerate((rq[:, 0, :], rq[:, 1, :], oat[:])):
                    act.wait_ge(s["R proj"], n * 3 + (m + 1))
                    nc.scalar.activation(dst, banks(2 * m, 2 * m + 2), ACT.Copy).then_inc(s["R copied"], 1)
                act.wait_ge(s["R values turned"], n + 1)
                nc.scalar.activation(vt[:].rearrange("p a b -> p (a b)"), banks(6, 8), ACT.Copy).then_inc(s["R values by token"], 1)
                for b in range(B):
                    act.wait_ge(s["R scores T"], n * B + (b + 1))
                    if b >= 2:
                        act.wait_ge(s["R pv"], n * B + (b - 1))
                    nc.scalar.activation(prob[:, b % 2, 0:HALF], ps[:, b % 4, :], ACT.Exp, scale=C ** -0.5).then_inc(s["R exp"], 1)

            def feed_forward(i, op, n):
                act.preload_act_table(ACT.Relu)
                act.wait_ge(s["R ffn weights"], n * 64 + 64)
                for k in range(0, 2 * G, 2):
                    act.wait_ge(s["R hidden"], n * 8 + (k + 1))
                    nc.scalar.activation(hidden[:, k, :], ps[:, k % 4, :], ACT.Relu, bias=b1s).then_inc(s["R relu scalar"], 1)

            routed("scalar", act, attention, feed_forward, lambda n: None)

        @block.vector
        def _(dve):
            link = Chain(dve, s["vector step"])
            dve.wait_ge(s["x loaded"], 16)
            nc.vector.memset(states[:, :, :, 0:1], 0.0)
            nc.vector.memset(mbx[:].rearrange("p a b c -> p (a b c)"), 0.0).then_inc(s["X ready"], 1)
            dve.wait_ge(s["L0 weights loaded"], 16)
            nc.vector.tensor_scalar(d_wout[:], W("L0_W_outT", E2), W("L0_D", E2), None, ALU.mult).then_inc(s["L0 d_wout"], 1)
            dve.wait_ge(s["L0 folds"], 1)
            nc.vector.tensor_tensor(z_b[:], W("L0_b_in", E2), ps[0:E2, 5, 0:1], ALU.add).then_inc(s["L0 d_wout"], 1)
            dve.wait_ge(s["L0 d_wout"], 2)
            nc.vector.scalar_tensor_tensor(u_w[:], ps[:, 4, 0:P], W("L0_gamma"), W("block"), ALU.mult, ALU.mult)
            nc.vector.tensor_tensor(g1[:], W("block"), ps[:, 4, P:2 * P], ALU.mult).then_inc(s["L0 z bias"], 1)
            dve.wait_ge(s["L0 folds"], 2)
            nc.vector.scalar_tensor_tensor(g2[:], ps[:, 4, 2 * P:3 * P], W("L0_gamma"), W("block"), ALU.mult, ALU.mult)
            nc.vector.tensor_copy(u_b[:], ps[:, 5, 2:3])
            nc.vector.tensor_tensor(o_b[:], W("L0_b_out"), ps[:, 5, 1:2], ALU.add).then_inc(s["L0 weights"], 1)
            norm_vector(dve, 0)

            def bias_bank(k):
                dve.wait_ge(s["bank filled"], k + 1)
                nc.vector.tensor_scalar(ps[0:NS, k, :], ps[0:NS, k, :], u_b[0:NS], None, ALU.add).then_inc(s["bank biased"], 1)

            bias_bank(0)
            for h in range(2):
                dve.wait_ge(s["L0 skip"], h + 1)
                nc.vector.scalar_tensor_tensor(halves(X)[h], ps[:, 6 + h, :], o_b[:], halves(X)[h], ALU.add, ALU.add)\
                    .then_inc(s["L0 skip added"], 1)
            dve.wait_ge(s["L0 skip added"], 2)
            bias_bank(1)
            dve.wait_ge(s["masks loaded"], 32)
            either = flags.rearrange("p n o -> p (n o)")[:, 0:NB * NOPS]
            link(nc.vector.tensor_tensor(acting[:, 0:NB * NOPS], masks[:, 0, :], masks[:, 1, :], ALU.max))
            link(nc.vector.tensor_copy(either, acting[:, 0:NB * NOPS]))
            link(nc.vector.memset(flags[:, NB, :], float(NB)))
            for i in reversed(range(NB)):
                link(nc.vector.scalar_tensor_tensor(skipped[:], flags[:, i + 1, :], -float(i), flags[:, i, :], ALU.add, ALU.mult))
                link(nc.vector.tensor_tensor(flags[:, i, :], flags[:, i + 1, :], skipped[:], ALU.subtract))
            link(nc.vector.tensor_copy(acting[:], flags.rearrange("p n o -> p (n o)")))
            for k in range(BANKS):
                if k > 0:
                    add_bank_out(dve, 0, k - 1)
                if 0 < k < BANKS - 1:
                    bias_bank(k + 1)
            link(add_bank_out(dve, 0, BANKS - 1))
            for j in range(J):
                ins = nc.vector.bn_stats(bn6[:, j, :], Xj[:, j, :])
            link(ins)
            for j in range(J):
                ins = nc.vector.bn_aggr(mv[:, j, :], bn6[:, j, :])
            ins.then_inc(s["gn stats"], 1)
            dve.wait_ge(s["lora products"], 1)
            nc.vector.tensor_copy(lora[:].rearrange("p a b -> p (a b)"), ps[:, 0, 0:3 * P])
            dve.wait_ge(s["gn sigma"], 1)
            link(nc.vector.reciprocal(rstd[:], rstd[:]))
            for j in range(J):
                ins = nc.vector.tensor_scalar(xn[:, j * T:(j + 1) * T], Xj[:, j, :], mv[:, j, 0:1], rstd[:, j:j + 1],
                                              ALU.subtract, ALU.mult)
            ins.then_inc(s["gn done"], 1)
            for i, (bias, a) in enumerate((("L1_b1", "L1_a1"), ("L1_b2", "L1_a2"), ("L1_ba", "L1_aa"))):
                dve.wait_ge(s["L1 biased"], i + 1)
                link(nc.vector.tensor_scalar(pm[:, i, :], pr[:, i, :], 0.0, W(a), ALU.min, ALU.mult))
                nc.vector.scalar_tensor_tensor(pm[:, i, :], pr[:, i, :], 0.0, pm[:, i, :], ALU.max, ALU.add)\
                    .then_inc(s["L1 prelu"], 1)
            dve.wait_ge(s["L1 prelu"], 3)
            for g in range(G):
                ins = nc.vector.tensor_scalar(e2z[:, g, :, :].rearrange("p j t -> p (j t)"), pm[:, 1, :],
                                              W("group_mask")[:, g:g + 1], None, ALU.mult)
            ins.then_inc(s["L1 keys"], 1)
            for b in range(B):
                j, g = b // G, b % G
                dve.wait_ge(s["L1 scores"], b + 1)
                nc.vector.reduce_max(mbx[:, j, :, C * g + NS], ps[:, b % 4, :].rearrange("p (q k) -> p q k", q=TT), AX)\
                    .then_inc(s["L1 max"], 1)
            dve.wait_ge(s["L1 max rows"], 1)
            nc.vector.tensor_tensor(e1m[:], pm[:, 0, :], ps[:, 4:6, :].rearrange("p a b -> p (a b)"), ALU.add)\
                .then_inc(s["L1 queries"], 1)
            for h in range(2):
                dve.wait_ge(s["L1 pv"], J // 2 * (h + 1))
                cols = slice(h * HALF, (h + 1) * HALF)
                link(nc.vector.reciprocal(den[:, cols], banks(6, 8)[:, cols]))
                link(nc.vector.tensor_tensor(oat[:, cols], den[:, cols], banks(4, 6)[:, cols], ALU.mult))
                ins = nc.vector.tensor_tensor(X[:, cols], X[:, cols], oat[:, cols], ALU.add)
            ins.then_inc(s["X ready"], 1)
            if upto == 1:
                dve.wait_ge(s["X ready"], 2)
                nc.vector.memset(bn6[:, 0, 0:1], 0.0).then_inc(s["stage done"], 1)
                return

            for i, w in enumerate("qkv"):
                link(nc.vector.scalar_tensor_tensor(wqkv[:, i, :], lora[:, i, :], 2.0,
                                                    W("block"), ALU.mult, ALU.mult))
                link(nc.vector.tensor_tensor(wqkv[:, i, :], wqkv[:, i, :], W(f"L2_w{w}T"), ALU.add))
            for i in range(2):
                even = wqkv[:, i, :].rearrange("p (d two) -> p two d", two=2)
                turned = wrot[:, i, :].rearrange("p (d two) -> p two d", two=2)
                nc.vector.tensor_scalar(turned[:, 0, :], even[:, 1, :], -1.0, None, ALU.mult)
                ins = nc.vector.tensor_copy(turned[:, 1, :], even[:, 0, :])
            ins.then_inc(s["L2 weights"], 1)
            norm_vector(dve, 1)
            for i in range(2):
                dve.wait_ge(s["L2 proj"], 2 * i + 2)
                angle = [W(t).unsqueeze(1).to_broadcast([P, J, T]) for t in ("cos", "sin")]
                bank = [ps[:, 4 * i + 2 * r:4 * i + 2 * r + 2, :].rearrange("p a (j t) -> p (a j) t", t=T) for r in range(2)]
                nc.vector.tensor_tensor(qk[:, i, :].rearrange("p (j t) -> p j t", j=J), angle[0], bank[0], ALU.mult)
                link(nc.vector.tensor_tensor(qrs.rearrange("p (j t) -> p j t", j=J), angle[1], bank[1], ALU.mult))
                ins = nc.vector.tensor_tensor(qk[:, i, :], qk[:, i, :], qrs, ALU.add)
                ins.then_inc(s["L2 rotated"], 1)
                dve.wait_ge(s["L2 rotated"], i + 1)
            for gh in range(8):
                ins = nc.vector.tensor_scalar(kz[:, gh, :, :].rearrange("p j t -> p (j t)"), qk[:, 1, :],
                                              W("head_mask")[:, gh:gh + 1], None, ALU.mult)
            dve.wait_ge(s["values turned"], 2)
            nc.vector.tensor_copy(vt[:].rearrange("p a b -> p (a b)"), banks(2, 4)).then_inc(s["L2 values by token"], 1)
            mbv = mb.rearrange("p (j q g h) -> p j q g h", j=J, q=TT, g=G)
            for b in range(B):
                j, g = b // G, b % G
                k0 = 3 * (b % 2)
                dve.wait_ge(s["L2 scores"], b + 1)
                nc.vector.reduce_max(mbv[:, j, 0, g, :], ps[:, k0, :].rearrange("p (h k) -> p h k", h=HEADS), AX)\
                    .then_inc(s["L2 max"], 1)
                nc.vector.reduce_max(mbv[:, j, 1, g, :], banks(k0 + 1, k0 + 3).rearrange("p (h k) -> p h k", h=HEADS), AX)\
                    .then_inc(s["L2 max"], 1)
            dve.wait_ge(s["L2 max rows"], 1)
            nc.vector.tensor_copy(nm[:, 0, :], ps[:, 6, 0:P]).then_inc(s["L2 max parts"], 1)
            dve.wait_ge(s["L2 max parts"], 1)
            nc.vector.tensor_tensor(nm[:, 1, :], ps[:, 6, 0:P], nm[:, 0, :], ALU.subtract).then_inc(s["L2 max parts"], 1)
            for b in range(B):
                g, sums = b % G, den[:, (b % 2) * T:(b % 2 + 1) * T]
                dve.wait_ge(s["L2 pv"], b + 1)
                link(nc.vector.reciprocal(sums, ps[:, 4 + b % 2, T:2 * T]))
                if b >= G:
                    dve.wait_ge(s["L2 out"], b - G + 1)
                nc.vector.tensor_tensor(oat[:, g * T:(g + 1) * T], sums, ps[:, 4 + b % 2, 0:T], ALU.mult)\
                    .then_inc(s["L2 attended"], 1)
            for h in range(2):
                dve.wait_ge(s["L2 out"], B // 2 * (h + 1))
                ins = nc.vector.tensor_tensor(halves(X)[h], halves(X)[h], ps[:, 6 + h, :], ALU.add)
            ins.then_inc(s["X ready"], 1)
            if upto == 2:
                dve.wait_ge(s["X ready"], 3)
                nc.vector.memset(bn6[:, 0, 0:1], 0.0).then_inc(s["stage done"], 1)
                return

            norm_vector(dve, 2)
            for h in range(2):
                dve.wait_ge(s["F proj"], h + 1)
                ins = nc.vector.bn_stats(bn6[:, h, :], ps[:, 4 + h, :])
            link(ins)
            link(nc.vector.bn_aggr(fst[:, 0:2], bn6[:, 0:2, :].rearrange("p a b -> p (a b)")))
            nc.vector.scalar_tensor_tensor(fst[:, 1:2], fst[:, 0:1], fst[:, 0:1], fst[:, 1:2], ALU.mult, ALU.add)\
                .then_inc(s["F row stats"], 1)
            dve.wait_ge(s["F stats"], 1)
            link(nc.vector.tensor_copy(fst[:, 2:4], ps[:, 6, 0:2]))
            link(nc.vector.tensor_tensor(fst[:, 4:5], fst[:, 2:3], fst[:, 2:3], ALU.mult))
            nc.vector.tensor_tensor(fst[:, 3:4], fst[:, 3:4], fst[:, 4:5], ALU.subtract).then_inc(s["F variance"], 1)
            dve.wait_ge(s["F sigma"], 1)
            link(nc.vector.reciprocal(fst[:, 3:4], fst[:, 3:4]))
            link(nc.vector.tensor_tensor(fst[:, 5:6], fst[:, 3:4], W("F_gamma"), ALU.mult))
            link(nc.vector.tensor_tensor(fst[:, 6:7], fst[:, 2:3], fst[:, 5:6], ALU.mult))
            link(nc.vector.tensor_tensor(fst[:, 6:7], W("F_beta"), fst[:, 6:7], ALU.subtract))
            for tc in range(TT):
                cols = slice(tc * P, (tc + 1) * P)
                nc.vector.tensor_scalar(xn[:].rearrange("p (j t) -> p j t", j=J)[:, :, cols],
                                        banks(4, 6).rearrange("p (j t) -> p j t", j=J)[:, :, cols], fst[:, 5:6], fst[:, 6:7],
                                        ALU.mult, ALU.add).then_inc(s["F input"], 1)
            nc.vector.memset(wbc.rearrange("p a b c -> p (a b c)"), 0.0)
            nc.vector.memset(xs[:, :, :, 0:K - 1], 0.0)
            link(nc.vector.memset(xs[:, :, :, T:T + K - 1], 0.0))
            nc.vector.memset(xdt.rearrange("p a g h e -> p (a g h e)"), 0.0)
            nc.vector.memset(c3[3 * ROWS:P, :, :], 0.0)
            for d, name in enumerate(("fwd", "bwd")):
                nc.vector.tensor_tensor(wx[:, d, :], W(name + "_proj")[:, 0:E2], W(name + "_taps")[:, 0:E2], ALU.mult)
                nc.vector.tensor_tensor(wbc[:, d, :, 0:NS], W(name + "_proj")[:, E2:].rearrange("p (a b) -> p a b", a=2),
                                        W(name + "_taps")[:, E2:].rearrange("p (a b) -> p a b", a=2), ALU.mult)
                ins = nc.vector.tensor_scalar(wout[:, d, :], W(name + "_out"), W(name + "_norm"), None, ALU.mult)
            ins.then_inc(s["M weights"], 1)
            for k in range(BANKS):
                ins = add_bank_out(dve, 1, k)
            ins.then_inc(s["X ready"], 1)
            if upto == 3:
                dve.wait_ge(s["X ready"], 4)
                nc.vector.memset(bn6[:, 0, 0:1], 0.0).then_inc(s["stage done"], 1)
                return
            norm_vector(dve, 3)
            rows = 2 * ROWS
            dve.wait_ge(s["M dt proj"], 1)
            link(nc.vector.tensor_scalar(drow[0:rows, 0, :], ps[0:rows, 4:6, :].rearrange("p a b -> p (a b)"),
                                         W("M_dt_bias", rows), None, ALU.add))
            nc.vector.scalar_tensor_tensor(drow[0:rows, 1, :], drow[0:rows, 0, :], -1.0, drow[0:rows, 0, :], ALU.mult, ALU.min)\
                .then_inc(s["M dt steps"], 1)
            dve.wait_ge(s["M dt log"], 1)
            nc.vector.scalar_tensor_tensor(drow[0:rows, 3, :], drow[0:rows, 0, :], 0.0, drow[0:rows, 1, :], ALU.max, ALU.add)\
                .then_inc(s["M dt"], 1)

            dve.wait_ge(s["M dt"], 1)
            dve.wait_ge(s["M dt exp"], 2)
            nc.vector.memset(cs[0:rows, :, 0:1], 0.0)
            nc.vector.memset(drow[0:rows, 1, 0:T], 1.0)
            link(nc.vector.tensor_scalar(drow[0:rows, 2, :], drow[0:rows, 3, :], fst[0:rows, 4:5], W("M_sign", rows),
                                         ALU.mult, ALU.mult))
            for j in range(J):
                ins = nc.vector.tensor_tensor_scan(cs[0:rows, j, 1:T + 1], drow[0:rows, 1, 0:T], drow[0:rows, 2, j * T:(j + 1) * T],
                                                   0.0, ALU.mult, ALU.add)
            link(ins)
            for part in range(3):
                decay_part(link, 0, part)
            for k in range(G + HEADS):
                ins = decay_operand(0, k)
            ins.then_inc(s["M decay operands"], 1)
            for d, name in enumerate(("fwd", "bwd")):
                if d == 1:
                    dve.wait_ge(s["M out"], 2)
                    nc.vector.tensor_copy(projected, banks(6, 8)).then_inc(s["M out saved"], 1)
                dve.wait_ge(s["M dt by token"], 1)
                for q in range(4):
                    dve.wait_ge(s["M x turned"], 4 * d + q + 1)
                    for i in range(2):
                        ins = nc.vector.tensor_tensor(
                            xdt[:, 2 * q:2 * q + 2].rearrange("p a g (q i) e -> p a (g q) (i e)", i=2)
                            [:, :, :, i * (C + PH):i * (C + PH) + PH],
                            ps[:, q, :].rearrange("p (a r e) -> p a r e", a=2, e=2 * PH)[:, :, :, i * PH:(i + 1) * PH],
                            dtt[:, 2 * q:2 * q + 2, :].rearrange("p a (r i) -> p a r i", i=2)
                            [:, :, d * ROWS // 2:d * ROWS // 2 + 2 * G, i:i + 1].to_broadcast([P, 2, 2 * G, PH]), ALU.mult)
                ins.then_inc(s["M xdt"], 1)
                dve.wait_ge(s["M B"], d + 1)
                for g in range(G):
                    ins = nc.vector.tensor_scalar(bz[:, g, :, :].rearrange("p j t -> p (j t)"), bp, W("group_mask")[:, g:g + 1],
                                                  None, ALU.mult)
                ins.then_inc(s["M B split"], 1)
                for n in range(3 * B):
                    b, count = n // 3, 3 * B * d + n
                    dve.wait_ge(s["M CB"], B * d + b + 1)
                    dve.wait_ge(s["M decay"], count + 1)
                    if count >= 3:
                        dve.wait_ge(s["M products"], count - 2)
                    nc.vector.tensor_tensor(gram[:, n % 3, :].rearrange("p (h t) -> p h t", h=HEADS),
                                            decay[:, n % 3, :].rearrange("p (h t) -> p h t", h=HEADS),
                                            ps[:, 4 + b % 2, (n % 3) * P:(n % 3 + 1) * P].unsqueeze(1).to_broadcast([P, HEADS, P]),
                                            ALU.mult).then_inc(s["M gram"], 1)
                    if n % 12 == 4 and n > 12:
                        gate(dve, link, d, n // 12 - 1)
                    if d == 0 and n in (6, 9, 12):
                        decay_part(link, 1, n // 3 - 2)
                    if d == 0 and 20 <= n < 20 + G + HEADS:
                        ins = decay_operand(1, n - 20)
                        if n == 20 + G + HEADS - 1:
                            ins.then_inc(s["M decay operands"], 1)
                    if d == 1 and n % 12 == 8:
                        cols = slice((n // 12) * T, (n // 12 + 1) * T)
                        link(nc.vector.reciprocal(oat[:, cols], oat[:, cols]))
                        link(nc.vector.tensor_tensor(projected[:, cols], projected[:, cols], oat[:, cols], ALU.mult))
                        ins = nc.vector.tensor_tensor(X[:, cols], X[:, cols], projected[:, cols], ALU.add)
                        if n == 44:
                            ins.then_inc(s["M forward added"], 1)
                gate(dve, link, d, J - 1)
            for h in range(2):
                dve.wait_ge(s["M sigma"], 2 + h + 1)
                link(nc.vector.reciprocal(halves(oat)[h], halves(oat)[h]))
                dve.wait_ge(s["M out"], 2 + h + 1)
                link(nc.vector.tensor_tensor(halves(oat)[h], halves(oat)[h], ps[:, 6 + h, :], ALU.mult))
                ins = nc.vector.tensor_tensor(halves(X)[h], halves(X)[h], halves(oat)[h], ALU.add)
            ins.then_inc(s["X ready"], 1)
            if upto == 4:
                dve.wait_ge(s["X ready"], 5)
                nc.vector.memset(bn6[:, 0, 0:1], 0.0).then_inc(s["stage done"], 1)
                return

            norm_vector(dve, 4)
            dve.wait_ge(s["normalised"], 10)
            picks = s["first of tokens"]

            def pick(n):
                nc.vector.transpose(h0[:], xn[0:C, 0:C]).then_inc(picks, 1)
                dve.wait_ge(picks, n * 3 + 1)
                dve.sem_inc(s["vector pick step"], 1)
                nc.vector.max(best[:], h0[0:1, 0:NOPS]).then_inc(picks, 1)
                dve.wait_ge(picks, n * 3 + 2)
                dve.sem_inc(s["vector pick step"], 1)
                nc.vector.max_index(op_at[:], best[:], h0[0:1, 0:NOPS]).then_inc(picks, 1)
                dve.wait_ge(picks, n * 3 + 3)
                nc.vector.memset(h0[0:1, 0:1], 0.0).then_inc(s["op picked"], 1)

            def attention(i, op, n):
                dve.wait_ge(s["R attention weights"], n * 64 + 64)
                for m in range(4):
                    ins = nc.vector.tensor_tensor(wbd[:, m, :].rearrange("p (g c) -> p g c", g=G),
                                                  w4[:, m, :].unsqueeze(1).to_broadcast([P, G, C]),
                                                  W("block").rearrange("p (g c) -> p g c", g=G), ALU.mult)
                ins.then_inc(s["R attention weights spread"], 1)
                dve.wait_ge(s["R copied"], n * 3 + 2)
                for g in range(G):
                    ins = nc.vector.tensor_scalar(rkz[:, g, :, :].rearrange("p j t -> p (j t)"), rq[:, 1, :],
                                                  W("group_mask")[:, g:g + 1], None, ALU.mult)
                ins.then_inc(s["R keys"], 1)
                for b in range(B):
                    j, g = b // G, b % G
                    dve.wait_ge(s["R scores"], n * B + (b + 1))
                    nc.vector.reduce_max(rmb.rearrange("p (j q g) -> p j q g", j=J, q=TT)[:, j, :, g],
                                         ps[:, b % 4, :].rearrange("p (q k) -> p q k", q=TT), AX).then_inc(s["R max"], 1)
                dve.wait_ge(s["R max rows"], n + 1)
                rows = J * TT * G
                nc.vector.tensor_copy(rnm[:, 0, :], ps[0:rows, 4, 0:P]).then_inc(s["R max parts"], 1)
                dve.wait_ge(s["R max parts"], n * 2 + 1)
                nc.vector.tensor_tensor(rnm[:, 1, :], ps[0:rows, 4, 0:P], rnm[:, 0, :], ALU.subtract).then_inc(s["R max parts"], 1)
                for h in range(2):
                    dve.wait_ge(s["R pv"], n * B + B // 2 * (h + 1))
                    cols = slice(h * HALF, (h + 1) * HALF)
                    nc.vector.reciprocal(den[:, cols], banks(6, 8)[:, cols]).then_inc(s["R reciprocal"], 1)
                    dve.wait_ge(s["R reciprocal"], n * 2 + (h + 1))
                    ins = nc.vector.tensor_tensor(oat[:, cols], den[:, cols], banks(4, 6)[:, cols], ALU.mult)
                ins.then_inc(s["R attended"], 1)
                dve.wait_ge(s["R attention out"], n + 1)
                nc.vector.tensor_copy(xn[:], banks(0, 2)).then_inc(s["R attention written"], 1)
                dve.wait_ge(s["R attention written"], n + 1)

            def feed_forward(i, op, n):
                dve.wait_ge(s["R ffn weights"], n * 64 + 64)
                for g in range(G):
                    nc.vector.tensor_scalar(w1z[:, g, :], w1s, W("group_mask")[:, g:g + 1], None, ALU.mult)\
                        .then_inc(s["R first weights spread"], 1)
                for k in range(1, 2 * G, 2):
                    dve.wait_ge(s["R hidden"], n * 8 + (k + 1))
                    nc.vector.tensor_scalar(hidden[:, k, :], ps[:, k % 4, :], b1s, 0.0, ALU.add, ALU.max)\
                        .then_inc(s["R relu vector"], 1)
                for h in range(2):
                    dve.wait_ge(s["R ffn out"], n * 8 + 4 * (h + 1))
                    ins = nc.vector.tensor_scalar(halves(xn)[h], ps[:, 4 + h, :], b2s, None, ALU.add)
                ins.then_inc(s["R ffn written"], 1)
                dve.wait_ge(s["R ffn written"], n + 1)

            pick(0)
            routed("vector", dve, attention, feed_forward, pick)
            nc.vector.tensor_tensor(X[:], X[:], xn[:], ALU.add).then_inc(s["X ready"], 1)


def _grouped(w):
    out = np.zeros((P, P), np.float32)
    for g in range(G):
        out[C * g:C * g + w.shape[0], C * g:C * g + w.shape[1]] = w
    return out


def _slots(v):
    out = np.zeros(v.shape[:-1] + (G, C), np.float32)
    out[..., :, :v.shape[-1]] = v[..., None, :]
    return out.reshape(v.shape[:-1] + (P,))


def _pack(a):
    w = np.zeros((P, NW), np.float32)

    def put(name, v):
        at, width = COL[name]
        v = np.asarray(v, np.float32)
        if v.ndim == 1:
            v = v[:, None]
        assert v.shape[1] == width, (name, v.shape)
        w[:v.shape[0], at:at + width] = v

    eye = np.eye(P, dtype=np.float32)
    put("ident", eye)
    put("neg_ident", -eye)
    put("block", _grouped(np.ones((C, C))))
    put("avg_c", _grouped(np.full((C, C), 1.0 / C)))
    put("avg_by_group", np.repeat(np.eye(G), C, axis=0) / C)
    put("avg_g", np.tile(np.eye(C), (G, G)) / G)
    put("eps", np.full(P, EPS))
    put("one", np.ones(P))
    put("ones32", np.ones((P, C)))
    put("group_mask", np.repeat(np.eye(G), C, axis=0))
    put("head_mask", np.repeat(np.eye(G * HEADS), HD, axis=0))
    by_head = np.zeros((HEADS, C, C), np.float32)
    for h in range(HEADS):
        by_head[h, h * HD:(h + 1) * HD] = a["L2_attn_wo"].T[h * HD:(h + 1) * HD]
    put("L2_wo_by_head", by_head.reshape(P, C))
    put("L0_W_in", np.tile(a["L0_conv_W_in"], (1, G)))
    put("L0_BmT", _slots(a["L0_conv_Bm"].T))
    put("L0_AT", _grouped(a["L0_conv_A"].T))
    put("L0_Cm", _slots(a["L0_conv_Cm"]))
    put("L0_W_outT", np.tile(a["L0_conv_W_out"].T, (1, G)))
    put("L0_D", a["L0_conv_D"])
    put("L0_b_in", a["L0_conv_b_in"])
    put("L0_W_inT", a["L0_conv_W_in"].T)
    put("L0_beta", a["L0_conv_beta"])
    put("L0_gamma", np.tile(a["L0_conv_gamma"], G))
    put("L0_b_out", np.tile(a["L0_conv_b_out"], G))
    for n in ("w1", "w2", "wa"):
        put(f"L1_{n}T", _grouped(a[f"L1_conv_{n}"].T))
    put("L1_b1", _slots(a["L1_conv_b1"]))
    put("L1_b2", _slots(np.concatenate([a["L1_conv_b2"], np.ones(1, np.float32)])))
    put("L1_ba", _slots(a["L1_conv_ba"]))
    for n in ("a1", "a2", "aa"):
        put("L1_" + n, np.broadcast_to(a["L1_conv_" + n], (P,)))
    for n in "qkv":
        put(f"L2_w{n}T", _grouped(a["L2_attn_w" + n].T))
    for n in "qkv":
        put(f"L2_A_{n}", np.tile(a["L2_attn_lora_A_" + n], (1, G)))
        put(f"L2_B_{n}T", np.tile(a["L2_attn_lora_B_" + n].T, (1, G)))
    freq = (1.0 / np.float32(10000.0) ** (np.arange(0, HD, 2, dtype=np.float32) / HD)).astype(np.float32)
    angle = np.arange(T, dtype=np.float32)[:, None] * freq[None, :]
    put("cos", np.tile(np.repeat(np.cos(angle), 2, axis=1).T, (P // HD, 1)))
    put("sin", np.tile(np.repeat(np.sin(angle), 2, axis=1).T, (P // HD, 1)))
    put("F_WT", _grouped(a["L2_ffn_W"].T))
    put("F_VT", _grouped(a["L2_ffn_V"].T))
    put("F_gamma", np.tile(a["L2_ffn_gamma"], G))
    put("F_beta", np.tile(a["L2_ffn_beta"], G))
    dtw, dtb, alog = (np.zeros(n + (2, 2, G, HEADS), np.float32) for n in ((P,), (), ()))
    for d, name in enumerate(("fwd", "bwd")):
        m = {k: a[f"L3_attn_{name}_{k}"] for k in ("in_proj", "conv_w", "conv_b", "A_log", "dt_bias", "D", "norm_w", "out_proj")}
        taps = m["conv_w"].T if d == 0 else m["conv_w"].T[::-1]
        put(name + "_proj", np.tile(m["in_proj"][:, E2:2 * E2 + 2 * NS], (K, 1)))
        put(name + "_taps", np.repeat(taps, C, axis=0))
        z = np.zeros((G, C, 2, 2, E2), np.float32)
        for g in range(G):
            z[g, :, g // 2, g % 2] = m["in_proj"][:, :E2]
        put(name + "_z", z.reshape(P, -1))
        put(name + "_bx", np.tile(m["conv_b"][:E2], 2))
        put(name + "_bB", _slots(m["conv_b"][E2:E2 + NS]))
        put(name + "_bC", _slots(m["conv_b"][E2 + NS:]))
        put(name + "_D", np.tile(np.repeat(m["D"], PH), 2))
        put(name + "_norm", np.tile(m["norm_w"], 2))
        o = np.zeros((2, E2, 2, C), np.float32)
        o[0, :, 0] = o[1, :, 1] = m["out_proj"]
        put(name + "_out", o.reshape(P, 2 * C))
        for g in range(G):
            dtw[C * g:C * g + C, d, :, g] = m["in_proj"][:, None, 2 * E2 + 2 * NS:]
        dtb[d], alog[d] = m["dt_bias"], m["A_log"]
    put("M_dtW", dtw.reshape(P, -1))
    put("M_dt_bias", dtb.reshape(-1))
    put("M_A_log", alog.reshape(-1))
    put("M_sign", np.repeat([-1.0, 1.0], ROWS))
    use, group, head = (v.reshape(-1) for v in np.meshgrid(range(2), range(G), range(HEADS), indexing="ij"))
    of_group, of_head = group[:, None] == np.arange(G), head[:, None] == np.arange(HEADS)
    for name, v in (("key_rows", of_group * use[:, None]), ("query_ones", of_group * (1 - use[:, None])),
                    ("query_rows", of_head * (1 - use[:, None])), ("key_minus_ones", -1 * of_head * use[:, None])):
        put(name, np.tile(v, (3, 1)))
    put("avg_e", np.repeat(np.repeat(np.eye(2), E2, axis=0), C, axis=1) / E2)
    return w


def _pack_consts(dtype):
    c = np.zeros((P, NC), np.float32)

    def put(name, v):
        at, width = CCOL[name]
        c[:v.shape[0], at:at + width] = v

    r = np.arange(P)
    put("identb", np.eye(P))
    put("mask_above", np.where(r[None, :] > r[:, None], MASKED, 0))
    put("mask_below", np.where(r[None, :] < r[:, None], MASKED, 0))
    return c.astype(dtype)


def _words(mask):
    padded = np.zeros(mask.shape + (4,), np.uint8)
    padded[..., 0] = mask.view(np.uint8)
    return padded.view(np.int32)[..., 0]


def kernel(**inputs):
    import concourse.bacc as bacc
    from concourse.bass_utils import run_bass_kernel_spmd

    a = {k: np.asarray(v) for k, v in inputs.items()}
    nc = bacc.Bacc("TRN2", target_bir_lowering=False, num_devices=1)
    arrays = {
        "x": np.ascontiguousarray(a["x"]),
        "weights": _pack(a),
        "consts": _pack_consts(mybir.dt.np(BF16)),
        "w1": a["L3_ffn_ffn_w1"], "b1": a["L3_ffn_ffn_b1"], "w2": a["L3_ffn_ffn_w2"], "b2": a["L3_ffn_ffn_b2"],
        "wq": a["L3_ffn_wq"], "wk": a["L3_ffn_wk"], "wv": a["L3_ffn_wv"], "wo": a["L3_ffn_wo"],
        "attn_mask": _words(a["L3_ffn_attn_mask"]), "ffn_mask": _words(a["L3_ffn_ffn_mask"]),
    }
    arrays = {k: np.ascontiguousarray(v) for k, v in arrays.items()}
    args = {k: nc.dram_tensor(k, v.shape, mybir.dt.from_np(v.dtype), kind="ExternalInput").ap() for k, v in arrays.items()}
    args["out"] = nc.dram_tensor("out", (B, C, 16, 16), F32, kind="ExternalOutput").ap()
    hybrid_block(nc, **args)
    return run_bass_kernel_spmd(nc, [arrays], core_ids=[0]).results[0]["out"]
```

```python
from contextlib import ExitStack

import numpy as np

import concourse.bass as bass
from concourse import mybir

ALU = mybir.AluOpType
ACT = mybir.ActivationFunctionType
F32 = mybir.dt.float32
BF16 = mybir.dt.bfloat16
U32 = mybir.dt.uint32
I32 = mybir.dt.int32
AX = mybir.AxisListType.X

P = 128
B, C, T = 16, 32, 256
G = P // C
J = B // G
N = J * T
HALF = N // 2
TT = T // P
HEADS = 4
HD = C // HEADS
E2 = 2 * C
NS = 16
PH = E2 // HEADS
K = 4
NB, NOPS, HID = 33, 19, 128
ARENA = 29696
BANKS = 8
STEP_BANK = HALF // B
assert BANKS * STEP_BANK == T
UNITS = 3 * B
STEPS = (4, 3, 3)
assert np.prod(STEPS) >= NB
EPS = 1e-5
MASKED = -1e30

ROWS = 2 * G * HEADS

WEIGHTS = [
    ("ident", P), ("centre", P), ("avg_by_group", G), ("block", P), ("eps", 1), ("one", 1),
    ("L0_W_in", P), ("L0_BmT", P), ("L0_AT", P), ("L0_Cm", P), ("L0_W_outT", P),
    ("L0_D", 1), ("L0_b_in", 1), ("L0_W_inT", E2), ("L0_beta", 1), ("L0_gamma", 1), ("L0_b_out", 1),
    ("L1_w1T", P), ("L1_w2T", P), ("L1_waT", P),
    ("L1_b1", 1), ("L1_b2", 1), ("L1_ba", 1), ("L1_a1", 1), ("L1_a2", 1), ("L1_aa", 1),
    ("neg_ident", P), ("ones32", C), ("group_mask", G),
    ("L2_wqT", P), ("L2_wkT", P), ("L2_wvT", P),
    ("L2_A_q", P), ("L2_A_k", P), ("L2_A_v", P), ("L2_B_qT", P), ("L2_B_kT", P), ("L2_B_vT", P),
    ("cos", T), ("sin", T), ("head_mask", G * HEADS), ("L2_wo_by_head", C),
    ("F_WT", P), ("F_VT", P), ("F_gamma", 1), ("F_beta", 1), ("avg_g", P),
    ("M_dtW", 2 * ROWS), ("M_dt_bias", 1), ("M_A_log", 1), ("M_sign", 1),
    ("key_rows", G), ("query_ones", G), ("query_rows", HEADS), ("key_minus_ones", HEADS), ("avg_e", 2 * C),
]
for _d in ("fwd", "bwd"):
    WEIGHTS += [(f"{_d}_proj", E2 + 2 * NS), (f"{_d}_taps", E2 + 2 * NS), (f"{_d}_z", 2 * P), (f"{_d}_bx", 1),
                (f"{_d}_bB", 1), (f"{_d}_bC", 1), (f"{_d}_D", 1), (f"{_d}_norm", 1), (f"{_d}_out", 2 * C)]
COL = {}
NW = 0
for _n, _w in WEIGHTS:
    COL[_n] = (NW, _w)
    NW += _w

CONSTS = [("identb", P), ("zeros", P), ("mask_above", P), ("mask_below", P), ("zeros2", P)]
CCOL = {}
NC = 0
for _n, _w in CONSTS:
    CCOL[_n] = (NC, _w)
    NC += _w


def hybrid_block(nc, x, weights, consts, w1, b1, w2, b2, wq, wk, wv, wo, attn_mask, ffn_mask, out, upto=99, dump=None):
    with ExitStack() as ctx:
        def sb(name, shape, dt=F32):
            return ctx.enter_context(nc.sbuf_tensor(name, shape, dt))

        class Signals(dict):
            def __missing__(self, what):
                self[what] = ctx.enter_context(nc.semaphore("s_" + what.replace(" ", "_")))
                return self[what]

        s = Signals()

        class Chain:
            def __init__(self, eng, sem):
                self.eng, self.sem, self.n = eng, sem, 0

            def __call__(self, ins):
                self.n += 1
                ins.then_inc(self.sem, 1)
                self.eng.wait_ge(self.sem, self.n)

        ps = ctx.enter_context(nc.psum_tensor("ps", [P, 8, HALF], F32))
        wsb = sb("wsb", [P, NW])
        csb = sb("csb", [P, NC], BF16)

        def W(name, rows=P):
            at, w = COL[name]
            return wsb[0:rows, at:at + w]

        def CB(name, rows=P):
            at, w = CCOL[name]
            return csb[0:rows, at:at + w]

        def CB_pair(first, second):
            assert CCOL[first][0] + CCOL[first][1] == CCOL[second][0]
            return csb[:, CCOL[first][0]:CCOL[second][0] + CCOL[second][1]]

        def banks(a, b):
            return ps[:, a:b, :].rearrange("p a b -> p (a b)")

        X = sb("X", [P, N])
        xc = sb("xc", [P, N])
        sq = sb("sq", [P, N])
        sigma = sb("sigma", [P, J * TT * G])
        xn = sb("xn", [P, N])
        u_w = sb("u_w", [P, P])
        g1 = sb("g1", [P, P])
        g2 = sb("g2", [P, P])
        d_wout = sb("d_wout", [E2, P])
        z_b = sb("z_b", [E2, 1])
        u_b = sb("u_b", [P, 1])
        o_b = sb("o_b", [P, 1])
        bn6 = sb("bn6", [P, J, 6])
        mv = sb("mv", [P, J, 2])
        rstd = sb("rstd", [P, J])
        prob = sb("prob", [P, 2, 3 * HALF])
        prob6 = prob[:].rearrange("p a (b c) -> p (a b) c", c=HALF)
        oat = sb("oat", [P, N])
        lora = sb("lora", [P, 3, P])
        den = sb("den", [P, N])
        vt = sb("vt", [P, J * TT, P])
        arena = sb("arena", [P, ARENA])
        states = arena[:, ARENA - B * (T + 1):].rearrange("p (g j t) -> p g j t", g=G, j=J)

        class Arena:
            def __init__(self):
                self.at = 0

            def __call__(self, *dims):
                n = int(np.prod(dims))
                v = arena[:, self.at:self.at + n]
                self.at += n
                assert self.at <= ARENA
                names = " ".join("abcd"[:len(dims)])
                if len(dims) == 1:
                    return v
                return v.rearrange(f"p ({names}) -> p {names}", **dict(zip("abcd", dims)))

        at = Arena()
        pr = at(3, N)
        pm = at(3, N)
        e2z = at(G, J, T)
        by_query1 = at(3, HALF)
        softmax1 = at(3, 4, TT)
        at = Arena()
        wqkv = sb("wqkv", [P, 3, P])
        wrot = sb("wrot", [P, 2, P])
        qk = at(2, N)
        qrs = at(N)
        kz = at(G * HEADS, J, T)
        by_query = at(3, HALF)
        softmax = at(3, 4, HEADS)
        nm = sb("nm", [P, 2, P], BF16)
        fst = sb("fst", [P, 8])
        at = Arena()
        xs = at(J, G, T + K - 1)
        wx = at(2, E2)
        wbc = at(2, 2, C)
        wout = at(2, 2 * C)
        xf = at(J, 2 * T)
        xdt = at(J * TT, G, HEADS, 2 * PH)
        bp = at(N)
        cp = at(N)
        bz = at(G, J, T)
        drow = bz.rearrange("p a b c -> p a (b c)")
        dtt = at(J * TT, 2 * ROWS)
        zf = at(J, 2 * T)
        yg = at(J, 2 * T)
        decay = at(3, HALF)
        gram = at(3, HALF)
        cs = at(J, T + 1)
        c3 = sb("c3", [P, J, T + 1], BF16)
        by_token = sb("by_token", [P, HEADS * N], BF16)
        low = lambda t: t.bitcast(BF16).rearrange("p (a n) -> p a n", n=N)
        key_side = ((low(xc[:]), low(sq[:])), (low(den[:]), low(vt[:].rearrange("p a b -> p (a b)"))))
        prob_flat = prob[:].rearrange("p a b -> p (a b)")
        query_side = (by_token[:].rearrange("p (h n) -> p h n", h=HEADS), low(prob_flat[:, 0:2 * N]))
        projected = prob_flat[:, 2 * N:3 * N]

        xr = x.rearrange("(j g) c h w -> (g c) j (h w)", g=G)
        Xj = X[:].rearrange("p (j t) -> p j t", j=J)

        def halves(t):
            return [t[:, h * HALF:(h + 1) * HALF] for h in range(2)]

        def norm_tensor(pe, n):
            for h in range(2):
                pe.wait_ge(s["X ready"], n + 1)
                nc.tensor.matmul(ps[:, h, :], W("centre"), halves(X)[h], start=True, stop=True).then_inc(s["centred"], 1)
            for h in range(2):
                pe.wait_ge(s["squares"], 2 * n + h + 1)
                for jt in range(h * 4, h * 4 + 4):
                    mm = nc.tensor.matmul(ps[:, 6 + h, jt * G:(jt + 1) * G], sq[:, jt * P:(jt + 1) * P], W("avg_by_group"),
                                          start=True, stop=True)
                mm.then_inc(s["variance"], 1)
            for h in range(2):
                pe.wait_ge(s["1/sigma"], 2 * n + h + 1)
                for jt in range(h * 4, h * 4 + 4):
                    mm = nc.tensor.matmul(ps[:, 2 + h, (jt % 4) * P:(jt % 4 + 1) * P],
                                          sq[:, jt * P:(jt + 1) * P], W("ident"),
                                          start=True, stop=True)
                mm.then_inc(s["1/sigma rows"], 1)

        def norm_vector(dve, n):
            for h in range(2):
                dve.wait_ge(s["squares"], 2 * n + h + 1)
                nc.vector.tensor_copy(halves(xc)[h], ps[:, h, :]).then_inc(s["centred copy"], 1)
            for h in range(2):
                dve.wait_ge(s["sigma"], 2 * n + h + 1)
                cols = sigma[:, h * 4 * G:(h + 1) * 4 * G]
                nc.vector.reciprocal(cols, cols).then_inc(s["1/sigma by token"], 1)
                dve.wait_ge(s["1/sigma by token"], 2 * n + h + 1)
                nc.vector.tensor_copy(halves(sq)[h].rearrange("p (a c) -> p a c", c=C),
                                      cols.unsqueeze(2).to_broadcast([P, 4 * G, C])).then_inc(s["1/sigma"], 1)
            for h in range(2):
                dve.wait_ge(s["1/sigma rows"], 2 * n + h + 1)
                dve.wait_ge(s["centred copy"], 2 * n + h + 1)
                nc.vector.tensor_tensor(halves(xn)[h], halves(xc)[h], ps[:, 2 + h, :], ALU.mult).then_inc(s["normalised"], 1)

        def norm_scalar(act, n):
            act.preload_act_table(ACT.Sqrt)
            for h in range(2):
                act.wait_ge(s["centred"], 2 * n + h + 1)
                nc.scalar.activation(halves(sq)[h], ps[:, h, :], ACT.Square).then_inc(s["squares"], 1)
            for h in range(2):
                act.wait_ge(s["variance"], 2 * n + h + 1)
                cols = slice(h * 4 * G, (h + 1) * 4 * G)
                nc.scalar.activation(sigma[:, cols], ps[:, 6 + h, cols], ACT.Sqrt, bias=W("eps")).then_inc(s["sigma"], 1)

        xnj = xn[:].rearrange("p (j t) -> p j t", j=J)

        def bank_fill(n, k, g, rows, w_in):
            mm = nc.tensor.matmul(ps[0:rows, k, g * P:(g + 1) * P], w_in[:, C * g:C * g + rows],
                                  xnj[:, :, STEP_BANK * k:STEP_BANK * (k + 1)], start=(g == 0), stop=True, skip_group_check=True)
            if g == G - 1:
                mm.then_inc(s["bank filled"], 1)

        def bank_out(k, g, rows, w_out):
            mm = nc.tensor.matmul(ps[C * g:C * g + C, k, 0:P], w_out, states[0:rows, g, :, STEP_BANK * k + 1:STEP_BANK * (k + 1) + 1],
                                  start=True, stop=True)
            if g == G - 1:
                mm.then_inc(s["bank out"], 1)

        def step_columns(k, rows, t):
            return ps[0:rows, k, :].rearrange("p (b t) -> p b t", t=STEP_BANK)[:, :, t]

        def recur_tensor(pe, n, rows, w_in, w_state, w_out):
            for t in range(T):
                k, r = t // STEP_BANK, t % STEP_BANK
                if r == 0 and n == 0:
                    pe.wait_ge(s["bank biased"], k + 1)
                if t > 0:
                    pe.wait_ge(s["state"], n * T + t)
                nc.tensor.matmul(step_columns(k, rows, r), w_state, states[0:rows, :, :, t].rearrange("p g j -> p (g j)"),
                                 start=False, stop=True, skip_group_check=True).then_inc(s["pre-state"], 1)
                if k > 0 and r in (4, 7, 10, 13):
                    bank_out(k - 1, (r - 4) // 3, rows, w_out)
                if k < BANKS - 1 and r in (17, 20, 23, 26):
                    if n == 0 and k + 1 == 6 and r == 17:
                        pe.wait_ge(s["L0 skip added"], 2)
                    if n == 1 and STEP_BANK * (k + 1) == P and r == 17:
                        pe.wait_ge(s["F input"], 2)
                    bank_fill(n, k + 1, (r - 17) // 3, rows, w_in)
            pe.wait_ge(s["state"], (n + 1) * T)
            for g in range(G):
                bank_out(BANKS - 1, g, rows, w_out)

        def recur_scalar(act, n, rows, func):
            for t in range(T):
                act.wait_ge(s["pre-state"], n * T + t + 1)
                nc.scalar.activation(states[0:rows, :, :, t + 1].rearrange("p g j -> p (g j)"),
                                     step_columns(t // STEP_BANK, rows, t % STEP_BANK), func).then_inc(s["state"], 1)

        def add_bank_out(dve, n, k):
            dve.wait_ge(s["bank out"], BANKS * n + k + 1)
            cols = Xj[:, :, STEP_BANK * k:STEP_BANK * (k + 1)]
            return nc.vector.tensor_tensor(cols, cols, ps[:, k, 0:P].rearrange("p (j t) -> p j t", j=J), ALU.add)

        def gate(dve, link, d, j):
            dve.wait_ge(s["M products"], 3 * B * d + 12 * (j + 1))
            link(nc.vector.scalar_tensor_tensor(yg[:, j, :], xf[:, j, :], W(("fwd", "bwd")[d] + "_D"), ps[:, 6 + j % 2, :],
                                                ALU.mult, ALU.add))
            dve.wait_ge(s["M z"], 4 * (d + 1))
            nc.vector.tensor_tensor(yg[:, j, :], yg[:, j, :], zf[:, j, :], ALU.mult).then_inc(s["M y"], 1)

        def decay_part(link, d, part):
            rows, dst = cs[ROWS * d:ROWS * (d + 1), :, :], c3[ROWS * part:ROWS * (part + 1), :, :]
            link(nc.vector.tensor_copy(dst, rows))
            if part < 2:
                link(nc.vector.tensor_tensor(rows, rows, dst, ALU.subtract))

        def decay_operand(d, k):
            sums = c3[:, :, 1 - d:1 - d + T]
            if k < G:
                return nc.vector.tensor_scalar(key_side[d][k // 2][:, k % 2, :].rearrange("p (j t) -> p j t", j=J), sums,
                                               W("key_rows")[:, k:k + 1], W("query_ones")[:, k:k + 1], ALU.mult, ALU.add)
            h = k - G
            return nc.vector.tensor_scalar(query_side[d][:, h, :].rearrange("p (j t) -> p j t", j=J), sums,
                                           W("query_rows")[:, h:h + 1], W("key_minus_ones")[:, h:h + 1], ALU.mult, ALU.add)

        at = Arena()
        w1z = at(G, HID)
        w1s = at(HID)
        w4 = at(4, C)
        wbd = at(4, P)
        hidden = at(2 * G, HALF)
        rq = at(2, N)
        rkz = at(G, J, T)
        rmb = at(J * TT * G)
        w2s = at(C)
        b1s = at(1)
        b2s = at(1)
        h0 = sb("h0", [C, C])
        best = sb("best", [1, 8])
        op_at = sb("op_at", [1, 8], U32)
        masks = sb("masks", [1, 2, NB * NOPS], I32)
        flags = prob[0:1].rearrange("p a b -> p (a b)")[:, 0:(NB + 1) * NOPS].rearrange("p (n o) -> p n o", n=NB + 1)
        skipped = sb("skipped", [1, NOPS])
        acting = sb("acting", [1, (NB + 1) * NOPS], I32)
        rnm = nm[0:J * TT * G]

        def routed(name, eng, attention, feed_forward, pick=None):
            count = [eng.alloc_register(f"n_{what}") for what in ("pick", "attention", "ffn")]
            for r in count:
                eng.reg_mov(r, 0)
            op, at, use_a, use_f = (eng.alloc_register(r) for r in ("op", "block", "attention_mask", "ffn_mask"))
            eng.wait_ge(s["op picked"], 1)
            eng.reg_load(op, op_at[0:1, 0:1])
            eng.reg_load(at, acting[0:1, bass.ds(nc.s_assert_within(eng.snap(op), 0, NOPS - 1), 1)])

            def step():
                i = nc.s_assert_within(eng.snap(at), 0, NB - 1)
                o = nc.s_assert_within(eng.snap(op), 0, NOPS - 1)
                at_op = nc.s_assert_within(i * NOPS + o, 0, NB * NOPS - 1)
                eng.reg_load(use_a, masks[0:1, 0, bass.ds(at_op, 1)])
                eng.reg_load(use_f, masks[0:1, 1, bass.ds(at_op, 1)])
                with eng.If_ne(use_a, 0):
                    attention(i, o, eng.snap(count[1]))
                    eng.reg_add(count[1], count[1], 1)
                eng.reg_add(count[0], count[0], 1)
                with eng.If_ne(use_f, 0):
                    feed_forward(i, o, eng.snap(count[2]), eng.snap(count[0]))
                    eng.reg_add(count[2], count[2], 1)
                if pick is not None:
                    with eng.If_eq(use_f, 0):
                        pick(eng.snap(count[0]))
                eng.wait_ge(s["op picked"], eng.snap(count[0]) + 1)
                eng.sem_inc(s[name + " saw the pick"], 1)
                eng.reg_load(op, op_at[0:1, 0:1])
                after = nc.s_assert_within(eng.snap(at) * NOPS + NOPS + eng.snap(op), 0, (NB + 1) * NOPS - 1)
                eng.reg_load(at, acting[0:1, bass.ds(after, 1)])

            outer, middle, inner = STEPS
            with eng.Fori(0, outer), eng.If_lt(at, NB), eng.Fori(0, middle), eng.If_lt(at, NB), eng.Fori(0, inner), eng.If_lt(at, NB):
                step()

        M_BLOCKS = (((0, 0), (0, 1), (1, 1)), ((0, 0), (1, 0), (1, 1)))

        block = ctx.enter_context(nc.Block())

        @block.sync
        def _(sp):
            sp.dma_start(Xj, xr).then_inc(s["x loaded"], 16)
            l0 = COL["L1_w1T"][0]
            sp.dma_start(wsb[:, 0:l0], weights[:, 0:l0]).then_inc(s["L0 weights loaded"], 16)
            sp.dma_start(wsb[:, l0:], weights[:, l0:]).then_inc(s["weights loaded"], 16)
            sp.dma_start(csb[:], consts).then_inc(s["consts loaded"], 16)
            sp.dma_start(masks[:, 0, :], attn_mask.rearrange("(a n) o -> a (n o)", a=1)).then_inc(s["masks loaded"], 16)
            sp.dma_start(masks[:, 1, :], ffn_mask.rearrange("(a n) o -> a (n o)", a=1)).then_inc(s["masks loaded"], 16)
            if upto >= 4:
                sp.wait_ge(s["M weights"], 1)
                sp.wait_ge(s["normalised"], 8)
                for i in range(K):
                    for g in range(G):
                        sp.dma_start(xs[C * i:C * i + C, :, g, K - 1 - i:K - 1 - i + T],
                                     xn[C * g:C * g + C, :].rearrange("p (j t) -> p j t", j=J)).then_inc(s["M stack"], 16)
            if upto < 99:
                sp.wait_ge(s["stage done"], 1)
                if dump == "X":
                    sp.dma_start(out.rearrange("(j g) c h w -> (g c) j (h w)", g=G), Xj).then_inc(s["stored"], 16)
                sp.wait_ge(s["stored"], 16)
                return
            sp.wait_ge(s["normalised"], 10)

            def attention(i, op, n):
                for m, w in enumerate((wq, wk, wv, wo)):
                    sp.dma_start(w4[:, m, :], w[bass.ds(i, 1), bass.ds(op, 1), :, :].rearrange("a b c d -> (a b) c d")
                                 .to_broadcast([G, C, C])).then_inc(s["R attention weights"], 16)

            def feed_forward(i, op, n, step):
                at = (bass.ds(i, 1), bass.ds(op, 1))
                sp.dma_start(w1s, w1[at[0], at[1], :, :].rearrange("a b c d -> (a b) c d").to_broadcast([G, C, HID]))\
                    .then_inc(s["R first weights"], 16)
                sp.wait_ge(s["R ffn written"], n * 2)
                sp.dma_start(b1s, b1[at[0], at[1], :].rearrange("a b (c d) -> (a b c) d", d=1)).then_inc(s["R ffn weights"], 16)
                sp.dma_start(w2s, w2[at[0], at[1], :, :].rearrange("a b c d -> (a b c) d")).then_inc(s["R ffn weights"], 16)
                sp.dma_start(b2s, b2[at[0], at[1], :].rearrange("a b (c d) -> (a b) c d", d=1).to_broadcast([G, C, 1]))\
                    .then_inc(s["R ffn weights"], 16)

            routed("sync", sp, attention, feed_forward)
            sp.wait_ge(s["X ready"], 6)
            sp.dma_start(out.rearrange("(j g) c h w -> (g c) j (h w)", g=G), Xj).then_inc(s["stored"], 16)
            sp.wait_ge(s["stored"], 16)

        @block.tensor
        def _(pe):
            pe.wait_ge(s["L0 weights loaded"], 16)
            nc.tensor.matmul(ps[:, 4, 0:P], W("L0_W_in", E2), W("L0_BmT", E2), start=True, stop=True)
            nc.tensor.matmul(ps[:, 4, P:2 * P], W("L0_Cm", E2), W("L0_W_outT", E2), start=True, stop=True)
            nc.tensor.matmul(ps[0:E2, 5, 0:1], W("L0_W_inT", C), W("L0_beta", C), start=True, stop=True).then_inc(s["L0 folds"], 1)
            pe.wait_ge(s["L0 z bias"], 1)
            nc.tensor.matmul(ps[:, 4, 2 * P:3 * P], W("L0_W_in", E2), d_wout[:], start=True, stop=True)
            nc.tensor.matmul(ps[:, 5, 2:3], W("L0_BmT", E2), z_b[:], start=True, stop=True)
            nc.tensor.matmul(ps[:, 5, 1:2], d_wout[:], z_b[:], start=True, stop=True).then_inc(s["L0 folds"], 1)
            norm_tensor(pe, 0)
            pe.wait_ge(s["L0 weights"], 1)
            pe.wait_ge(s["normalised"], 2)
            for g in range(G):
                bank_fill(0, 0, g, NS, u_w[:])
            for h in range(2):
                nc.tensor.matmul(ps[:, 6 + h, :], g2[:], halves(xn)[h], start=True, stop=True).then_inc(s["L0 skip"], 1)
            recur_tensor(pe, 0, NS, u_w[:], W("L0_AT", NS)[:, 0:NS], g1[0:NS, 0:C])
            pe.wait_ge(s["weights loaded"], 16)
            for i, w in enumerate("qkv"):
                mm = nc.tensor.matmul(ps[:, 0, i * P:(i + 1) * P], W("L2_A_" + w, HD), W(f"L2_B_{w}T", HD), start=True, stop=True)
            mm.then_inc(s["lora products"], 1)
            pe.wait_ge(s["gn done"], 1)
            for i, w in enumerate(("L1_w2T", "L1_w1T", "L1_waT")):
                for h in range(2):
                    nc.tensor.matmul(ps[:, 2 * i + h, :], W(w), halves(xn)[h], start=True, stop=True).then_inc(s["L1 proj"], 1)
            keys, queries, _ = (pm[:, i, :].rearrange("p (j t) -> p j t", j=J) for i in range(3))
            pe.wait_ge(s["L1 prelu"], 2)
            for b in range(B + 4):
                if b < B:
                    j, g = b // G, b % G
                    if b < G:
                        pe.wait_ge(s["L1 keys"], b + 1)
                    if b >= 3:
                        pe.wait_ge(s["L1 exp"], b - 2)
                    for qt in range(TT):
                        mm = nc.tensor.matmul(ps[:, b % 3, qt * T:(qt + 1) * T], queries[:, j, qt * P:(qt + 1) * P], e2z[:, g, j, :],
                                              start=True, stop=True)
                    mm.then_inc(s["L1 scores"], 1)
                if b == 1:
                    pe.wait_ge(s["L1 prelu"], 3)
                    for jt in range(J * TT):
                        mm = nc.tensor.matmul(ps[:, 6 + jt // 4, (jt % 4) * P:(jt % 4 + 1) * P], pm[:, 2, jt * P:(jt + 1) * P],
                                              W("ident"), is_transpose=True, start=True, stop=True)
                    mm.then_inc(s["values turned"], 1)
                if 2 <= b < B + 2:
                    v = b - 2
                    pe.wait_ge(s["L1 probabilities"], v + 1)
                    if v >= 3:
                        pe.wait_ge(s["L1 turned saved"], v - 2)
                    for i in range(4):
                        mm = nc.tensor.matmul(ps[:, 3 + v % 3, i * P:(i + 1) * P], by_query1[:, v % 3, i * P:(i + 1) * P],
                                              W("ident"), is_transpose=True, start=True, stop=True)
                    mm.then_inc(s["L1 turned"], 1)
                if b >= 7 and b % G == 3:
                    j = (b - 7) // G
                    pe.wait_ge(s["L1 turned saved"], G * (j + 1))
                    pe.wait_ge(s["values by token"], 1)
                    for qt in range(TT):
                        c0 = (j % 2) * T + qt * P
                        for kt in range(TT):
                            for g in range(G):
                                mm = nc.tensor.matmul(ps[C * g:C * g + C, 6 + j // 2, c0:c0 + P], vt[:, j * TT + kt, C * g:C * g + C],
                                                      prob6[:, (j * G + g) % 6, (qt * TT + kt) * P:(qt * TT + kt + 1) * P],
                                                      start=(kt == 0), stop=(kt == TT - 1))
                    mm.then_inc(s["L1 pv"], 1)
            if upto == 1:
                return
            norm_tensor(pe, 1)
            pe.wait_ge(s["L2 weights"], 1)
            pe.wait_ge(s["normalised"], 4)
            for i, w in enumerate((wqkv[:, 1, :], wrot[:, 1, :], wqkv[:, 0, :], wrot[:, 0, :])):
                for h in range(2):
                    mm = nc.tensor.matmul(ps[:, 2 * i + h, :], w, halves(xn)[h], start=True, stop=True)
                mm.then_inc(s["L2 proj"], 1)
            pe.wait_ge(s["L2 rotated"], 1)
            for jt in range(J * TT):
                mm = nc.tensor.matmul(ps[:, jt // 4, (jt % 4) * P:(jt % 4 + 1) * P], xn[:, jt * P:(jt + 1) * P], wqkv[:, 2, :],
                                      start=True, stop=True)
            mm.then_inc(s["L2 proj"], 1)
            pe.wait_ge(s["consts loaded"], 16)
            pe.wait_ge(s["L2 values by token"], 1)
            pe.wait_ge(s["L2 rotated"], 2)
            q = qk[:, 0, :].rearrange("p (j t) -> p j t", j=J)
            for u in range(UNITS + 5):
                if u < UNITS:
                    b, part = u // 3, u % 3
                    j, g = b // G, b % G
                    if b < G and part == 0:
                        pe.wait_ge(s["L2 keys"] if g % 2 else s["L2 keys scalar"], g // 2 + 1)
                    if u >= 3:
                        pe.wait_ge(s["L2 exp"], u - 2)
                    bank = ps[:, part, :]
                    if part == 0:
                        nc.tensor.matmul(bank, CB("identb"), CB("mask_above").unsqueeze(1).to_broadcast([P, HEADS, P]),
                                         start=True, stop=False)
                        for h in range(HEADS):
                            mm = nc.tensor.matmul(bank[:, h * P:(h + 1) * P], q[:, j, 0:P], kz[:, g * HEADS + h, j, 0:P],
                                                  start=False, stop=(h == HEADS - 1))
                    else:
                        for h in range(2):
                            nc.tensor.matmul(bank[:, h * T:(h + 1) * T], q[:, j, P:T],
                                                  kz[:, g * HEADS + 2 * (part - 1) + h, j, :], start=(h == 0), stop=False)
                        mm = nc.tensor.matmul(bank.rearrange("p (h k) -> p h k", h=2)[:, :, P:T], CB("identb"),
                                              CB("mask_above").unsqueeze(1).to_broadcast([P, 2, P]), start=False, stop=True)
                    mm.then_inc(s["L2 scores"], 1)
                if u >= 2 and u - 2 < UNITS:
                    v = u - 2
                    pe.wait_ge(s["L2 probabilities"], v + 1)
                    if v >= 3:
                        pe.wait_ge(s["L2 turned saved"], v - 2)
                    for i in range(4):
                        mm = nc.tensor.matmul(ps[:, 3 + v % 3, i * P:(i + 1) * P], by_query[:, v % 3, i * P:(i + 1) * P],
                                              W("ident"), is_transpose=True, start=True, stop=True)
                    mm.then_inc(s["L2 turned"], 1)
                if u >= 5 and (u - 5) % 3 == 0 and (u - 5) // 3 < B:
                    b = (u - 5) // 3
                    j, g = b // G, b % G
                    pe.wait_ge(s["L2 turned saved"], 3 * (b + 1))
                    if b >= 2:
                        pe.wait_ge(s["L2 added"], b - 1)
                    for qt, kt in ((0, 0), (1, 0), (1, 1)):
                        for h in range(HEADS):
                            part, c0 = (0, h * P) if qt == 0 else (1 + h // 2, (h % 2) * T + kt * P)
                            mm = nc.tensor.matmul(ps[C * h:C * h + C, 6 + b % 2, qt * P:(qt + 1) * P],
                                                  vt[:, j * TT + kt, C * g:C * g + C], prob6[:, (3 * b + part) % 6, c0:c0 + P],
                                                  start=(kt == 0), stop=(kt == qt))
                    mm.then_inc(s["L2 pv"], 1)
                if u >= 7 and (u - 7) % 3 == 0:
                    b = (u - 7) // 3
                    pe.wait_ge(s["L2 attended"], b + 1)
                    nc.tensor.matmul(ps[C * (b % G):C * (b % G) + C, 6 + b % 2, T:2 * T], W("L2_wo_by_head"),
                                     oat[:, (b % G) * T:(b % G + 1) * T], start=True, stop=True).then_inc(s["L2 out"], 1)
            if upto == 2:
                return
            norm_tensor(pe, 2)
            pe.wait_ge(s["normalised"], 6)
            for h in range(2):
                nc.tensor.matmul(ps[:, 4 + h, :], W("F_WT"), halves(xn)[h], start=True, stop=True).then_inc(s["F proj"], 1)
            pe.wait_ge(s["F row stats"], 1)
            nc.tensor.matmul(ps[:, 6, 0:2], W("avg_g"), fst[:, 0:2], start=True, stop=True).then_inc(s["F stats"], 1)
            pe.wait_ge(s["F input"], 1)
            for g in range(G):
                bank_fill(1, 0, g, C, W("ident"))
            recur_tensor(pe, 1, C, W("ident"), W("F_VT", C)[:, 0:C], W("ident", C)[:, 0:C])
            if upto == 3:
                return
            norm_tensor(pe, 3)
            pe.wait_ge(s["normalised"], 8)
            for h in range(2):
                mm = nc.tensor.matmul(ps[0:2 * ROWS, 4 + h, :], W("M_dtW"), halves(xn)[h], start=True, stop=True)
            mm.then_inc(s["M dt proj"], 1)

            def project_x(d):
                off = (K - 1) * d
                for gp in range(2):
                    for h in range(2):
                        for gl in range(2):
                            mm = nc.tensor.matmul(ps[E2 * gl:E2 * (gl + 1), 2 * gp + h, :], wx[:, d, :],
                                                  xs[:, 2 * h:2 * h + 2, 2 * gp + gl, off:off + T], start=True, stop=True)
                        mm.then_inc(s["M x proj"], 1)

            def project_z(d):
                for gp in range(2):
                    for h in range(2):
                        nc.tensor.matmul(ps[:, 2 * gp + h, :], W(("fwd", "bwd")[d] + "_z")[:, gp * P:(gp + 1) * P], halves(xn)[h],
                                         start=True, stop=True).then_inc(s["M z proj"], 1)

            def project_out(d):
                pe.wait_ge(s["M squares"], J * (d + 1))
                for bank, lhs, rhs, done in ((4, W("avg_e"), zf, s["M mean squares"]), (6, wout[:, d, :], yg, s["M out"])):
                    for h in range(2):
                        for gp in range(2):
                            mm = nc.tensor.matmul(ps[2 * C * gp:2 * C * (gp + 1), bank + h, :], lhs,
                                                  rhs[:, 2 * h:2 * h + 2, gp * T:(gp + 1) * T], start=True, stop=True)
                        mm.then_inc(done, 1)

            project_z(0)
            pe.wait_ge(s["M weights"], 1)
            pe.wait_ge(s["M stack"], 16 * K * G)
            pe.wait_ge(s["M z"], 4)
            project_x(0)
            pe.wait_ge(s["M dt"], 1)
            for jt in range(J * TT):
                mm = nc.tensor.matmul(ps[:, 6, jt * 2 * ROWS:(jt + 1) * 2 * ROWS], drow[0:2 * ROWS, 3, jt * P:(jt + 1) * P],
                                      W("ident", 2 * ROWS)[:, 0:2 * ROWS], is_transpose=True, start=True, stop=True)
            mm.then_inc(s["M dt turned"], 1)
            for d in range(2):
                off = (K - 1) * d
                if d == 1:
                    pe.wait_ge(s["M decay"], 3 * B)
                    project_x(1)
                    project_out(0)
                pe.wait_ge(s["M x"], 4 * (d + 1))
                for jt in range(J * TT):
                    for gp in range(2):
                        c0 = gp * T + (jt % TT) * P
                        mm = nc.tensor.matmul(ps[:, jt // 2, (2 * (jt % 2) + gp) * P:(2 * (jt % 2) + gp + 1) * P],
                                              xf[:, jt // TT, c0:c0 + P], W("ident"), is_transpose=True, start=True, stop=True)
                    if jt % 2 == 1:
                        mm.then_inc(s["M x turned"], 1)
                for i in range(2):
                    if d == 1:
                        pe.wait_ge(s["M sigma"] if i == 0 else s["M out saved"], 2 if i == 0 else 1)
                    elif i == 1:
                        pe.wait_ge(s["M dt by token"], 1)
                    for h in range(2):
                        for g in range(G):
                            mm = nc.tensor.matmul(ps[C * g:C * g + C, 4 + 2 * i + h, :], wbc[:, d, i, :],
                                                  xs[:, 2 * h:2 * h + 2, g, off:off + T], start=True, stop=True)
                    mm.then_inc(s["M bc"], 1)
                if d == 1:
                    pe.wait_ge(s["M xdt"], 2)
                    project_z(1)
                pe.wait_ge(s["M decay operands"], d + 1)
                pe.wait_ge(s["M xdt"], d + 1)
                pe.wait_ge(s["M B split"], d + 1)
                pe.wait_ge(s["M C"], d + 1)
                pe.wait_ge(s["M z"], 4 * (d + 1))
                cpj = cp.rearrange("p (j t) -> p j t", j=J)
                blocks = M_BLOCKS[d]

                for n in range(3 * B + 2):
                    if n < 3 * B:
                        b, (st_, tt_) = n // 3, blocks[n % 3]
                        j, g = b // G, b % G
                        count = 3 * B * d + n
                        if count >= 4:
                            pe.wait_ge(s["M decay"], count - 3)
                        if n % 3 == 0:
                            if b >= 2:
                                pe.wait_ge(s["M gram"], 3 * B * d + 3 * (b - 1))
                            for i, (sk, tq) in enumerate(blocks):
                                mm = nc.tensor.matmul(ps[:, 4 + b % 2, i * P:(i + 1) * P], bz[:, g, j, sk * P:(sk + 1) * P],
                                                      cpj[:, j, tq * P:(tq + 1) * P], start=(i == 0), stop=(i == 2))
                            mm.then_inc(s["M CB"], 1)
                        diag = st_ == tt_
                        if diag:
                            nc.tensor.matmul(ps[:, n % 4, :], CB("identb"),
                                             CB("mask_below" if d == 0 else "mask_above").unsqueeze(1).to_broadcast([P, HEADS, P]),
                                             start=True, stop=False)
                        keys, queries = j * T + st_ * P, j * T + tt_ * P
                        nc.tensor.matmul(ps[:, n % 4, :], key_side[d][g // 2][:, g % 2, keys:keys + P],
                                         query_side[d][:, :, queries:queries + P], start=not diag, stop=True)\
                            .then_inc(s["M exponent"], 1)
                    if n >= 2:
                        m = n - 2
                        b, (st_, tt_) = m // 3, blocks[m % 3]
                        j, g = b // G, b % G
                        first = m % 3 == (0 if tt_ == 0 else 1 + d)
                        last = m % 3 == (d if tt_ == 0 else 2)
                        if m % 12 == 0 and 4 * d + j >= 2:
                            pe.wait_ge(s["M y"], 4 * d + j - 1)
                        pe.wait_ge(s["M gram"], 3 * B * d + m + 1)
                        c0 = (g // 2) * T + tt_ * P
                        y = [ps[E2 * (g % 2) + C * pair:E2 * (g % 2) + C * (pair + 1), 6 + j % 2, c0:c0 + P] for pair in range(2)]
                        for i in range(2):
                            for pair in range(2):
                                h = 2 * pair + i
                                mm = nc.tensor.matmul(y[pair], xdt[:, j * TT + st_, g, h, :], gram[:, m % 3, h * P:(h + 1) * P],
                                                      start=(first and i == 0), stop=(last and i == 1))
                        mm.then_inc(s["M products"], 1)
            project_out(1)
            if upto == 4:
                return
            norm_tensor(pe, 4)

            def attention(i, op, n):
                pe.wait_ge(s["R attention weights spread"], n + 1)
                for m in range(3):
                    for h in range(2):
                        mm = nc.tensor.matmul(ps[:, 2 * m + h, :], wbd[:, m, :], halves(xn)[h], start=True, stop=True)
                    mm.then_inc(s["R proj"], 1)
                pe.wait_ge(s["R copied"], n * 3 + 3)
                for jt in range(J * TT):
                    mm = nc.tensor.matmul(ps[:, 6 + jt // 4, (jt % 4) * P:(jt % 4 + 1) * P], oat[:, jt * P:(jt + 1) * P],
                                          W("ident"), is_transpose=True, start=True, stop=True)
                mm.then_inc(s["R values turned"], 1)
                pe.wait_ge(s["R keys"], n + 1)
                q = rq[:, 0, :].rearrange("p (j t) -> p j t", j=J)
                for b in range(B):
                    j, g = b // G, b % G
                    if b >= 4:
                        pe.wait_ge(s["R max"], n * B + (b - 3))
                    for qt in range(TT):
                        mm = nc.tensor.matmul(ps[:, b % 4, qt * T:(qt + 1) * T], q[:, j, qt * P:(qt + 1) * P], rkz[:, g, j, :],
                                              start=True, stop=True)
                    mm.then_inc(s["R scores"], 1)
                pe.wait_ge(s["R max"], n * B + B)
                nc.tensor.matmul(ps[0:J * TT * G, 4, 0:P], rmb, W("neg_ident"), start=True, stop=True).then_inc(s["R max rows"], 1)
                pe.wait_ge(s["R max parts"], n * 2 + 2)
                pe.wait_ge(s["R values by token"], n + 1)
                rows = J * TT * G
                for b in range(B + 1):
                    if b < B:
                        j, g = b // G, b % G
                        if b >= 4:
                            pe.wait_ge(s["R exp"], n * B + (b - 3))
                        for kt in range(TT):
                            nc.tensor.matmul(ps[:, b % 4, kt * T:(kt + 1) * T], rkz[:, g, j, kt * P:(kt + 1) * P], q[:, j, :],
                                             start=(kt == 0), stop=False)
                            for qt in range(TT):
                                row = (j * TT + qt) * G + g
                                for part in range(2):
                                    c0 = kt * T + qt * P
                                    mm = nc.tensor.matmul(ps[:, b % 4, c0:c0 + P],
                                                          CB("identb", rows)[:, row:row + 1].to_broadcast([rows, P]),
                                                          rnm[:, part, :], start=False, stop=(kt == 1 and qt == 1 and part == 1))
                        mm.then_inc(s["R scores T"], 1)
                    if b >= 1:
                        j, g = (b - 1) // G, (b - 1) % G
                        pe.wait_ge(s["R exp"], n * B + b)
                        for kt in range(TT):
                            pk = prob[:, (b - 1) % 2, kt * T:(kt + 1) * T]
                            cols = slice((j % 2) * T, (j % 2 + 1) * T)
                            nc.tensor.matmul(ps[C * g:C * g + C, 4 + j // 2, cols], vt[:, j * TT + kt, C * g:C * g + C], pk,
                                             start=(kt == 0), stop=(kt == TT - 1))
                            mm = nc.tensor.matmul(ps[C * g:C * g + C, 6 + j // 2, cols], W("ones32"), pk,
                                                  start=(kt == 0), stop=(kt == TT - 1))
                        mm.then_inc(s["R pv"], 1)
                pe.wait_ge(s["R attended"], n + 1)
                for h in range(2):
                    mm = nc.tensor.matmul(ps[:, h, :], wbd[:, 3, :], halves(oat)[h], start=True, stop=True)
                mm.then_inc(s["R attention out"], 1)
                pe.wait_ge(s["R attention written"], n + 1)

            def feed_forward(i, op, n, step):
                for k in range(2 * G):
                    if k >= 4:
                        done = s["R relu scalar"] if k % 2 == 0 else s["R relu vector"]
                        pe.wait_ge(done, n * 4 + (k - 4) // 2 + 1)
                    if k < G:
                        pe.wait_ge(s["R first weights spread"], n * G + (k + 1))
                    nc.tensor.matmul(ps[:, k % 4, :], w1z[:, k % G, :], halves(xn)[k // G], start=True, stop=True)\
                        .then_inc(s["R hidden"], 1)
                    if k in (5, 7):
                        h = k // 6
                        pe.wait_ge(s["R ffn weights"], n * 48 + 48)
                        for name in ("R relu scalar", "R relu vector"):
                            pe.wait_ge(s[name], n * 4 + (2 * h + 2))
                        for g in range(G):
                            nc.tensor.matmul(ps[C * g:C * g + C, 4 + h, :], w2s, hidden[:, G * h + g, :], start=True, stop=True)\
                                .then_inc(s["R ffn out"], 1)

            routed("tensor", pe, attention, feed_forward)

        @block.scalar
        def _(act):
            norm_scalar(act, 0)
            act.preload_act_table(ACT.Tanh)
            recur_scalar(act, 0, NS, ACT.Tanh)
            act.wait_ge(s["gn stats"], 1)
            nc.scalar.activation(rstd[:], mv[:, :, 1], ACT.Sqrt, bias=W("eps")).then_inc(s["gn sigma"], 1)
            for i, bias in enumerate(("L1_b2", "L1_b1", "L1_ba")):
                act.wait_ge(s["L1 proj"], 2 * i + 2)
                nc.scalar.activation(pr[:, i, :], ps[:, 2 * i:2 * i + 2, :].rearrange("p a b -> p (a b)"), ACT.Identity,
                                     bias=W(bias)).then_inc(s["L1 biased"], 1)
            act.preload_act_table(ACT.Exp)
            for b in range(B + 2):
                if b < B:
                    act.wait_ge(s["L1 minus max"], b + 1)
                    if b >= 3:
                        act.wait_ge(s["L1 turned"], b - 2)
                    for qt in range(TT):
                        ins = nc.scalar.activation(by_query1[:, b % 3, qt * T:(qt + 1) * T], ps[:, b % 3, qt * T:(qt + 1) * T], ACT.Exp,
                                                   bias=softmax1[:, b % 3, 1, qt:qt + 1], accum_out=softmax1[:, b % 3, 2, qt:qt + 1])
                    ins.then_inc(s["L1 exp"], 1)
                if b == 1:
                    act.wait_ge(s["values turned"], 1)
                    nc.scalar.activation(vt[:].rearrange("p a b -> p (a b)"), banks(6, 8), ACT.Copy).then_inc(s["values by token"], 1)
                if b >= 2:
                    v = b - 2
                    act.wait_ge(s["L1 turned"], v + 1)
                    if v >= 6:
                        act.wait_ge(s["L1 pv"], (v - 6) // G + 1)
                    nc.scalar.activation(prob6[:, v % 6, :], ps[:, 3 + v % 3, :], ACT.Copy).then_inc(s["L1 turned saved"], 1)
            if upto == 1:
                return
            norm_scalar(act, 1)
            act.wait_ge(s["L2 rotated"], 1)

            def keys_scalar(g):
                for h in range(HEADS):
                    gh = g * HEADS + h
                    ins = nc.scalar.activation(kz[:, gh, :, :].rearrange("p j t -> p (j t)"), qk[:, 1, :], ACT.Copy,
                                               scale=W("head_mask")[:, gh:gh + 1])
                ins.then_inc(s["L2 keys scalar"], 1)

            keys_scalar(0)
            act.wait_ge(s["L2 proj"], 5)
            nc.scalar.activation(vt[:].rearrange("p a b -> p (a b)"), banks(0, 2), ACT.Copy).then_inc(s["L2 values by token"], 1)
            act.preload_act_table(ACT.Exp)
            for u in range(UNITS + 2):
                if u == 1:
                    keys_scalar(2)
                if u < UNITS:
                    heads, width = (HEADS, P) if u % 3 == 0 else (2, T)
                    act.wait_ge(s["L2 minus max"], u + 1)
                    if u >= 3:
                        act.wait_ge(s["L2 turned"], u - 2)
                    for h in range(heads):
                        ins = nc.scalar.activation(by_query[:, u % 3, h * width:(h + 1) * width],
                                                   ps[:, u % 3, h * width:(h + 1) * width], ACT.Exp,
                                                   bias=softmax[:, u % 3, 1, h:h + 1], scale=HD ** -0.5,
                                                   accum_out=softmax[:, u % 3, 2, h:h + 1])
                    ins.then_inc(s["L2 exp"], 1)
                if u >= 2:
                    v = u - 2
                    act.wait_ge(s["L2 turned"], v + 1)
                    if v >= 6:
                        act.wait_ge(s["L2 pv"], v // 3 - 1)
                    nc.scalar.activation(prob6[:, v % 6, :], ps[:, 3 + v % 3, :], ACT.Copy).then_inc(s["L2 turned saved"], 1)
            if upto == 2:
                return
            norm_scalar(act, 2)
            act.wait_ge(s["F variance"], 1)
            nc.scalar.activation(fst[:, 3:4], fst[:, 3:4], ACT.Sqrt, bias=W("eps")).then_inc(s["F sigma"], 1)
            act.preload_act_table(ACT.Sigmoid)
            recur_scalar(act, 1, C, ACT.Sigmoid)
            if upto == 3:
                return
            norm_scalar(act, 3)
            rows = 2 * ROWS
            act.wait_ge(s["M dt steps"], 1)
            nc.scalar.activation(drow[0:rows, 1, :], drow[0:rows, 1, :], ACT.Exp).then_inc(s["M dt exp"], 1)
            nc.scalar.activation(fst[0:rows, 4:5], W("M_A_log", rows), ACT.Exp).then_inc(s["M dt exp"], 1)
            act.wait_ge(s["M dt exp"], 1)
            nc.scalar.activation(drow[0:rows, 1, :], drow[0:rows, 1, :], ACT.Ln, bias=W("one", rows)).then_inc(s["M dt log"], 1)
            act.preload_act_table(ACT.Silu)

            def gates(d):
                for k in range(4):
                    gp, h = k // 2, k % 2
                    act.wait_ge(s["M z proj"], 4 * d + k + 1)
                    nc.scalar.activation(zf[:, 2 * h:2 * h + 2, gp * T:(gp + 1) * T],
                                         ps[:, k, :].rearrange("p (j t) -> p j t", j=2), ACT.Silu).then_inc(s["M z"], 1)

            def sigmas(d):
                for h in range(2):
                    act.wait_ge(s["M mean squares"], 2 * d + h + 1)
                    if d == 1:
                        act.wait_ge(s["M forward added"], 1)
                    nc.scalar.activation(halves(oat)[h], ps[:, 4 + h, :], ACT.Sqrt, bias=W("eps")).then_inc(s["M sigma"], 1)

            def squares(d, j):
                act.wait_ge(s["M y"], J * d + j + 1)
                nc.scalar.activation(zf[:, j, :], yg[:, j, :], ACT.Square).then_inc(s["M squares"], 1)

            gates(0)
            for d in range(2):
                name = ("fwd", "bwd")[d]
                if d == 1:
                    sigmas(0)
                    act.wait_ge(s["M y"], J)
                for k in range(4):
                    gp, h = k // 2, k % 2
                    act.wait_ge(s["M x proj"], 4 * d + k + 1)
                    nc.scalar.activation(xf[:, 2 * h:2 * h + 2, gp * T:(gp + 1) * T],
                                         ps[:, k, :].rearrange("p (j t) -> p j t", j=2), ACT.Silu, bias=W(name + "_bx"))\
                        .then_inc(s["M x"], 1)
                if d == 0:
                    act.wait_ge(s["M dt turned"], 1)
                    nc.scalar.activation(dtt.rearrange("p a b -> p (a b)"), ps[:, 6, :], ACT.Copy).then_inc(s["M dt by token"], 1)
                act.wait_ge(s["M bc"], 2 * d + 1)
                nc.scalar.activation(bp, banks(4, 6), ACT.Silu, bias=W(name + "_bB")).then_inc(s["M B"], 1)
                act.wait_ge(s["M bc"], 2 * d + 2)
                nc.scalar.activation(cp, banks(6, 8), ACT.Silu, bias=W(name + "_bC")).then_inc(s["M C"], 1)
                if d == 1:
                    gates(1)
                act.preload_act_table(ACT.Exp)
                for n in range(3 * B):
                    count = 3 * B * d + n
                    act.wait_ge(s["M exponent"], count + 1)
                    if count >= 3:
                        act.wait_ge(s["M gram"], count - 2)
                    nc.scalar.activation(decay[:, n % 3, :], ps[:, n % 4, :], ACT.Exp).then_inc(s["M decay"], 1)
                    if n % 12 == 6 and n > 12:
                        squares(d, n // 12 - 1)
                squares(d, J - 1)
                act.preload_act_table(ACT.Sqrt)
            sigmas(1)
            if upto == 4:
                return
            norm_scalar(act, 4)

            def attention(i, op, n):
                for m, dst in enumerate((rq[:, 0, :], rq[:, 1, :], oat[:])):
                    act.wait_ge(s["R proj"], n * 3 + (m + 1))
                    nc.scalar.activation(dst, banks(2 * m, 2 * m + 2), ACT.Copy).then_inc(s["R copied"], 1)
                act.wait_ge(s["R values turned"], n + 1)
                nc.scalar.activation(vt[:].rearrange("p a b -> p (a b)"), banks(6, 8), ACT.Copy).then_inc(s["R values by token"], 1)
                for b in range(B):
                    act.wait_ge(s["R scores T"], n * B + (b + 1))
                    if b >= 2:
                        act.wait_ge(s["R pv"], n * B + (b - 1))
                    nc.scalar.activation(prob[:, b % 2, 0:HALF], ps[:, b % 4, :], ACT.Exp, scale=C ** -0.5).then_inc(s["R exp"], 1)

            def feed_forward(i, op, n, step):
                act.preload_act_table(ACT.Relu)
                act.wait_ge(s["R ffn weights"], n * 48 + 48)
                for k in range(0, 2 * G, 2):
                    act.wait_ge(s["R hidden"], n * 8 + (k + 1))
                    nc.scalar.activation(hidden[:, k, :], ps[:, k % 4, :], ACT.Relu, bias=b1s).then_inc(s["R relu scalar"], 1)

            routed("scalar", act, attention, feed_forward)

        @block.vector
        def _(dve):
            link = Chain(dve, s["vector step"])
            dve.wait_ge(s["x loaded"], 16)
            nc.vector.memset(states[:, :, :, 0:1], 0.0).then_inc(s["X ready"], 1)
            dve.wait_ge(s["L0 weights loaded"], 16)
            nc.vector.tensor_scalar(d_wout[:], W("L0_W_outT", E2), W("L0_D", E2), None, ALU.mult).then_inc(s["L0 d_wout"], 1)
            dve.wait_ge(s["L0 folds"], 1)
            nc.vector.tensor_tensor(z_b[:], W("L0_b_in", E2), ps[0:E2, 5, 0:1], ALU.add).then_inc(s["L0 d_wout"], 1)
            dve.wait_ge(s["L0 d_wout"], 2)
            nc.vector.scalar_tensor_tensor(u_w[:], ps[:, 4, 0:P], W("L0_gamma"), W("block"), ALU.mult, ALU.mult)
            nc.vector.tensor_tensor(g1[:], W("block"), ps[:, 4, P:2 * P], ALU.mult).then_inc(s["L0 z bias"], 1)
            dve.wait_ge(s["L0 folds"], 2)
            nc.vector.scalar_tensor_tensor(g2[:], ps[:, 4, 2 * P:3 * P], W("L0_gamma"), W("block"), ALU.mult, ALU.mult)
            nc.vector.tensor_copy(u_b[:], ps[:, 5, 2:3])
            nc.vector.tensor_tensor(o_b[:], W("L0_b_out"), ps[:, 5, 1:2], ALU.add).then_inc(s["L0 weights"], 1)
            norm_vector(dve, 0)

            def bias_bank(k):
                dve.wait_ge(s["bank filled"], k + 1)
                nc.vector.tensor_scalar(ps[0:NS, k, :], ps[0:NS, k, :], u_b[0:NS], None, ALU.add).then_inc(s["bank biased"], 1)

            bias_bank(0)
            for h in range(2):
                dve.wait_ge(s["L0 skip"], h + 1)
                nc.vector.scalar_tensor_tensor(halves(X)[h], ps[:, 6 + h, :], o_b[:], halves(X)[h], ALU.add, ALU.add)\
                    .then_inc(s["L0 skip added"], 1)
            dve.wait_ge(s["L0 skip added"], 2)
            bias_bank(1)
            dve.wait_ge(s["masks loaded"], 32)
            either = flags.rearrange("p n o -> p (n o)")[:, 0:NB * NOPS]
            link(nc.vector.tensor_tensor(acting[:, 0:NB * NOPS], masks[:, 0, :], masks[:, 1, :], ALU.max))
            link(nc.vector.tensor_copy(either, acting[:, 0:NB * NOPS]))
            link(nc.vector.memset(flags[:, NB, :], float(NB)))
            for i in reversed(range(NB)):
                link(nc.vector.scalar_tensor_tensor(skipped[:], flags[:, i + 1, :], -float(i), flags[:, i, :], ALU.add, ALU.mult))
                link(nc.vector.tensor_tensor(flags[:, i, :], flags[:, i + 1, :], skipped[:], ALU.subtract))
            link(nc.vector.tensor_copy(acting[:], flags.rearrange("p n o -> p (n o)")))
            for k in range(BANKS):
                if k > 0:
                    add_bank_out(dve, 0, k - 1)
                if 0 < k < BANKS - 1:
                    bias_bank(k + 1)
            link(add_bank_out(dve, 0, BANKS - 1))
            for j in range(J):
                ins = nc.vector.bn_stats(bn6[:, j, :], Xj[:, j, :])
            link(ins)
            for j in range(J):
                ins = nc.vector.bn_aggr(mv[:, j, :], bn6[:, j, :])
            ins.then_inc(s["gn stats"], 1)
            dve.wait_ge(s["lora products"], 1)
            nc.vector.tensor_copy(lora[:].rearrange("p a b -> p (a b)"), ps[:, 0, 0:3 * P])
            dve.wait_ge(s["gn sigma"], 1)
            link(nc.vector.reciprocal(rstd[:], rstd[:]))
            for j in range(J):
                ins = nc.vector.tensor_scalar(xn[:, j * T:(j + 1) * T], Xj[:, j, :], mv[:, j, 0:1], rstd[:, j:j + 1],
                                              ALU.subtract, ALU.mult)
            ins.then_inc(s["gn done"], 1)
            for i, w in enumerate("qkv"):
                link(nc.vector.scalar_tensor_tensor(wqkv[:, i, :], lora[:, i, :], 2.0,
                                                    W("block"), ALU.mult, ALU.mult))
                link(nc.vector.tensor_tensor(wqkv[:, i, :], wqkv[:, i, :], W(f"L2_w{w}T"), ALU.add))
            for i in range(2):
                even = wqkv[:, i, :].rearrange("p (d two) -> p two d", two=2)
                turned = wrot[:, i, :].rearrange("p (d two) -> p two d", two=2)
                nc.vector.tensor_scalar(turned[:, 0, :], even[:, 1, :], -1.0, None, ALU.mult)
                ins = nc.vector.tensor_copy(turned[:, 1, :], even[:, 0, :])
            ins.then_inc(s["L2 weights"], 1)

            def prelu(i, slope):
                dve.wait_ge(s["L1 biased"], i + 1)
                link(nc.vector.tensor_scalar(pm[:, i, :], pr[:, i, :], 0.0, W(slope), ALU.min, ALU.mult))
                nc.vector.scalar_tensor_tensor(pm[:, i, :], pr[:, i, :], 0.0, pm[:, i, :], ALU.max, ALU.add)\
                    .then_inc(s["L1 prelu"], 1)

            prelu(0, "L1_a2")
            prelu(1, "L1_a1")
            dve.wait_ge(s["L1 prelu"], 1)
            for g in range(G):
                nc.vector.tensor_scalar(e2z[:, g, :, :].rearrange("p j t -> p (j t)"), pm[:, 0, :],
                                        W("group_mask")[:, g:g + 1], None, ALU.mult).then_inc(s["L1 keys"], 1)
            prelu(2, "L1_aa")
            for b in range(B + 1):
                if b < B:
                    dve.wait_ge(s["L1 scores"], b + 1)
                    if b >= 3:
                        dve.wait_ge(s["L1 exp"], b - 2)
                    link(nc.vector.reduce_max(softmax1[:, b % 3, 0, :], ps[:, b % 3, :].rearrange("p (q k) -> p q k", q=TT), AX))
                    nc.vector.tensor_scalar(softmax1[:, b % 3, 1, :], softmax1[:, b % 3, 0, :], -1.0, None, ALU.mult)\
                        .then_inc(s["L1 minus max"], 1)
                if b >= 1:
                    v = b - 1
                    dve.wait_ge(s["L1 exp"], v + 1)
                    link(nc.vector.reciprocal(softmax1[:, v % 3, 3, :], softmax1[:, v % 3, 2, :]))
                    rows = by_query1[:, v % 3, :].rearrange("p (q k) -> p q k", q=TT)
                    nc.vector.tensor_tensor(rows, rows, softmax1[:, v % 3, 3, :].unsqueeze(2).to_broadcast([P, TT, T]), ALU.mult)\
                        .then_inc(s["L1 probabilities"], 1)
            for h in range(2):
                dve.wait_ge(s["L1 pv"], J // 2 * (h + 1))
                ins = nc.vector.tensor_tensor(halves(X)[h], halves(X)[h], ps[:, 6 + h, :], ALU.add)
            ins.then_inc(s["X ready"], 1)
            if upto == 1:
                dve.wait_ge(s["X ready"], 2)
                nc.vector.memset(bn6[:, 0, 0:1], 0.0).then_inc(s["stage done"], 1)
                return

            norm_vector(dve, 1)
            for i in range(2):
                dve.wait_ge(s["L2 proj"], 2 * i + 2)
                angle = [W(t).unsqueeze(1).to_broadcast([P, J, T]) for t in ("cos", "sin")]
                bank = [ps[:, 4 * i + 2 * r:4 * i + 2 * r + 2, :].rearrange("p a (j t) -> p (a j) t", t=T) for r in range(2)]
                dst = qk[:, 1 - i, :]
                nc.vector.tensor_tensor(dst.rearrange("p (j t) -> p j t", j=J), angle[0], bank[0], ALU.mult)
                link(nc.vector.tensor_tensor(qrs.rearrange("p (j t) -> p j t", j=J), angle[1], bank[1], ALU.mult))
                ins = nc.vector.tensor_tensor(dst, dst, qrs, ALU.add)
                ins.then_inc(s["L2 rotated"], 1)
                dve.wait_ge(s["L2 rotated"], i + 1)

            def keys_vector(g):
                for h in range(HEADS):
                    gh = g * HEADS + h
                    ins = nc.vector.tensor_scalar(kz[:, gh, :, :].rearrange("p j t -> p (j t)"), qk[:, 1, :],
                                                  W("head_mask")[:, gh:gh + 1], None, ALU.mult)
                ins.then_inc(s["L2 keys"], 1)

            for u in range(UNITS + 6):
                if u in (1, 4):
                    keys_vector(u // 4 * 2 + 1)
                if u < UNITS:
                    heads = HEADS if u % 3 == 0 else 2
                    dve.wait_ge(s["L2 scores"], u + 1)
                    if u >= 3:
                        dve.wait_ge(s["L2 exp"], u - 2)
                    link(nc.vector.reduce_max(softmax[:, u % 3, 0, 0:heads], ps[:, u % 3, :].rearrange("p (h k) -> p h k", h=heads), AX))
                    nc.vector.tensor_scalar(softmax[:, u % 3, 1, 0:heads], softmax[:, u % 3, 0, 0:heads], -HD ** -0.5, None, ALU.mult)\
                        .then_inc(s["L2 minus max"], 1)
                if u >= 1 and u - 1 < UNITS:
                    v = u - 1
                    heads = HEADS if v % 3 == 0 else 2
                    dve.wait_ge(s["L2 exp"], v + 1)
                    link(nc.vector.reciprocal(softmax[:, v % 3, 3, 0:heads], softmax[:, v % 3, 2, 0:heads]))
                    rows = by_query[:, v % 3, :].rearrange("p (h k) -> p h k", h=heads)
                    nc.vector.tensor_tensor(rows, rows, softmax[:, v % 3, 3, 0:heads].unsqueeze(2)
                                            .to_broadcast([P, heads, HALF // heads]), ALU.mult).then_inc(s["L2 probabilities"], 1)
                if u >= 6 and (u - 6) % 3 == 0 and (u - 6) // 3 < B:
                    b = (u - 6) // 3
                    dve.wait_ge(s["L2 pv"], b + 1)
                    if b >= G:
                        dve.wait_ge(s["L2 out"], b - G + 1)
                    nc.vector.tensor_copy(oat[:, (b % G) * T:(b % G + 1) * T], ps[:, 6 + b % 2, 0:T]).then_inc(s["L2 attended"], 1)
                if u >= 8 and (u - 8) % 3 == 0:
                    b = (u - 8) // 3
                    dve.wait_ge(s["L2 out"], b + 1)
                    rows = X[C * (b % G):C * (b % G) + C, (b // G) * T:(b // G + 1) * T]
                    ins = nc.vector.tensor_tensor(rows, rows, ps[C * (b % G):C * (b % G) + C, 6 + b % 2, T:2 * T], ALU.add)
                    ins.then_inc(s["L2 added"] if b < B - 1 else s["X ready"], 1)
            if upto == 2:
                dve.wait_ge(s["X ready"], 3)
                nc.vector.memset(bn6[:, 0, 0:1], 0.0).then_inc(s["stage done"], 1)
                return

            norm_vector(dve, 2)
            for h in range(2):
                dve.wait_ge(s["F proj"], h + 1)
                ins = nc.vector.bn_stats(bn6[:, h, :], ps[:, 4 + h, :])
            link(ins)
            link(nc.vector.bn_aggr(fst[:, 0:2], bn6[:, 0:2, :].rearrange("p a b -> p (a b)")))
            nc.vector.scalar_tensor_tensor(fst[:, 1:2], fst[:, 0:1], fst[:, 0:1], fst[:, 1:2], ALU.mult, ALU.add)\
                .then_inc(s["F row stats"], 1)
            dve.wait_ge(s["F stats"], 1)
            link(nc.vector.tensor_copy(fst[:, 2:4], ps[:, 6, 0:2]))
            link(nc.vector.tensor_tensor(fst[:, 4:5], fst[:, 2:3], fst[:, 2:3], ALU.mult))
            nc.vector.tensor_tensor(fst[:, 3:4], fst[:, 3:4], fst[:, 4:5], ALU.subtract).then_inc(s["F variance"], 1)
            dve.wait_ge(s["F sigma"], 1)
            link(nc.vector.reciprocal(fst[:, 3:4], fst[:, 3:4]))
            link(nc.vector.tensor_tensor(fst[:, 5:6], fst[:, 3:4], W("F_gamma"), ALU.mult))
            link(nc.vector.tensor_tensor(fst[:, 6:7], fst[:, 2:3], fst[:, 5:6], ALU.mult))
            link(nc.vector.tensor_tensor(fst[:, 6:7], W("F_beta"), fst[:, 6:7], ALU.subtract))
            for tc in range(TT):
                cols = slice(tc * P, (tc + 1) * P)
                nc.vector.tensor_scalar(xn[:].rearrange("p (j t) -> p j t", j=J)[:, :, cols],
                                        banks(4, 6).rearrange("p (j t) -> p j t", j=J)[:, :, cols], fst[:, 5:6], fst[:, 6:7],
                                        ALU.mult, ALU.add).then_inc(s["F input"], 1)
            nc.vector.memset(wbc.rearrange("p a b c -> p (a b c)"), 0.0)
            nc.vector.memset(xs[:, :, :, 0:K - 1], 0.0)
            link(nc.vector.memset(xs[:, :, :, T:T + K - 1], 0.0))
            nc.vector.memset(xdt.rearrange("p a g h e -> p (a g h e)"), 0.0)
            nc.vector.memset(c3[3 * ROWS:P, :, :], 0.0)
            for d, name in enumerate(("fwd", "bwd")):
                nc.vector.tensor_tensor(wx[:, d, :], W(name + "_proj")[:, 0:E2], W(name + "_taps")[:, 0:E2], ALU.mult)
                nc.vector.tensor_tensor(wbc[:, d, :, 0:NS], W(name + "_proj")[:, E2:].rearrange("p (a b) -> p a b", a=2),
                                        W(name + "_taps")[:, E2:].rearrange("p (a b) -> p a b", a=2), ALU.mult)
                ins = nc.vector.tensor_scalar(wout[:, d, :], W(name + "_out"), W(name + "_norm"), None, ALU.mult)
            ins.then_inc(s["M weights"], 1)
            for k in range(BANKS):
                ins = add_bank_out(dve, 1, k)
            ins.then_inc(s["X ready"], 1)
            if upto == 3:
                dve.wait_ge(s["X ready"], 4)
                nc.vector.memset(bn6[:, 0, 0:1], 0.0).then_inc(s["stage done"], 1)
                return
            norm_vector(dve, 3)
            rows = 2 * ROWS
            dve.wait_ge(s["M dt proj"], 1)
            link(nc.vector.tensor_scalar(drow[0:rows, 0, :], ps[0:rows, 4:6, :].rearrange("p a b -> p (a b)"),
                                         W("M_dt_bias", rows), None, ALU.add))
            nc.vector.scalar_tensor_tensor(drow[0:rows, 1, :], drow[0:rows, 0, :], -1.0, drow[0:rows, 0, :], ALU.mult, ALU.min)\
                .then_inc(s["M dt steps"], 1)
            dve.wait_ge(s["M dt log"], 1)
            nc.vector.scalar_tensor_tensor(drow[0:rows, 3, :], drow[0:rows, 0, :], 0.0, drow[0:rows, 1, :], ALU.max, ALU.add)\
                .then_inc(s["M dt"], 1)

            dve.wait_ge(s["M dt"], 1)
            dve.wait_ge(s["M dt exp"], 2)
            nc.vector.memset(cs[0:rows, :, 0:1], 0.0)
            nc.vector.memset(drow[0:rows, 1, 0:T], 1.0)
            link(nc.vector.tensor_scalar(drow[0:rows, 2, :], drow[0:rows, 3, :], fst[0:rows, 4:5], W("M_sign", rows),
                                         ALU.mult, ALU.mult))
            for j in range(J):
                ins = nc.vector.tensor_tensor_scan(cs[0:rows, j, 1:T + 1], drow[0:rows, 1, 0:T], drow[0:rows, 2, j * T:(j + 1) * T],
                                                   0.0, ALU.mult, ALU.add)
            link(ins)
            for part in range(3):
                decay_part(link, 0, part)
            for k in range(G + HEADS):
                ins = decay_operand(0, k)
            ins.then_inc(s["M decay operands"], 1)
            for d, name in enumerate(("fwd", "bwd")):
                if d == 1:
                    dve.wait_ge(s["M out"], 2)
                    nc.vector.tensor_copy(projected, banks(6, 8)).then_inc(s["M out saved"], 1)
                dve.wait_ge(s["M dt by token"], 1)
                for q in range(4):
                    dve.wait_ge(s["M x turned"], 4 * d + q + 1)
                    for i in range(2):
                        ins = nc.vector.tensor_tensor(
                            xdt[:, 2 * q:2 * q + 2].rearrange("p a g (q i) e -> p a (g q) (i e)", i=2)
                            [:, :, :, i * (C + PH):i * (C + PH) + PH],
                            ps[:, q, :].rearrange("p (a r e) -> p a r e", a=2, e=2 * PH)[:, :, :, i * PH:(i + 1) * PH],
                            dtt[:, 2 * q:2 * q + 2, :].rearrange("p a (r i) -> p a r i", i=2)
                            [:, :, d * ROWS // 2:d * ROWS // 2 + 2 * G, i:i + 1].to_broadcast([P, 2, 2 * G, PH]), ALU.mult)
                ins.then_inc(s["M xdt"], 1)
                dve.wait_ge(s["M B"], d + 1)
                for g in range(G):
                    ins = nc.vector.tensor_scalar(bz[:, g, :, :].rearrange("p j t -> p (j t)"), bp, W("group_mask")[:, g:g + 1],
                                                  None, ALU.mult)
                ins.then_inc(s["M B split"], 1)
                for n in range(3 * B):
                    b, count = n // 3, 3 * B * d + n
                    dve.wait_ge(s["M CB"], B * d + b + 1)
                    dve.wait_ge(s["M decay"], count + 1)
                    if count >= 3:
                        dve.wait_ge(s["M products"], count - 2)
                    nc.vector.tensor_tensor(gram[:, n % 3, :].rearrange("p (h t) -> p h t", h=HEADS),
                                            decay[:, n % 3, :].rearrange("p (h t) -> p h t", h=HEADS),
                                            ps[:, 4 + b % 2, (n % 3) * P:(n % 3 + 1) * P].unsqueeze(1).to_broadcast([P, HEADS, P]),
                                            ALU.mult).then_inc(s["M gram"], 1)
                    if n % 12 == 4 and n > 12:
                        gate(dve, link, d, n // 12 - 1)
                    if d == 0 and n in (6, 9, 12):
                        decay_part(link, 1, n // 3 - 2)
                    if d == 0 and 20 <= n < 20 + G + HEADS:
                        ins = decay_operand(1, n - 20)
                        if n == 20 + G + HEADS - 1:
                            ins.then_inc(s["M decay operands"], 1)
                    if d == 1 and n % 12 == 8:
                        cols = slice((n // 12) * T, (n // 12 + 1) * T)
                        link(nc.vector.reciprocal(oat[:, cols], oat[:, cols]))
                        link(nc.vector.tensor_tensor(projected[:, cols], projected[:, cols], oat[:, cols], ALU.mult))
                        ins = nc.vector.tensor_tensor(X[:, cols], X[:, cols], projected[:, cols], ALU.add)
                        if n == 44:
                            ins.then_inc(s["M forward added"], 1)
                gate(dve, link, d, J - 1)
            for h in range(2):
                dve.wait_ge(s["M sigma"], 2 + h + 1)
                link(nc.vector.reciprocal(halves(oat)[h], halves(oat)[h]))
                dve.wait_ge(s["M out"], 2 + h + 1)
                link(nc.vector.tensor_tensor(halves(oat)[h], halves(oat)[h], ps[:, 6 + h, :], ALU.mult))
                ins = nc.vector.tensor_tensor(halves(X)[h], halves(X)[h], halves(oat)[h], ALU.add)
            ins.then_inc(s["X ready"], 1)
            if upto == 4:
                dve.wait_ge(s["X ready"], 5)
                nc.vector.memset(bn6[:, 0, 0:1], 0.0).then_inc(s["stage done"], 1)
                return

            norm_vector(dve, 4)
            dve.wait_ge(s["normalised"], 10)
            picks = s["first of tokens"]

            def pick(n):
                nc.vector.transpose(h0[:], xn[0:C, 0:C]).then_inc(picks, 1)
                dve.wait_ge(picks, n * 3 + 1)
                dve.sem_inc(s["vector pick step"], 1)
                nc.vector.max(best[:], h0[0:1, 0:NOPS]).then_inc(picks, 1)
                dve.wait_ge(picks, n * 3 + 2)
                dve.sem_inc(s["vector pick step"], 1)
                nc.vector.max_index(op_at[:], best[:], h0[0:1, 0:NOPS]).then_inc(picks, 1)
                dve.wait_ge(picks, n * 3 + 3)
                nc.vector.memset(h0[0:1, 0:1], 0.0).then_inc(s["op picked"], 1)

            def attention(i, op, n):
                dve.wait_ge(s["R attention weights"], n * 64 + 64)
                for m in range(4):
                    ins = nc.vector.tensor_tensor(wbd[:, m, :].rearrange("p (g c) -> p g c", g=G),
                                                  w4[:, m, :].unsqueeze(1).to_broadcast([P, G, C]),
                                                  W("block").rearrange("p (g c) -> p g c", g=G), ALU.mult)
                ins.then_inc(s["R attention weights spread"], 1)
                dve.wait_ge(s["R copied"], n * 3 + 2)
                for g in range(G):
                    ins = nc.vector.tensor_scalar(rkz[:, g, :, :].rearrange("p j t -> p (j t)"), rq[:, 1, :],
                                                  W("group_mask")[:, g:g + 1], None, ALU.mult)
                ins.then_inc(s["R keys"], 1)
                for b in range(B):
                    j, g = b // G, b % G
                    dve.wait_ge(s["R scores"], n * B + (b + 1))
                    nc.vector.reduce_max(rmb.rearrange("p (j q g) -> p j q g", j=J, q=TT)[:, j, :, g],
                                         ps[:, b % 4, :].rearrange("p (q k) -> p q k", q=TT), AX).then_inc(s["R max"], 1)
                dve.wait_ge(s["R max rows"], n + 1)
                rows = J * TT * G
                nc.vector.tensor_copy(rnm[:, 0, :], ps[0:rows, 4, 0:P]).then_inc(s["R max parts"], 1)
                dve.wait_ge(s["R max parts"], n * 2 + 1)
                nc.vector.tensor_tensor(rnm[:, 1, :], ps[0:rows, 4, 0:P], rnm[:, 0, :], ALU.subtract).then_inc(s["R max parts"], 1)
                for h in range(2):
                    dve.wait_ge(s["R pv"], n * B + B // 2 * (h + 1))
                    cols = slice(h * HALF, (h + 1) * HALF)
                    nc.vector.reciprocal(den[:, cols], banks(6, 8)[:, cols]).then_inc(s["R reciprocal"], 1)
                    dve.wait_ge(s["R reciprocal"], n * 2 + (h + 1))
                    ins = nc.vector.tensor_tensor(oat[:, cols], den[:, cols], banks(4, 6)[:, cols], ALU.mult)
                ins.then_inc(s["R attended"], 1)
                dve.wait_ge(s["R attention out"], n + 1)
                nc.vector.tensor_copy(xn[:], banks(0, 2)).then_inc(s["R attention written"], 1)
                dve.wait_ge(s["R attention written"], n + 1)

            def feed_forward(i, op, n, step):
                dve.wait_ge(s["R first weights"], n * 16 + 16)
                for g in range(G):
                    nc.vector.tensor_scalar(w1z[:, g, :], w1s, W("group_mask")[:, g:g + 1], None, ALU.mult)\
                        .then_inc(s["R first weights spread"], 1)
                dve.wait_ge(s["R ffn weights"], n * 48 + 48)

                def out_half(h):
                    dve.wait_ge(s["R ffn out"], n * 8 + 4 * (h + 1))
                    nc.vector.tensor_scalar(halves(xn)[h], ps[:, 4 + h, :], b2s, None, ALU.add).then_inc(s["R ffn written"], 1)

                for k in range(1, 2 * G, 2):
                    if k == 2 * G - 1:
                        out_half(0)
                        dve.wait_ge(s["R ffn written"], n * 2 + 1)
                        pick(step)
                    dve.wait_ge(s["R hidden"], n * 8 + (k + 1))
                    nc.vector.tensor_scalar(hidden[:, k, :], ps[:, k % 4, :], b1s, 0.0, ALU.add, ALU.max)\
                        .then_inc(s["R relu vector"], 1)
                out_half(1)
                dve.wait_ge(s["R ffn written"], n * 2 + 2)

            pick(0)
            routed("vector", dve, attention, feed_forward, pick)
            nc.vector.tensor_tensor(X[:], X[:], xn[:], ALU.add).then_inc(s["X ready"], 1)


def _grouped(w):
    out = np.zeros((P, P), np.float32)
    for g in range(G):
        out[C * g:C * g + w.shape[0], C * g:C * g + w.shape[1]] = w
    return out


def _slots(v):
    out = np.zeros(v.shape[:-1] + (G, C), np.float32)
    out[..., :, :v.shape[-1]] = v[..., None, :]
    return out.reshape(v.shape[:-1] + (P,))


def _pack(a):
    w = np.zeros((P, NW), np.float32)

    def put(name, v):
        at, width = COL[name]
        v = np.asarray(v, np.float32)
        if v.ndim == 1:
            v = v[:, None]
        assert v.shape[1] == width, (name, v.shape)
        w[:v.shape[0], at:at + width] = v

    eye = np.eye(P, dtype=np.float32)
    put("ident", eye)
    put("neg_ident", -eye)
    put("block", _grouped(np.ones((C, C))))
    put("centre", _grouped(np.eye(C) - 1.0 / C))
    put("avg_by_group", np.repeat(np.eye(G), C, axis=0) / C)
    put("avg_g", np.tile(np.eye(C), (G, G)) / G)
    put("eps", np.full(P, EPS))
    put("one", np.ones(P))
    put("ones32", np.ones((P, C)))
    put("group_mask", np.repeat(np.eye(G), C, axis=0))
    put("head_mask", np.repeat(np.eye(G * HEADS), HD, axis=0))
    by_head = np.zeros((HEADS, C, C), np.float32)
    for h in range(HEADS):
        by_head[h, h * HD:(h + 1) * HD] = a["L2_attn_wo"].T[h * HD:(h + 1) * HD]
    put("L2_wo_by_head", by_head.reshape(P, C))
    put("L0_W_in", np.tile(a["L0_conv_W_in"], (1, G)))
    put("L0_BmT", _slots(a["L0_conv_Bm"].T))
    put("L0_AT", _grouped(a["L0_conv_A"].T))
    put("L0_Cm", _slots(a["L0_conv_Cm"]))
    put("L0_W_outT", np.tile(a["L0_conv_W_out"].T, (1, G)))
    put("L0_D", a["L0_conv_D"])
    put("L0_b_in", a["L0_conv_b_in"])
    put("L0_W_inT", a["L0_conv_W_in"].T)
    put("L0_beta", a["L0_conv_beta"])
    put("L0_gamma", np.tile(a["L0_conv_gamma"], G))
    put("L0_b_out", np.tile(a["L0_conv_b_out"], G))
    for n in ("w1", "w2", "wa"):
        put(f"L1_{n}T", _grouped(a[f"L1_conv_{n}"].T))
    put("L1_b1", _slots(a["L1_conv_b1"]))
    put("L1_b2", _slots(a["L1_conv_b2"]))
    put("L1_ba", _slots(a["L1_conv_ba"]))
    for n in ("a1", "a2", "aa"):
        put("L1_" + n, np.broadcast_to(a["L1_conv_" + n], (P,)))
    for n in "qkv":
        put(f"L2_w{n}T", _grouped(a["L2_attn_w" + n].T))
    for n in "qkv":
        put(f"L2_A_{n}", np.tile(a["L2_attn_lora_A_" + n], (1, G)))
        put(f"L2_B_{n}T", np.tile(a["L2_attn_lora_B_" + n].T, (1, G)))
    freq = (1.0 / np.float32(10000.0) ** (np.arange(0, HD, 2, dtype=np.float32) / HD)).astype(np.float32)
    angle = np.arange(T, dtype=np.float32)[:, None] * freq[None, :]
    put("cos", np.tile(np.repeat(np.cos(angle), 2, axis=1).T, (P // HD, 1)))
    put("sin", np.tile(np.repeat(np.sin(angle), 2, axis=1).T, (P // HD, 1)))
    put("F_WT", _grouped(a["L2_ffn_W"].T))
    put("F_VT", _grouped(a["L2_ffn_V"].T))
    put("F_gamma", np.tile(a["L2_ffn_gamma"], G))
    put("F_beta", np.tile(a["L2_ffn_beta"], G))
    dtw, dtb, alog = (np.zeros(n + (2, 2, G, HEADS), np.float32) for n in ((P,), (), ()))
    for d, name in enumerate(("fwd", "bwd")):
        m = {k: a[f"L3_attn_{name}_{k}"] for k in ("in_proj", "conv_w", "conv_b", "A_log", "dt_bias", "D", "norm_w", "out_proj")}
        taps = m["conv_w"].T if d == 0 else m["conv_w"].T[::-1]
        put(name + "_proj", np.tile(m["in_proj"][:, E2:2 * E2 + 2 * NS], (K, 1)))
        put(name + "_taps", np.repeat(taps, C, axis=0))
        z = np.zeros((G, C, 2, 2, E2), np.float32)
        for g in range(G):
            z[g, :, g // 2, g % 2] = m["in_proj"][:, :E2]
        put(name + "_z", z.reshape(P, -1))
        put(name + "_bx", np.tile(m["conv_b"][:E2], 2))
        put(name + "_bB", _slots(m["conv_b"][E2:E2 + NS]))
        put(name + "_bC", _slots(m["conv_b"][E2 + NS:]))
        put(name + "_D", np.tile(np.repeat(m["D"], PH), 2))
        put(name + "_norm", np.tile(m["norm_w"], 2))
        o = np.zeros((2, E2, 2, C), np.float32)
        o[0, :, 0] = o[1, :, 1] = m["out_proj"]
        put(name + "_out", o.reshape(P, 2 * C))
        for g in range(G):
            dtw[C * g:C * g + C, d, :, g] = m["in_proj"][:, None, 2 * E2 + 2 * NS:]
        dtb[d], alog[d] = m["dt_bias"], m["A_log"]
    put("M_dtW", dtw.reshape(P, -1))
    put("M_dt_bias", dtb.reshape(-1))
    put("M_A_log", alog.reshape(-1))
    put("M_sign", np.repeat([-1.0, 1.0], ROWS))
    use, group, head = (v.reshape(-1) for v in np.meshgrid(range(2), range(G), range(HEADS), indexing="ij"))
    of_group, of_head = group[:, None] == np.arange(G), head[:, None] == np.arange(HEADS)
    for name, v in (("key_rows", of_group * use[:, None]), ("query_ones", of_group * (1 - use[:, None])),
                    ("query_rows", of_head * (1 - use[:, None])), ("key_minus_ones", -1 * of_head * use[:, None])):
        put(name, np.tile(v, (3, 1)))
    put("avg_e", np.repeat(np.repeat(np.eye(2), E2, axis=0), C, axis=1) / E2)
    return w


def _pack_consts(dtype):
    c = np.zeros((P, NC), np.float32)

    def put(name, v):
        at, width = CCOL[name]
        c[:v.shape[0], at:at + width] = v

    r = np.arange(P)
    put("identb", np.eye(P))
    put("mask_above", np.where(r[None, :] > r[:, None], MASKED, 0))
    put("mask_below", np.where(r[None, :] < r[:, None], MASKED, 0))
    return c.astype(dtype)


def _words(mask):
    padded = np.zeros(mask.shape + (4,), np.uint8)
    padded[..., 0] = mask.view(np.uint8)
    return padded.view(np.int32)[..., 0]


def kernel(**inputs):
    import concourse.bacc as bacc
    from concourse.bass_utils import run_bass_kernel_spmd

    a = {k: np.asarray(v) for k, v in inputs.items()}
    nc = bacc.Bacc("TRN2", target_bir_lowering=False, num_devices=1)
    arrays = {
        "x": np.ascontiguousarray(a["x"]),
        "weights": _pack(a),
        "consts": _pack_consts(mybir.dt.np(BF16)),
        "w1": a["L3_ffn_ffn_w1"], "b1": a["L3_ffn_ffn_b1"], "w2": a["L3_ffn_ffn_w2"], "b2": a["L3_ffn_ffn_b2"],
        "wq": a["L3_ffn_wq"], "wk": a["L3_ffn_wk"], "wv": a["L3_ffn_wv"], "wo": a["L3_ffn_wo"],
        "attn_mask": _words(a["L3_ffn_attn_mask"]), "ffn_mask": _words(a["L3_ffn_ffn_mask"]),
    }
    arrays = {k: np.ascontiguousarray(v) for k, v in arrays.items()}
    args = {k: nc.dram_tensor(k, v.shape, mybir.dt.from_np(v.dtype), kind="ExternalInput").ap() for k, v in arrays.items()}
    args["out"] = nc.dram_tensor("out", (B, C, 16, 16), F32, kind="ExternalOutput").ap()
    hybrid_block(nc, **args)
    return run_bass_kernel_spmd(nc, [arrays], core_ids=[0]).results[0]["out"]
```
